# Optimizing a Trainium2 kernel written in Bass

```python
import numpy as np
import jax
import jax.numpy as jnp

def _softmax(x, axis=-1):
    return jax.nn.softmax(x, axis=axis)

def _gelu(x):
    return jax.nn.gelu(x, approximate=True)

def _silu(x):
    return jax.nn.silu(x)

def _sigmoid(x):
    return jax.nn.sigmoid(x)

def _layernorm(x, axis=-1, eps=1e-05):
    m = jnp.mean(x, axis=axis, keepdims=True)
    v = jnp.var(x, axis=axis, keepdims=True)
    return (x - m) / jnp.sqrt(v + eps)

def _scatter_add(tgt, idx, src, axis=0):
    return tgt.at[idx].add(src)

def _segment_sum(src, seg, n):
    return jax.ops.segment_sum(src, seg, n)
kernel_name = 'mk_lm_tower_d1_tok_ids256_r4_c10b38'

def setup_inputs(seed: int=0):
    np.random.seed(seed)
    _w = jnp.asarray

    def _rec_inputs():
        import jax
        import jax.numpy as jnp
        _rk = jax.random.key(seed)
        x = jax.random.randint(jax.random.fold_in(_rk, 1), (16, 1024), 0, 31993, jnp.int32)
        return x
    x = _rec_inputs()

    def _L0_tok_setup():
        import jax, jax.numpy as jnp
        import numpy as np
        VOCAB = 8000
        EMBED_DIM = 64
        NUM_RULES = 100
        BATCH, SEQ = (4, 512)
        key = jax.random.key(seed)
        k1, k2, k3, k4 = jax.random.split(key, 4)
        token_ids = jax.random.randint(k1, (BATCH, SEQ), 0, VOCAB)
        base_embeddings = jax.random.normal(k2, (VOCAB, EMBED_DIM), dtype=jnp.float32)
        rule_transform = jax.random.normal(k3, (NUM_RULES, EMBED_DIM, EMBED_DIM), dtype=jnp.float32)
        token_rules = jax.random.randint(k4, (VOCAB,), 0, NUM_RULES)
        return {'token_ids': token_ids, 'base_embeddings': base_embeddings, 'rule_transform': rule_transform, 'token_rules': token_rules}
    _L0_tok_all = _L0_tok_setup()
    _L0_tok_in = {k: v for k, v in _L0_tok_all.items() if k in ('base_embeddings', 'rule_transform', 'token_rules')}
    del _L0_tok_all

    def _L0_attn_setup():
        import jax, jax.numpy as jnp
        import numpy as np
        BS = 32
        NUM_HOPS = 1

        def _connectivity(edge_index, edge_values, positions, nb):
            rows, cols = (edge_index[0], edge_index[1])
            br, bc = (rows // BS, cols // BS)
            in_block = (br == bc) & (br < nb)
            r_l, c_l = (rows % BS, cols % BS)
            b_safe = jnp.where(in_block, br, nb)
            dx = positions[cols] - positions[rows]
            ef_flat = jnp.concatenate([dx, edge_values[:, None]], axis=1)
            adj = jnp.zeros((nb, BS, BS), jnp.float32).at[b_safe, r_l, c_l].set(1.0, mode='drop')
            eye = jnp.eye(BS, dtype=jnp.float32)
            reachable = jnp.broadcast_to(eye[None], (nb, BS, BS))
            cur = adj
            for _ in range(NUM_HOPS):
                reachable = jnp.clip(reachable + cur, 0.0, 1.0)
                cur = jnp.matmul(cur, adj)
            attn_mask = jnp.concatenate([reachable, jnp.ones((nb, BS, 1), jnp.float32)], axis=2)
            edge_feats = jnp.zeros((nb, BS, BS + 1, 4), jnp.float32)
            edge_feats = edge_feats.at[b_safe, r_l, c_l, :].set(ef_flat, mode='drop')
            return (attn_mask, edge_feats)
        key = jax.random.key(seed)
        ks = jax.random.split(key, 10)
        B, N, C, H = (1, 32768, 64, 4)
        E = 8 * N
        x = jax.random.normal(ks[0], (B, N, C), dtype=jnp.float32)
        rows = jax.random.randint(ks[1], (E,), 0, N)
        offs = jax.random.randint(ks[2], (E,), 0, BS)
        cols = rows // BS * BS + offs
        edge_index = jnp.stack([rows, cols]).astype(jnp.int64)
        edge_values = jax.random.normal(ks[3], (E,), dtype=jnp.float32)
        positions = jax.random.uniform(ks[4], (N, 3), dtype=jnp.float32)
        qkv_w = jax.random.normal(ks[5], (3 * C, C), dtype=jnp.float32) * 0.02
        qkv_b = jnp.zeros((3 * C,), dtype=jnp.float32)
        proj_w = jax.random.normal(ks[6], (C, C), dtype=jnp.float32) * 0.02
        proj_b = jnp.zeros((C,), dtype=jnp.float32)
        gate_w = jax.random.normal(ks[7], (H, 4), dtype=jnp.float32) * 0.01
        gate_b = jnp.zeros((H,), dtype=jnp.float32)
        return {'x': x, 'edge_index': edge_index, 'edge_values': edge_values, 'positions': positions, 'qkv_w': qkv_w, 'qkv_b': qkv_b, 'proj_w': proj_w, 'proj_b': proj_b, 'gate_w': gate_w, 'gate_b': gate_b}
    _L0_attn_all = _L0_attn_setup()
    _L0_attn_in = {k: v for k, v in _L0_attn_all.items() if k in ('edge_index', 'edge_values', 'positions', 'qkv_w', 'qkv_b', 'proj_w', 'proj_b', 'gate_w', 'gate_b')}
    del _L0_attn_all

    def _L0_ffn_setup():
        import jax, jax.numpy as jnp
        import numpy as np
        B, N, D = (16, 1024, 64)
        NUM_EXPERTS, TOP_K, HEADS = (4, 2, 4)
        N_EDGES = 262144
        LN_EPS = 1e-05

        def _layernorm(x, g, b):
            mu = x.mean(-1, keepdims=True)
            var = ((x - mu) ** 2).mean(-1, keepdims=True)
            return (x - mu) * jax.lax.rsqrt(var + LN_EPS) * g + b

        def _forward(x, edge_index, W_gat, att_src, att_dst, b_gat, ln_gamma, ln_beta, W1, b1, W2, b2):
            Bc, Nc, Dc = x.shape
            M = Bc * Nc
            x_flat = x.reshape(M, Dc)
            h = (x_flat @ W_gat).reshape(M, HEADS, NUM_EXPERTS)
            loops = jnp.arange(M, dtype=edge_index.dtype)
            src = jnp.concatenate([edge_index[0], loops])
            dst = jnp.concatenate([edge_index[1], loops])
            a_src = (h * att_src).sum(-1)
            a_dst = (h * att_dst).sum(-1)
            e = jax.nn.leaky_relu(a_src[src] + a_dst[dst], negative_slope=0.2)
            e_max = jax.ops.segment_max(e, dst, num_segments=M)
            ee = jnp.exp(e - e_max[dst])
            denom = jax.ops.segment_sum(ee, dst, num_segments=M)
            alpha = ee / (denom[dst] + 1e-16)
            msg = h[src] * alpha[:, :, None]
            agg = jax.ops.segment_sum(msg, dst, num_segments=M).reshape(M, HEADS * NUM_EXPERTS) + b_gat
            scores = _layernorm(agg, ln_gamma, ln_beta).reshape(M, HEADS, NUM_EXPERTS).mean(1)
            scores = scores.reshape(Bc, Nc, NUM_EXPERTS)
            topk_s, topk_i = jax.lax.top_k(scores, TOP_K)
            w = jax.nn.softmax(topk_s, axis=-1)
            out = jnp.zeros_like(x)
            for ei in range(NUM_EXPERTS):
                g = jnp.where(topk_i == ei, w, 0.0).sum(-1)
                hh = jax.nn.gelu(x @ W1[ei] + b1[ei], approximate=False)
                out = out + g[..., None] * (hh @ W2[ei] + b2[ei])
            return out
        key = jax.random.key(seed)
        ks = jax.random.split(key, 8)
        s = 0.05
        return {'x': jax.random.normal(ks[0], (B, N, D), jnp.float32), 'W_gat': jax.random.normal(ks[1], (D, HEADS * NUM_EXPERTS), jnp.float32) * s, 'att_src': jax.random.normal(ks[2], (HEADS, NUM_EXPERTS), jnp.float32) * s, 'att_dst': jax.random.normal(ks[3], (HEADS, NUM_EXPERTS), jnp.float32) * s, 'b_gat': jnp.zeros((HEADS * NUM_EXPERTS,), jnp.float32), 'ln_gamma': jnp.ones((HEADS * NUM_EXPERTS,), jnp.float32), 'ln_beta': jnp.zeros((HEADS * NUM_EXPERTS,), jnp.float32), 'W1': jax.random.normal(ks[4], (NUM_EXPERTS, D, 2 * D), jnp.float32) * s, 'b1': jnp.zeros((NUM_EXPERTS, 2 * D), jnp.float32), 'W2': jax.random.normal(ks[5], (NUM_EXPERTS, 2 * D, D), jnp.float32) * s, 'b2': jnp.zeros((NUM_EXPERTS, D), jnp.float32), 'edge_index': jax.random.randint(ks[6], (2, N_EDGES), 0, B * N, jnp.int32)}
    _L0_ffn_all = _L0_ffn_setup()
    _L0_ffn_in = {k: v for k, v in _L0_ffn_all.items() if k in ('W_gat', 'att_src', 'att_dst', 'b_gat', 'ln_gamma', 'ln_beta', 'W1', 'b1', 'W2', 'b2', 'edge_index')}
    del _L0_ffn_all
    return {'x': x, 'L0_tok_base_embeddings': _L0_tok_in['base_embeddings'], 'L0_tok_rule_transform': _L0_tok_in['rule_transform'], 'L0_tok_token_rules': _L0_tok_in['token_rules'], 'L0_attn_edge_index': _L0_attn_in['edge_index'], 'L0_attn_edge_values': _L0_attn_in['edge_values'], 'L0_attn_positions': _L0_attn_in['positions'], 'L0_attn_qkv_w': _L0_attn_in['qkv_w'], 'L0_attn_qkv_b': _L0_attn_in['qkv_b'], 'L0_attn_proj_w': _L0_attn_in['proj_w'], 'L0_attn_proj_b': _L0_attn_in['proj_b'], 'L0_attn_gate_w': _L0_attn_in['gate_w'], 'L0_attn_gate_b': _L0_attn_in['gate_b'], 'L0_ffn_W_gat': _L0_ffn_in['W_gat'], 'L0_ffn_att_src': _L0_ffn_in['att_src'], 'L0_ffn_att_dst': _L0_ffn_in['att_dst'], 'L0_ffn_b_gat': _L0_ffn_in['b_gat'], 'L0_ffn_ln_gamma': _L0_ffn_in['ln_gamma'], 'L0_ffn_ln_beta': _L0_ffn_in['ln_beta'], 'L0_ffn_W1': _L0_ffn_in['W1'], 'L0_ffn_b1': _L0_ffn_in['b1'], 'L0_ffn_W2': _L0_ffn_in['W2'], 'L0_ffn_b2': _L0_ffn_in['b2'], 'L0_ffn_edge_index': _L0_ffn_in['edge_index']}

def reference(x, L0_tok_base_embeddings, L0_tok_rule_transform, L0_tok_token_rules, L0_attn_edge_index, L0_attn_edge_values, L0_attn_positions, L0_attn_qkv_w, L0_attn_qkv_b, L0_attn_proj_w, L0_attn_proj_b, L0_attn_gate_w, L0_attn_gate_b, L0_ffn_W_gat, L0_ffn_att_src, L0_ffn_att_dst, L0_ffn_b_gat, L0_ffn_ln_gamma, L0_ffn_ln_beta, L0_ffn_W1, L0_ffn_b1, L0_ffn_W2, L0_ffn_b2, L0_ffn_edge_index):
    import jax
    import jax.numpy as jnp

    def _L0_tok_ref(token_ids, base_embeddings, rule_transform, token_rules):
        import jax, jax.numpy as jnp
        import numpy as np
        VOCAB = 8000
        EMBED_DIM = 64
        NUM_RULES = 100
        BATCH, SEQ = (4, 512)
        base_embeds = base_embeddings[token_ids]
        rule_indices = token_rules[token_ids]
        rule_matrices = rule_transform[rule_indices]
        return jnp.einsum('bsd,bsde->bse', base_embeds, rule_matrices)

    def _L0_attn_ref(x, edge_index, edge_values, positions, qkv_w, qkv_b, proj_w, proj_b, gate_w, gate_b):
        import jax, jax.numpy as jnp
        import numpy as np
        BS = 32
        NUM_HOPS = 1

        def _connectivity(edge_index, edge_values, positions, nb):
            rows, cols = (edge_index[0], edge_index[1])
            br, bc = (rows // BS, cols // BS)
            in_block = (br == bc) & (br < nb)
            r_l, c_l = (rows % BS, cols % BS)
            b_safe = jnp.where(in_block, br, nb)
            dx = positions[cols] - positions[rows]
            ef_flat = jnp.concatenate([dx, edge_values[:, None]], axis=1)
            adj = jnp.zeros((nb, BS, BS), jnp.float32).at[b_safe, r_l, c_l].set(1.0, mode='drop')
            eye = jnp.eye(BS, dtype=jnp.float32)
            reachable = jnp.broadcast_to(eye[None], (nb, BS, BS))
            cur = adj
            for _ in range(NUM_HOPS):
                reachable = jnp.clip(reachable + cur, 0.0, 1.0)
                cur = jnp.matmul(cur, adj)
            attn_mask = jnp.concatenate([reachable, jnp.ones((nb, BS, 1), jnp.float32)], axis=2)
            edge_feats = jnp.zeros((nb, BS, BS + 1, 4), jnp.float32)
            edge_feats = edge_feats.at[b_safe, r_l, c_l, :].set(ef_flat, mode='drop')
            return (attn_mask, edge_feats)
        B, N, C = x.shape
        H = gate_w.shape[0]
        hd = C // H
        scale = hd ** (-0.5)
        nb = N // BS
        attn_mask, edge_feats = _connectivity(edge_index, edge_values, positions, nb)
        x_blk = x.reshape(B, nb, BS, C)
        block_node = x_blk.mean(axis=2, keepdims=True)
        kv = jnp.concatenate([x_blk, block_node], axis=2)
        qkv_q = x_blk @ qkv_w.T + qkv_b
        qkv_kv = kv @ qkv_w.T + qkv_b
        q = qkv_q[..., :C].reshape(B, nb, BS, H, hd)
        k = qkv_kv[..., C:2 * C].reshape(B, nb, BS + 1, H, hd)
        v = qkv_kv[..., 2 * C:].reshape(B, nb, BS + 1, H, hd)
        scores = jnp.einsum('bnqhd,bnkhd->bnqkh', q, k) * scale
        ar = jnp.arange(BS)
        bias_physics = edge_feats.at[:, :, BS, :].set(0.0).at[:, :, BS, 3].set(1.0)
        bias_physics = bias_physics.at[:, ar, ar, :].set(0.0).at[:, ar, ar, 3].set(1.0)
        scores = scores + bias_physics[None, ..., 3:4]
        mask = attn_mask[None, :, :, :, None]
        scores = jnp.where(mask == 0, -jnp.inf, scores)
        attn_probs = jax.nn.softmax(scores, axis=3)
        gate = bias_physics @ gate_w.T + gate_b
        gate = jnp.where(mask == 0, 0.0, gate[None])
        combined = attn_probs + gate
        x_out = jnp.einsum('bnqkh,bnkhd->bnqhd', combined, v).reshape(B, nb, BS, C)
        out = x_out.reshape(B, N, C) @ proj_w.T + proj_b
        return out

    def _L0_ffn_ref(x, W_gat, att_src, att_dst, b_gat, ln_gamma, ln_beta, W1, b1, W2, b2, edge_index):
        import jax, jax.numpy as jnp
        import numpy as np
        B, N, D = (16, 1024, 64)
        NUM_EXPERTS, TOP_K, HEADS = (4, 2, 4)
        N_EDGES = 262144
        LN_EPS = 1e-05

        def _layernorm(x, g, b):
            mu = x.mean(-1, keepdims=True)
            var = ((x - mu) ** 2).mean(-1, keepdims=True)
            return (x - mu) * jax.lax.rsqrt(var + LN_EPS) * g + b

        def _forward(x, edge_index, W_gat, att_src, att_dst, b_gat, ln_gamma, ln_beta, W1, b1, W2, b2):
            Bc, Nc, Dc = x.shape
            M = Bc * Nc
            x_flat = x.reshape(M, Dc)
            h = (x_flat @ W_gat).reshape(M, HEADS, NUM_EXPERTS)
            loops = jnp.arange(M, dtype=edge_index.dtype)
            src = jnp.concatenate([edge_index[0], loops])
            dst = jnp.concatenate([edge_index[1], loops])
            a_src = (h * att_src).sum(-1)
            a_dst = (h * att_dst).sum(-1)
            e = jax.nn.leaky_relu(a_src[src] + a_dst[dst], negative_slope=0.2)
            e_max = jax.ops.segment_max(e, dst, num_segments=M)
            ee = jnp.exp(e - e_max[dst])
            denom = jax.ops.segment_sum(ee, dst, num_segments=M)
            alpha = ee / (denom[dst] + 1e-16)
            msg = h[src] * alpha[:, :, None]
            agg = jax.ops.segment_sum(msg, dst, num_segments=M).reshape(M, HEADS * NUM_EXPERTS) + b_gat
            scores = _layernorm(agg, ln_gamma, ln_beta).reshape(M, HEADS, NUM_EXPERTS).mean(1)
            scores = scores.reshape(Bc, Nc, NUM_EXPERTS)
            topk_s, topk_i = jax.lax.top_k(scores, TOP_K)
            w = jax.nn.softmax(topk_s, axis=-1)
            out = jnp.zeros_like(x)
            for ei in range(NUM_EXPERTS):
                g = jnp.where(topk_i == ei, w, 0.0).sum(-1)
                hh = jax.nn.gelu(x @ W1[ei] + b1[ei], approximate=False)
                out = out + g[..., None] * (hh @ W2[ei] + b2[ei])
            return out
        return _forward(x, edge_index, W_gat, att_src, att_dst, b_gat, ln_gamma, ln_beta, W1, b1, W2, b2)
    h = _L0_tok_ref(x, L0_tok_base_embeddings, L0_tok_rule_transform, L0_tok_token_rules)
    h = h + _L0_attn_ref(_layernorm(h, axis=-1), L0_attn_edge_index, L0_attn_edge_values, L0_attn_positions, L0_attn_qkv_w, L0_attn_qkv_b, L0_attn_proj_w, L0_attn_proj_b, L0_attn_gate_w, L0_attn_gate_b)
    h = h + _L0_ffn_ref(_layernorm(h, axis=-1), L0_ffn_W_gat, L0_ffn_att_src, L0_ffn_att_dst, L0_ffn_b_gat, L0_ffn_ln_gamma, L0_ffn_ln_beta, L0_ffn_W1, L0_ffn_b1, L0_ffn_W2, L0_ffn_b2, L0_ffn_edge_index)
    return h

_drawn_inputs = setup_inputs


def setup_inputs(seed=0):
    import zlib

    import numpy as np

    out = dict(_drawn_inputs(seed))
    spreads = {'L0_attn_qkv_b': (0.0, 0.8),
     'L0_attn_proj_b': (0.0, 0.505),
     'L0_attn_gate_b': (0.0, 0.8),
     'L0_ffn_b_gat': (0.0, 2.0),
     'L0_ffn_ln_gamma': (1.0, 0.6),
     'L0_ffn_ln_beta': (0.0, 0.8),
     'L0_ffn_b1': (0.0, 0.8),
     'L0_ffn_b2': (0.0, 0.699)}
    factors = {'L0_attn_edge_values': 8.0,
     'L0_attn_positions': 8.0,
     'L0_attn_qkv_w': 8.0,
     'L0_attn_proj_w': 6.522,
     'L0_attn_gate_w': 8.0,
     'L0_ffn_W_gat': 3.447,
     'L0_ffn_att_src': 22.008,
     'L0_ffn_att_dst': 35.888,
     'L0_ffn_W1': 4.15,
     'L0_ffn_W2': 3.292}
    for name, (base, spread) in spreads.items():
        noise = np.random.default_rng([zlib.crc32(name.encode()), seed]).standard_normal(out[name].shape)
        drawn = base * np.exp(spread * noise) if base else spread * noise
        out[name] = jnp.asarray(drawn.astype(out[name].dtype))
    for name, factor in factors.items():
        out[name] = (out[name] * factor).astype(out[name].dtype)
    return out
```

```python
from contextlib import ExitStack

import concourse.bass as bass
from concourse import mybir

FP32 = mybir.dt.float32
BF16 = mybir.dt.bfloat16
I32 = mybir.dt.int32
ALU = mybir.AluOpType
ACT = mybir.ActivationFunctionType
AX = mybir.AxisListType

P = 128
N = 16384
AN = 1024
AT = AN // P
NT = N // P
E = 262144
ET = E // P
J = 8
STEPS = ET // J
PLACES = E + N
RUN = PLACES // P
D = 64
H = 4
HD = 16
BS = 32
NB = P // BS
KV = BS + 1
VOCAB = 8000
VP = 125
VT = VOCAB // VP
RULES = 100
NX = 4
FF = 128
GW = 24
EPS = 1e-5
ABSENT = -1e30
SKIP = float(1 << 20)
MAGIC = 8388608.0
LC = 136
LCN = RUN // LC
GC = 64
GCN = RUN // GC


class Chain:

    def __init__(self, eng, sem):
        self.eng, self.sem, self.base, self.k = eng, sem, 0, 0

    def link(self, ins):
        ins.then_inc(self.sem, 1)
        self.k += 1
        self.eng.wait_ge(self.sem, self.base + self.k)

    def enter(self, i, per, start):
        self.base, self.k, self.per, self.start = i * per + start, 0, per, start

    def leave(self, times):
        assert self.k == self.per, (self.k, self.per)
        self.base, self.k = self.start + self.per * times, 0



def tower(nc, ids, emb, rule_mats, rules, a_edge_t, a_edge_n, a_val_t, pos_t, qkv_wt, qkv_b, proj_wt,
          proj_b, gate_w, gate_wt, gate_b, w_gat, att_src, att_dst, b_gat, ln_g, ln_b, w1, b1t, w2, b2,
          g_edge_t, g_edge_n, out):
    ctx = ExitStack()
    with ctx:
        def sem(name):
            return ctx.enter_context(nc.semaphore(name))

        def sb(name, shape, dt=FP32, where=None):
            return (where or ctx).enter_context(nc.sbuf_tensor(name, shape, dt))

        def dram(name, shape, dt=FP32):
            return nc.dram_tensor(name, shape, dt, kind="Internal").ap()

        words_d = dram("words_d", [VOCAB, D])
        akey_d = dram("akey_d", [ET, P])
        gkey_d = dram("gkey_d", [ET, P])
        asort_d = dram("asort_d", [PLACES, 4])
        gsort_d = dram("gsort_d", [PLACES, 4])
        ascan_d = dram("ascan_d", [PLACES, BS])
        gscan_d = dram("gscan_d", [PLACES, GW])
        node_d = dram("node_d", [N, GW])
        expert_d = dram("expert_d", [P, NT, NX, D])
        credit_d = dram("credit_d", [4, P])

        bank = [ctx.enter_context(nc.psum_tensor(f"bank{n}", [P, 512], FP32)) for n in range(7)]
        pair_ps = bank[0:2]
        cnt_ps = bank[2]
        wk = bank[3:7]
        oht_ps = ctx.enter_context(nc.psum_tensor("oht_ps", [P, 1024], BF16))

        ident = sb("ident", [P, P])
        identb = sb("identb", [P, P], BF16)
        earlier = sb("earlier", [P, P])
        prefix = sb("prefix", [P, P])
        zerob = sb("zerob", [P, P], BF16)
        iota = sb("iota", [P, P])
        iotai = sb("iotai", [P, P], I32)
        node_i = sb("node_i", [P, P], I32)
        node_f = sb("node_f", [P, P])
        sel = sb("sel", [J, J, P])
        part_f = sb("part_f", [P, 1])
        part_i = sb("part_i", [P, 1], I32)
        ones = sb("ones", [P, P])
        a_head, a_end, g_head, g_end = (sb(n, [P, NT], I32) for n in ("a_head", "a_end", "g_head", "g_end"))
        a_first, g_first = sb("a_first", [P, P]), sb("g_first", [P, P])
        scratch = sb("scratch", [P, 6 * J * P])
        oh_hi = scratch[:, 0:J * P].bitcast(BF16).rearrange("p (b j e) -> p b j e", b=2, j=J)
        oh_lo = scratch[:, J * P:2 * J * P].bitcast(BF16).rearrange("p (b j e) -> p b j e", b=2, j=J)
        oht = scratch[:, 2 * J * P:4 * J * P].rearrange("p (b j e) -> p b j e", b=2, j=J)
        junk = scratch[:, 4 * J * P:6 * J * P].bitcast(BF16).rearrange("p (b k j e) -> p b k j e", b=2, k=2, j=J)
        table = sb("table", [P, 2, P])
        krow = sb("krow", [J, 2, P])
        keys = sb("keys", [P, 2, 4 * J])
        before = sb("before", [P, 2, 3, J])
        place = sb("place", [P, 2, J], I32)
        record = sb("record", [P, 2, J, 4])

        s_const, s_load, s_dve, s_act, s_pool = (sem(n) for n in ("s_const", "s_load", "s_dve", "s_act", "s_pool"))
        s_tick = sem("s_tick")
        dve_n = [0]

        both = ctx.enter_context(ExitStack())
        a_val = sb("a_val", [P, AT, BS])
        h_all = sb("h_all", [P, NT, D])
        mean = sb("mean", [P, NT])
        rstd = sb("rstd", [P, NT])
        g_keys = sb("g_keys", [P, (STEPS + 1) * 4 * J], where=both)
        g_pay = sb("g_pay", [P, ET * 2], I32, both)

        early = ExitStack()
        a_keys = sb("a_keys", [P, (STEPS + 1) * 4 * J], where=early)
        a_pay = sb("a_pay", [P, ET * 2], where=early)
        prep = ExitStack()
        er = sb("er", [P, ET], I32, prep)
        ec = sb("ec", [P, ET], I32, prep)
        spare = h_all[:, :, :].rearrange("p t d -> p (t d)")
        t0, t1 = (spare[:, x * ET:(x + 1) * ET].bitcast(I32) for x in range(2))
        f0, f1 = (spare[:, x * ET:(x + 1) * ET] for x in range(2, 4))
        s_er, s_free, s_keys, s_kd = sem("s_er"), sem("s_free"), sem("s_keys"), sem("s_kd")
        s_ms = sem("s_ms")
        with nc.Block() as block:
            @block.sync
            def _(sp):
                natural = lambda a: a.rearrange("(b q) p -> q b p", q=P)
                blocks = lambda a: a[:, :].rearrange("q (b p) -> q b p", p=P)
                sp.dma_start(er[:, :], a_edge_t[0]).then_inc(s_er, 16)
                sp.dma_start(ec[:, :], a_edge_t[1]).then_inc(s_er, 16)
                sp.dma_start(f0[:, :], a_val_t[:, :]).then_inc(s_er, 16)
                sp.wait_ge(s_free, 1)
                sp.dma_start(blocks(er), natural(a_edge_n[0])).then_inc(s_er, 16)
                sp.dma_start(blocks(ec), natural(a_edge_n[1])).then_inc(s_er, 16)
                sp.wait_ge(s_keys, 1)
                sp.dma_start(natural(akey_d), blocks(f0)).then_inc(s_kd, 16)
                sp.dma_start(er[:, :], g_edge_t[1]).then_inc(s_er, 16)
                sp.dma_start(ec[:, :], g_edge_t[0]).then_inc(s_er, 16)
                sp.wait_ge(s_free, 2)
                sp.dma_start(blocks(er), natural(g_edge_n[1])).then_inc(s_er, 16)
                sp.wait_ge(s_keys, 2)
                sp.dma_start(natural(gkey_d), blocks(f1)).then_inc(s_kd, 16)
                sp.wait_ge(s_kd, 32)

            @block.vector
            def _(dve):
                ch = Chain(dve, s_dve)

                def attention_keys(key, valid):
                    ch.link(dve.tensor_scalar(t0[:, :], er[:, :], 5, None, ALU.logical_shift_right))
                    ch.link(dve.tensor_scalar(t1[:, :], ec[:, :], 5, None, ALU.logical_shift_right))
                    ch.link(dve.tensor_tensor(valid[:, :], t0[:, :], t1[:, :], ALU.is_equal))
                    ch.link(dve.tensor_scalar(t1[:, :], er[:, :], float(AN), None, ALU.is_lt))
                    ch.link(dve.tensor_tensor(valid[:, :], valid[:, :], t1[:, :], ALU.mult))
                    ch.link(dve.scalar_tensor_tensor(out=key, in0=er[:, :], scalar=-float(N), in1=valid[:, :],
                                                     op0=ALU.add, op1=ALU.mult))
                    ch.link(dve.tensor_scalar(key, key, float(N), None, ALU.add))

                def split(keys_, key):
                    f = keys_[:, :].rearrange("p (s f j) -> p f s j", f=4, j=J)
                    tiles = lambda x: x[:, :].rearrange("p (s j) -> p s j", j=J)
                    ch.link(dve.tensor_copy(f[:, 0, 0:STEPS], tiles(key)))
                    ch.link(dve.tensor_copy(t0[:, :], key[:, :]))
                    ch.link(dve.tensor_scalar(t1[:, :], t0[:, :], P - 1, None, ALU.bitwise_and))
                    ch.link(dve.tensor_copy(f[:, 1, 0:STEPS], tiles(t1)))
                    ch.link(dve.tensor_scalar(t1[:, :], t0[:, :], 7, None, ALU.logical_shift_right))
                    ch.link(dve.tensor_copy(f[:, 2, 0:STEPS], tiles(t1)))
                    ch.link(dve.memset(f[:, :, STEPS, :], 0.0))
                    return f[:, 3, 0:STEPS], tiles

                dve.wait_ge(s_er, 48)
                ch.link(dve.tensor_copy(a_pay[:, :].rearrange("p (t f) -> p t f", f=2)[:, :, 1], f0[:, :]))
                attention_keys(f0[:, :], f1)
                inv, tiles = split(a_keys, f0)
                ch.link(dve.tensor_scalar(inv, tiles(f1), -SKIP, SKIP, ALU.mult, ALU.add))
                ch.link(dve.tensor_scalar(t0[:, :], ec[:, :], BS - 1, None, ALU.bitwise_and))
                ins = dve.tensor_copy(a_pay[:, :].rearrange("p (t f) -> p t f", f=2)[:, :, 0], t0[:, :])
                ch.link(ins)
                dve.sem_inc(s_free, 1)
                dve.wait_ge(s_er, 80)
                attention_keys(f0[:, :], f1)
                dve.sem_inc(s_keys, 1)
                dve.wait_ge(s_er, 112)
                ch.link(dve.tensor_copy(f1[:, :], er[:, :]))
                inv, _ = split(g_keys, f1)
                ch.link(dve.memset(inv, 0.0))
                pay = g_pay[:, :].rearrange("p (t f) -> p t f", f=2)
                ch.link(dve.tensor_copy(pay[:, :, 0], ec[:, :]))
                ch.link(dve.tensor_copy(pay[:, :, 1], er[:, :]))
                dve.sem_inc(s_free, 1)
                dve.wait_ge(s_er, 128)
                ch.link(dve.tensor_copy(f1[:, :], er[:, :]))
                dve.sem_inc(s_keys, 1)
                dve.wait_ge(s_const, 3)
                ch.link(dve.tensor_copy(iota[:, :], iotai[:, :]))
                ch.link(dve.tensor_copy(node_f[:, :], node_i[:, :]))
                ch.link(dve.tensor_copy(part_f[:, :], part_i[:, :]))
                dve.wait_ge(s_ms, 10)
                ch.link(dve.tensor_copy(identb[:, :], ident[:, :]))
                dve_n[0] = ch.k

            @block.gpsimd
            def _(pool):
                pool.iota(iotai[:, :], [[1, P]], base=0, channel_multiplier=0).then_inc(s_const, 1)
                pool.iota(node_i[:, :], [[1, P]], base=0, channel_multiplier=P).then_inc(s_const, 1)
                pool.iota(part_i[:, :], [[0, 1]], base=0, channel_multiplier=RUN).then_inc(s_const, 1)
                pool.memset(zerob[:, :], 0.0).then_inc(s_ms, 1)
                pool.memset(ident[:, :], 0.0).then_inc(s_ms, 1)
                pool.memset(ones[:, :], 1.0).then_inc(s_ms, 1)
                pool.memset(earlier[:, :], 1.0).then_inc(s_ms, 1)
                pool.memset(prefix[:, :], 1.0).then_inc(s_ms, 1)
                pool.memset(sel[:, :, :], 0.0).then_inc(s_ms, 1)
                pool.wait_ge(s_ms, 6)
                pool.affine_select(out=ident[:, :], in_=ident[:, :], compare_op=ALU.not_equal, fill=1.0, base=0,
                                   pattern=[[-1, P]], channel_multiplier=1).then_inc(s_ms, 1)
                pool.affine_select(out=earlier[:, :], in_=earlier[:, :], compare_op=ALU.is_gt, fill=0.0, base=0,
                                   pattern=[[-1, P]], channel_multiplier=1).then_inc(s_ms, 1)
                pool.affine_select(out=prefix[:, :], in_=prefix[:, :], compare_op=ALU.is_gt, fill=0.0, base=0,
                                   pattern=[[1, P]], channel_multiplier=-1).then_inc(s_ms, 1)
                pool.affine_select(out=sel[:, :, :], in_=sel[:, :, :], compare_op=ALU.not_equal, fill=1.0, base=0,
                                   pattern=[[-1, J], [0, P]], channel_multiplier=1).then_inc(s_ms, 1)
        prep.close()

        def one_hots(dve, keys_, step, par, signal):
            f = keys_[:, :].rearrange("p (s f) -> p s f", f=4 * J)
            cols = iota[:, :].unsqueeze(1).broadcast_to([P, J, P])
            for buf, field in ((oh_hi, 2), (oh_lo, 1)):
                k = f[:, bass.ds(step, 1), field * J:(field + 1) * J].rearrange("p a j -> p (a j)")
                ins = dve.tensor_tensor(buf[:, par], k.unsqueeze(2).broadcast_to([P, J, P]), cols, ALU.is_equal)
            ins.then_inc(signal, 1)

        ones128 = ones[:, :]

        def count_pass(tag, keys_, head, end, first):
            s_oh, s_used, s_cnt, s_st = sem(tag + "_oh"), sem(tag + "_used"), sem(tag + "_cnt"), sem(tag + "_st")
            tmp = ExitStack()
            cnt = sb(tag + "_c", [P, P], where=tmp)
            inc = sb(tag + "_i", [P, P], where=tmp)
            hp = sb(tag + "_h", [P, P], where=tmp)
            ep = sb(tag + "_e", [P, P], where=tmp)
            with nc.Block() as block:
                @block.vector
                def _(dve):
                    ch = Chain(dve, s_dve)
                    ch.base = dve_n[0]
                    with dve.Fori(0, STEPS // 2) as i:
                        for par in range(2):
                            dve.wait_ge(s_used, i * 2 + (par + 1))
                            one_hots(dve, keys_, i * 2 + par, par, s_oh)
                    dve.wait_ge(s_cnt, 1)
                    ch.link(dve.tensor_copy(cnt[:, :], cnt_ps[:, 0:P]))
                    ch.link(dve.tensor_tensor_scan(inc[:, :], ones128, cnt[:, :], 0.0, ALU.mult, ALU.add))
                    dve.sem_inc(s_st, 1)
                    dve.wait_ge(s_cnt, 2)
                    ch.link(dve.tensor_tensor(hp[:, :], inc[:, :], cnt[:, :], ALU.subtract))
                    ch.link(dve.tensor_scalar(hp[:, :], hp[:, :], cnt_ps[:, P:P + 1], None, ALU.add))
                    ch.link(dve.tensor_tensor(hp[:, :], hp[:, :], node_f[:, :], ALU.add))
                    ch.link(dve.tensor_tensor(ep[:, :], hp[:, :], cnt[:, :], ALU.add))
                    ch.link(dve.tensor_scalar(first[:, :], hp[:, :], 1.0, None, ALU.add))
                    dve.sem_inc(s_st, 1)
                    dve.wait_ge(s_cnt, 3)
                    ch.link(dve.tensor_copy(head[:, :], wk[0][:, 0:P]))
                    ch.link(dve.tensor_copy(end[:, :], wk[0][:, P:2 * P]))
                    dve_n[0] += ch.k

                @block.tensor
                def _(pe):
                    pe.sem_inc(s_used, 2)
                    pe.matmul(cnt_ps[:, 0:P], zerob[:, :], zerob[:, :], start=True, stop=False, skip_group_check=True)
                    with pe.Fori(0, STEPS // 2) as i:
                        for par in range(2):
                            pe.wait_ge(s_oh, i * 2 + (par + 1))
                            for j in range(J):
                                m = pe.matmul(cnt_ps[:, 0:P], oh_hi[:, par, j], oh_lo[:, par, j],
                                              start=False, stop=False, skip_group_check=True)
                            m.then_inc(s_used, 1)
                    pe.matmul(cnt_ps[:, 0:P], zerob[:, :], zerob[:, :], start=False, stop=True,
                              skip_group_check=True).then_inc(s_cnt, 1)
                    pe.wait_ge(s_st, 1)
                    pe.matmul(cnt_ps[:, P:P + 1], prefix[:, :], inc[:, P - 1:P], start=True, stop=True).then_inc(s_cnt, 1)
                    pe.wait_ge(s_st, 2)
                    pe.transpose(wk[0][:, 0:P], hp[:, :], ident[:, :])
                    pe.transpose(wk[0][:, P:2 * P], ep[:, :], ident[:, :]).then_inc(s_cnt, 1)
            tmp.close()

        count_pass("ac", a_keys, a_head, a_end, a_first)
        count_pass("gc", g_keys, g_head, g_end, g_first)

        class Rank:

            def __init__(self, tag, keys_, pay, first, key_d, sort_d, rec_f):
                self.keys, self.pay, self.first, self.key_d, self.sort_d, self.rec_f = keys_, pay, first, key_d, sort_d, rec_f
                self.oh, self.ready, self.used = sem(tag + "_oh2"), sem(tag + "_ready"), sem(tag + "_used2")
                self.oht_ps, self.oht_sb, self.upd = sem(tag + "_oht_ps"), sem(tag + "_oht_sb"), sem(tag + "_upd")
                self.tab, self.place, self.sum = sem(tag + "_tab"), sem(tag + "_place"), sem(tag + "_sum")
                self.done = [sem(f"{tag}_done{x}") for x in range(2)]
                self.kr = [sem(f"{tag}_kr{x}") for x in range(2)]

            def sp_step(self, sp, i, par, last=False):
                sp.wait_ge(self.upd, i * (2 * J) + (par * J + J + 1))
                sp.dma_start(krow[:, par], self.key_d[bass.ds(i * (2 * J) + par * J, J), :]).then_inc(self.kr[par], 16)

            def pe_start(self, pe):
                pe.matmul(cnt_ps[:, 0:P], ident[:, :], self.first[:, :], start=True, stop=False,
                          skip_group_check=True).then_inc(self.upd, 2 * J + 1)
                pe.wait_ge(self.oh, 1)
                self.pe_transposes(pe, 0, 1)

            def pe_transposes(self, pe, par, n):
                pe.wait_ge(self.oht_sb, n)
                for j in range(J):
                    m = pe.transpose(oht_ps[:, j * P:(j + 1) * P], oh_hi[:, par, j], identb[:, :])
                m.then_inc(self.oht_ps, 1)

            def pe_ahead(self, pe, i, par):
                pe.wait_ge(self.oh, i * 2 + (par + 2))
                self.pe_transposes(pe, 1 - par, i * 2 + (par + 2))

            def pe_step(self, pe, i, par, between=None):
                pe.wait_ge(self.kr[par], i * 16 + 16)
                for j in range(J):
                    self.pe_tile(pe, i, par, j)
                    if j == J // 2:
                        self.pe_ahead(pe, i, par)
                    if between:
                        between(par * J + j)

            def act_step(self, act, i, par, between=None):
                for j in range(J):
                    self.act_tile(act, i, par, j)
                    if j == J // 2:
                        self.act_ahead(act, i, par)
                    if between:
                        between(par * J + j)

            def dve_step(self, dve, i, par, between=None):
                self.dve_ahead(dve, i, par)
                for j in range(J):
                    self.dve_tile(dve, i, par, j)
                    if between:
                        between(par * J + j)
                self.dve_places(dve, i, par)

            def pe_tile(self, pe, i, par, j):
                ps = pair_ps[j // 2 % 2]
                if j % 2 == 0:
                    pe.wait_ge(self.used, i * J + (par * J // 2 + j // 2 + 1))
                pe.matmul(ps[:, bass.ts(j % 2, P)], sel[:, j], krow[:, par], start=True, stop=True)
                pe.wait_ge(self.tab, i * (2 * J) + (par * J + j + 1))
                x = pe.matmul(ps[:, bass.ts(2 + j % 2, P)], oht[:, par, j], table[:, j % 2], start=True, stop=True)
                if j % 2:
                    x.then_inc(self.ready, 1)
                pe.matmul(cnt_ps[:, 0:P], oh_hi[:, par, j], oh_lo[:, par, j], start=False, stop=False,
                          skip_group_check=True).then_inc(self.upd, 1)

            def act_start(self, act):
                act.sem_inc(self.oht_sb, 1)
                act.wait_ge(self.oht_ps, 1)
                act.activation(oht[:, 0].rearrange("p j e -> p (j e)"), oht_ps[:, :], ACT.Copy).then_inc(self.oht_sb, 1)

            def act_ahead(self, act, i, par):
                act.wait_ge(self.oht_ps, i * 2 + (par + 2))
                act.wait_ge(self.upd, i * (2 * J) + (par * J + 2 * J + 1))
                act.activation(oht[:, 1 - par].rearrange("p j e -> p (j e)"), oht_ps[:, :], ACT.Copy).then_inc(self.oht_sb, 1)

            def act_tile(self, act, i, par, j):
                act.wait_ge(self.upd, i * (2 * J) + (par * J + j + 2 * J + 1))
                if j % J == 0:
                    act.wait_ge(self.oht_sb, i * 2 + (par + 2))
                act.activation(table[:, j % 2], cnt_ps[:, 0:P], ACT.Copy).then_inc(self.tab, 1)

            def dve_start(self, dve, ch):
                ch.link(dve.memset(record[:, :, :, :], 1.0))
                dve.sem_inc(self.used, 2)
                dve.wait_ge(self.upd, 1)
                one_hots(dve, self.keys, 0, 0, self.oh)

            def dve_ahead(self, dve, i, par):
                dve.wait_ge(self.upd, i * (2 * J) + (par * J + 2 * J + 1))
                one_hots(dve, self.keys, i * 2 + (par + 1), 1 - par, self.oh)
                dve.wait_ge(self.done[par], i * (16 * J) + 16)
                f = self.keys[:, :].rearrange("p (s f) -> p s f", f=4 * J)
                dve.tensor_scalar(keys[:, par], f[:, bass.ds(i * 2 + par, 1), :].rearrange("p a f -> p (a f)"), 0.0, None,
                                  ALU.add).then_inc(self.sum, 1)
                pv = self.pay[:, :].rearrange("p (s j f) -> p s (j f)", j=J, f=2)
                src = pv[:, bass.ds(i * 2 + par, 1), :].rearrange("p a (j f) -> p (a j) f", f=2)
                rec = record[:, par] if self.rec_f == FP32 else record[:, par].bitcast(I32)
                off = 1 if self.rec_f == FP32 else 0
                dve.tensor_copy(rec[:, :, off:off + 2], src).then_inc(self.sum, 1)
                dve.wait_ge(self.sum, i * 6 + (par * 3 + 2))

            def dve_tile(self, dve, i, par, j):
                ps = pair_ps[j // 2 % 2]
                if j % 2 == 0:
                    dve.wait_ge(self.ready, i * J + (par * J // 2 + j // 2 + 1))
                dve.scalar_tensor_tensor(out=junk[:, par, 0, j], in0=ps[:, bass.ts(j % 2, P)], scalar=keys[:, par, j:j + 1],
                                         in1=earlier[:, :], op0=ALU.is_equal, op1=ALU.mult,
                                         accum_out=before[:, par, 0, j:j + 1])
                x = dve.scalar_tensor_tensor(out=junk[:, par, 1, j], in0=iota[:, :], scalar=keys[:, par, J + j:J + j + 1],
                                             in1=ps[:, bass.ts(2 + j % 2, P)], op0=ALU.is_equal, op1=ALU.mult,
                                             accum_out=before[:, par, 1, j:j + 1])
                if j % 2:
                    x.then_inc(self.used, 1)

            def dve_places(self, dve, i, par):
                dve.wait_ge(self.used, i * J + ((par + 1) * J // 2 + 2))
                dve.tensor_tensor(before[:, par, 2], before[:, par, 0], before[:, par, 1], ALU.add).then_inc(self.sum, 1)
                dve.wait_ge(self.sum, i * 6 + (par * 3 + 3))
                dve.tensor_tensor(place[:, par], before[:, par, 2], keys[:, par, 3 * J:4 * J], ALU.add).then_inc(self.place, 1)

            def pool_start(self, pool):
                for par in range(2):
                    pool.dma_start(credit_d[par:par + 1, :], ones[0:1, :]).then_inc(self.done[par], 16)

            def pool_step(self, pool, i, par):
                pool.wait_ge(self.place, i * 2 + (par + 1))
                pool.sem_inc(s_tick, 1)
                for j in range(J):
                    pool.indirect_dma_start(
                        out=self.sort_d[:, :], out_offset=bass.IndirectOffsetOnAxis(ap=place[:, par, j:j + 1], axis=0),
                        in_=record[:, par, j], in_offset=None, bounds_check=PLACES - 1,
                        oob_is_err=False).then_inc(self.done[par], 16)

            def pool_end(self, pool):
                for par in range(2):
                    pool.wait_ge(self.done[par], 16 + 16 * J * (STEPS // 2))

        a_rank = Rank("ar", a_keys, a_pay, a_first, akey_d, asort_d, FP32)
        g_rank = Rank("gr", g_keys, g_pay, g_first, gkey_d, gsort_d, I32)

        tmp = ExitStack()
        mats = sb("mats", [VP, D * D], where=tmp)
        prod = sb("prod", [VP, D * D], where=tmp)
        wsum = sb("wsum", [VP, D], where=tmp)
        words = h_all[0:VP, 0:VT, :]
        rule_i = sb("rule_i", [VP, VT], I32, tmp)
        rule_c = sb("rule_c", [VP, VT], I32, tmp)
        ridx = sb("ridx", [VP, 2], I32, tmp)
        a_rec = sb("a_rec", [P, 4], where=tmp)
        s_w, s_ridx, s_mat, s_wd, s_hd, s_arec, s_wst, s_fill = (sem(n) for n in ("s_w", "s_ridx", "s_mat", "s_wd", "s_hd", "s_arec", "s_wst", "s_fill"))
        s_mats = [sem(f"s_mat{x}") for x in range(2)]
        VPI = 2
        with nc.Block() as block:
            @block.sync
            def _(sp):
                sp.dma_start(words[:, :, :], emb.rearrange("(p t) d -> p t d", t=VT)).then_inc(s_w, 16)
                sp.dma_start(rule_i[:, :], rules.rearrange("(p t) -> p t", t=VT)).then_inc(s_w, 16)
                sp.wait_ge(s_arec, 1)
                sp.dma_start(asort_d.rearrange("(p t) f -> p t f", p=P),
                             a_rec[:, :].unsqueeze(1).broadcast_to([P, RUN, 4])).then_inc(s_fill, 16)
                with sp.Fori(0, STEPS // 2) as i:
                    for par in range(2):
                        a_rank.sp_step(sp, i, par)
                sp.wait_ge(s_wd, VT)
                sp.dma_start(words_d.rearrange("(p t) d -> p t d", t=VT), words[:, :, :]).then_inc(s_wst, 16)
                sp.wait_ge(s_wst, 16)

            @block.tensor
            def _(pe):
                a_rank.pe_start(pe)
                with pe.Fori(0, STEPS // 2) as i:
                    for par in range(2):
                        a_rank.pe_step(pe, i, par)

            @block.scalar
            def _(act):
                a_rank.act_start(act)
                with act.Fori(0, STEPS // 2) as i:
                    for par in range(2):
                        a_rank.act_step(act, i, par)

            @block.vector
            def _(dve):
                ch = Chain(dve, s_dve)
                ch.base = dve_n[0]
                ch.link(dve.memset(a_rec[:, :], 0.0))
                ch.link(dve.memset(a_rec[:, 2:3], ABSENT))
                dve.sem_inc(s_arec, 1)
                dve.wait_ge(s_w, 32)
                ch.link(dve.tensor_scalar(rule_c[:, :], rule_i[:, :], 0.0, float(RULES - 1), ALU.max, ALU.min))
                a_rank.dve_start(dve, ch)
                start = ch.base + ch.k
                with dve.Fori(0, VT) as i:
                    ch.enter(i, 5, start)
                    wt = 0
                    ch.link(dve.tensor_copy(ridx[:, 0:1], rule_c[:, bass.ds(i, 1)]))
                    dve.sem_inc(s_ridx, 1)
                    for step in range(4):
                        a_rank.dve_step(dve, i * 2 + step // 2, step % 2)
                        if step == 2:
                            dve.wait_ge(s_mat, i * 16 + 16)
                            m = mats[:, :]
                            w = words[:, bass.ds(i, 1), :].rearrange("p a d -> p (a d)")
                            ch.link(dve.tensor_tensor(prod[:, :].rearrange("p (d e) -> p d e", e=D),
                                                      m.rearrange("p (d e) -> p d e", e=D),
                                                      w.unsqueeze(2).broadcast_to([VP, D, D]), ALU.mult))
                            ch.link(dve.tensor_reduce(wsum[:, :], prod[:, :].rearrange("p (d e) -> p e d", e=D),
                                                      AX.X, ALU.add))
                            ch.link(dve.tensor_scalar(w, wsum[:, :], 0.0, None, ALU.add))
                            dve.sem_inc(s_wd, 1)
                    ch.link(dve.memset(prod[:, 0:1], 0.0))
                ch.leave(VT)
                dve_n[0] = ch.base

            @block.gpsimd
            def _(pool):
                a_rank.pool_start(pool)
                pool.wait_ge(s_fill, 16)
                for t in range(NT):
                    pool.indirect_dma_start(out=asort_d[:, :], out_offset=bass.IndirectOffsetOnAxis(ap=a_head[:, t:t + 1], axis=0),
                                            in_=a_rec[:, :], in_offset=None, bounds_check=PLACES - 1,
                                            oob_is_err=False).then_inc(s_hd, 16)
                with pool.Fori(0, VT) as i:
                    pool.wait_ge(s_ridx, i + 1)
                    pool.sem_inc(s_tick, 1)
                    pool.indirect_dma_start(out=mats[:, :], out_offset=None, in_=rule_mats[:, :],
                                            in_offset=bass.IndirectOffsetOnAxis(ap=ridx[:, 0:1], axis=0)).then_inc(s_mat, 16)
                    for step in range(4):
                        a_rank.pool_step(pool, i * 2 + step // 2, step % 2)
                a_rank.pool_end(pool)
                pool.wait_ge(s_hd, 16 * NT)
        tmp.close()
        early.close()

        a_vals = sb("a_vals", [P, NT, BS], where=both)
        tmp = ExitStack()
        work = sb("work", [P, 2 * LC * BS], where=tmp)
        cen = work[:, 0:NT * D].rearrange("p (t d) -> p t d", d=D)
        rec = scratch[:, 0:8 * LC].rearrange("p (b t f) -> p b t f", b=2, f=4)
        lead = scratch[:, 8 * LC:10 * LC].rearrange("p (b t) -> p b t", b=2)
        keepm = work[:, 0:LC * BS].rearrange("p (t c) -> p t c", c=BS)
        evin = work[:, LC * BS:2 * LC * BS].rearrange("p (t c) -> p t c", c=BS)
        last = sb("last", [P, 2, LC, BS], where=tmp)
        nlead = sb("nlead", [P, 1], where=tmp)
        part = sb("part", [P, 1], where=tmp)
        thru = sb("thru", [P, 1], where=tmp)
        thrub = sb("thrub", [P, BS], where=tmp)
        tt = scratch[0:BS, 10 * LC + 0 * P:10 * LC + 1 * P]
        d0 = scratch[0:BS, 10 * LC + 1 * P:10 * LC + 2 * P]
        d1 = scratch[0:BS, 10 * LC + 2 * P:10 * LC + 3 * P]
        cout = scratch[0:BS, 10 * LC + 3 * P:10 * LC + 4 * P]
        cinn = scratch[0:BS, 10 * LC + 4 * P:10 * LC + 5 * P]
        fixf = sb("fixf", [P, 4], where=tmp)
        fixi = sb("fixi", [P, 2], I32, tmp)
        fixv = sb("fixv", [P, BS], where=tmp)
        fixw = sb("fixw", [P, BS], where=tmp)
        diag = sb("diag", [P, BS], where=tmp)
        ndiag = sb("ndiag", [P, BS], where=tmp)
        id_raw = scratch[:, 10 * LC + 5 * P:10 * LC + 6 * P].bitcast(I32)
        id_f = scratch[:, 10 * LC + 6 * P:10 * LC + 7 * P]
        id_n = scratch[:, 10 * LC + 7 * P:10 * LC + 8 * P]
        id_i = scratch[:, 10 * LC + 8 * P:10 * LC + 9 * P].bitcast(I32)

        def stats(dve, ch, x, cen, s_var, s_std):
            n = 1.0 / D
            ch.link(dve.tensor_reduce(mean[:, :], x[:, :, :], AX.X, ALU.add))
            ch.link(dve.tensor_scalar(mean[:, :], mean[:, :], n, None, ALU.mult))
            ch.link(dve.tensor_tensor(cen[:, :, :], x[:, :, :], mean[:, :].unsqueeze(2).broadcast_to([P, NT, D]), ALU.subtract))
            ch.link(dve.tensor_tensor(cen[:, :, :], cen[:, :, :], cen[:, :, :], ALU.mult))
            ch.link(dve.tensor_reduce(rstd[:, :], cen[:, :, :], AX.X, ALU.add))
            ch.link(dve.tensor_scalar(rstd[:, :], rstd[:, :], n, EPS, ALU.mult, ALU.add))
            dve.sem_inc(s_var, 1)
            dve.wait_ge(s_std, 1)
            ch.link(dve.reciprocal(rstd[:, :], rstd[:, :]))

        s_pos = sem("s_pos")
        pos_d = dram("pos_d", [3, N])
        s_id, s_idx, s_tok, s_var, s_std = sem("s_id"), sem("s_idx"), sem("s_tok"), sem("s_var"), sem("s_std")
        s_rec = [sem(f"s_rec{x}") for x in range(2)]
        s_st = [sem(f"s_st{x}") for x in range(2)]
        s_rfree, s_last = sem("s_rfree"), sem("s_last")
        s_fx, s_fpe, s_fg, s_fs, s_av = sem("s_fx"), sem("s_fpe"), sem("s_fg"), sem("s_fs"), sem("s_av")
        scan_v = ascan_d.rearrange("(p t) f -> p t f", p=P)
        with nc.Block() as block:
            @block.sync
            def _(sp):
                sp.dma_start(id_raw[:, :], ids[:, :]).then_inc(s_id, 16)
                sp.dma_start(pos_d.rearrange("k (s n) -> k s n", n=AN),
                             pos_t[:, 0:AN].unsqueeze(1).broadcast_to([3, NT // AT, AN])).then_inc(s_pos, 16)
                sp.wait_ge(s_pos, 16)
                for par in range(2):
                    sp.dma_start(credit_d[par:par + 1, :], ones[0:1, :]).then_inc(s_st[par], 16)
                v = asort_d.rearrange("(p t) f -> p t f", p=P)
                with sp.Fori(0, LCN // 2) as i:
                    for par in range(2):
                        sp.wait_ge(s_rfree, i * 2 + (par + 1))
                        sp.dma_start(rec[:, par], v[:, bass.ds(i * (2 * LC) + par * LC, LC), :]).then_inc(s_rec[par], 16)
                    for par in range(2):
                        sp.wait_ge(s_last, i * 2 + (par + 1))
                        sp.dma_start(scan_v[:, bass.ds(i * (2 * LC) + par * LC, LC), :], last[:, par]).then_inc(s_st[par], 16)
                for par in range(2):
                    sp.wait_ge(s_st[par], 16 + 16 * (LCN // 2))

            @block.vector
            def _(dve):
                ch = Chain(dve, s_dve)
                ch.base = dve_n[0]
                dve.wait_ge(s_id, 16)
                ch.link(dve.tensor_copy(id_f[:, :], id_raw[:, :]))
                ch.link(dve.tensor_scalar(id_n[:, :], id_f[:, :], 0.0, float(VOCAB), ALU.is_lt, ALU.mult))
                ch.link(dve.tensor_tensor(id_f[:, :], id_f[:, :], id_n[:, :], ALU.add))
                ch.link(dve.tensor_scalar(id_i[:, :], id_f[:, :], 0.0, float(VOCAB - 1), ALU.max, ALU.min))
                dve.sem_inc(s_idx, 1)
                ch.link(dve.memset(last[:, 1, LC - 1, :], ABSENT))
                ch.link(dve.memset(lead[:, 1, LC - 1:LC], 1.0))
                ch.link(dve.memset(nlead[:, :], 0.0))
                ch.link(dve.tensor_reduce(diag[:, :], ident[:, :].rearrange("p (b c) -> p c b", c=BS), AX.X, ALU.add))
                ch.link(dve.tensor_scalar(ndiag[:, :], diag[:, :], -1.0, 1.0, ALU.mult, ALU.add))
                dve.sem_inc(s_rfree, 2)
                start = ch.base + ch.k
                with dve.Fori(0, LCN // 2) as i:
                    ch.enter(i, 12, start)
                    for par in range(2):
                        dve.wait_ge(s_rec[par], i * 16 + 16)
                        dve.wait_ge(s_st[par], i * 16 + 16)
                        keep, col, val = (rec[:, par, :, f] for f in range(3))
                        for c in range(BS):
                            x = dve.scalar_tensor_tensor(out=keepm[:, :, c], in0=keep, scalar=float(c), in1=col,
                                                         op0=ALU.mult, op1=ALU.not_equal)
                        ch.link(x)
                        ch.link(dve.scalar_tensor_tensor(out=evin[:, :, :], in0=keepm[:, :, :], scalar=0.5,
                                                         in1=val.unsqueeze(2).broadcast_to([P, LC, BS]),
                                                         op0=ALU.is_lt, op1=ALU.mult))
                        for c in range(BS):
                            x = dve.tensor_tensor_scan(last[:, par, :, c], keepm[:, :, c], evin[:, :, c],
                                                       last[:, 1 - par, LC - 1, c:c + 1], ALU.mult, ALU.add)
                        ch.link(x)
                        dve.sem_inc(s_last, 1)
                        ch.link(dve.tensor_tensor_scan(lead[:, par], keep, keep, lead[:, 1 - par, LC - 1:LC], ALU.mult, ALU.mult))
                        ch.link(dve.tensor_reduce(part[:, :], lead[:, par], AX.X, ALU.add))
                        dve.sem_inc(s_rfree, 1)
                        ch.link(dve.tensor_tensor(nlead[:, :], nlead[:, :], part[:, :], ALU.add))
                ch.leave(LCN // 2)
                ch.link(dve.tensor_scalar(thru[:, :], nlead[:, :], float(RUN), None, ALU.is_equal))
                ch.link(dve.tensor_copy(thrub[:, :], thru[:, :].broadcast_to([P, BS])))
                ch.link(dve.tensor_tensor(fixf[:, 0:1], nlead[:, :], part_f[:, :], ALU.add))
                ch.link(dve.tensor_scalar(fixf[:, 0:1], fixf[:, 0:1], -1.0, None, ALU.add))
                ch.link(dve.tensor_scalar(fixf[:, 1:2], fixf[:, 0:1], 0.0, None, ALU.max))
                ch.link(dve.tensor_copy(fixi[:, 0:1], fixf[:, 1:2]))
                ch.link(dve.tensor_scalar(fixf[:, 2:3], nlead[:, :], 0.0, SKIP, ALU.is_equal, ALU.mult))
                ch.link(dve.tensor_tensor(fixf[:, 3:4], fixf[:, 1:2], fixf[:, 2:3], ALU.add))
                ch.link(dve.tensor_copy(fixi[:, 1:2], fixf[:, 3:4]))
                dve.sem_inc(s_fx, 1)
                dve.wait_ge(s_fpe, 1)
                ch.link(dve.tensor_copy(tt[:, :], wk[0][0:BS, 0:P]))
                ch.link(dve.scalar_tensor_tensor(out=d0[:, :], in0=tt[:, :], scalar=ABSENT, in1=wk[0][0:BS, P:2 * P],
                                                 op0=ALU.is_equal, op1=ALU.mult))
                ch.link(dve.scalar_tensor_tensor(out=d1[:, :], in0=d0[:, :], scalar=0.5, in1=tt[:, :],
                                                 op0=ALU.is_lt, op1=ALU.mult))
                ch.link(dve.tensor_tensor_scan(cout[:, :], d0[:, :], d1[:, :], ABSENT, ALU.mult, ALU.add))
                ch.link(dve.memset(cinn[:, 0:1], ABSENT))
                ch.link(dve.tensor_copy(cinn[:, 1:P], cout[:, 0:P - 1]))
                dve.sem_inc(s_fx, 1)
                dve.wait_ge(s_fpe, 2)
                dve.wait_ge(s_fg, 16)
                ch.link(dve.scalar_tensor_tensor(out=fixw[:, :], in0=fixv[:, :], scalar=ABSENT, in1=wk[0][:, 0:BS],
                                                 op0=ALU.is_equal, op1=ALU.mult))
                ch.link(dve.scalar_tensor_tensor(out=fixv[:, :], in0=fixv[:, :], scalar=ABSENT, in1=fixv[:, :],
                                                 op0=ALU.not_equal, op1=ALU.mult))
                ch.link(dve.tensor_tensor(fixv[:, :], fixv[:, :], fixw[:, :], ALU.add))
                dve.sem_inc(s_fx, 1)
                dve.wait_ge(s_tok, 16 * NT)
                stats(dve, ch, h_all, cen, s_var, s_std)
                dve.wait_ge(s_av, 16 * AT)
                full = lambda x: x[:, :].unsqueeze(1).broadcast_to([P, AT, BS])
                own = a_val[:, :, :]
                ch.link(dve.tensor_tensor(own, own, full(ndiag), ALU.mult))
                ch.link(dve.tensor_tensor(own, own, full(diag), ALU.add))
                for seq in range(NT // AT):
                    x = dve.tensor_copy(a_vals[:, seq * AT:(seq + 1) * AT, :], own)
                ch.link(x)
                dve_n[0] = ch.base + ch.k

            @block.scalar
            def _(act):
                act.wait_ge(s_var, 1)
                act.activation(rstd[:, :], rstd[:, :], ACT.Sqrt).then_inc(s_std, 1)

            @block.tensor
            def _(pe):
                pe.wait_ge(s_fx, 1)
                pe.transpose(wk[0][0:BS, 0:P], last[:, 1, LC - 1, :], ident[:, :])
                pe.matmul(wk[0][0:BS, P:2 * P], thrub[:, :], ident[:, :], start=True, stop=True).then_inc(s_fpe, 1)
                pe.wait_ge(s_fx, 2)
                pe.transpose(wk[0][:, 0:BS], cinn[:, :], ident[0:BS, 0:BS]).then_inc(s_fpe, 1)

            @block.gpsimd
            def _(pool):
                def gather(dst, src, idx, signal):
                    pool.indirect_dma_start(out=dst, out_offset=None, in_=src,
                                            in_offset=bass.IndirectOffsetOnAxis(ap=idx, axis=0)).then_inc(signal, 16)
                pool.wait_ge(s_idx, 1)
                for t in range(NT):
                    gather(h_all[:, t], words_d[:, :], id_i[:, t:t + 1], s_tok)
                pool.wait_ge(s_fx, 1)
                for par in range(2):
                    pool.wait_ge(s_st[par], 16 + 16 * (LCN // 2))
                gather(fixv[:, :], ascan_d[:, :], fixi[:, 0:1], s_fg)
                pool.wait_ge(s_fx, 3)
                pool.indirect_dma_start(out=ascan_d[:, :], out_offset=bass.IndirectOffsetOnAxis(ap=fixi[:, 1:2], axis=0),
                                        in_=fixv[:, :], in_offset=None, bounds_check=PLACES - 1,
                                        oob_is_err=False).then_inc(s_fs, 16)
                pool.wait_ge(s_fs, 16)
                for t in range(AT):
                    gather(a_val[:, t], ascan_d[:, :], a_end[:, t:t + 1], s_av)
                pool.wait_ge(s_tok, 16 * NT)
        tmp.close()

        tmp = ExitStack()
        wq = sb("wq", [D + 1, D], where=tmp)
        wkk = sb("wkk", [D + 1, D], where=tmp)
        wv = sb("wv", [D + 1, D], where=tmp)
        wo = sb("wo", [D + 1, D], where=tmp)
        bavg = sb("bavg", [P, P], where=tmp)
        gate4 = sb("gate4", [P, H], where=tmp)
        gateb = sb("gateb", [P, H], where=tmp)
        gw16 = sb("gw16", [P, H * 4], where=tmp)
        gwt = sb("gwt", [4, H], where=tmp)
        gl = sb("gl", [7, H, P], where=tmp)
        gr = sb("gr", [7, H, P], where=tmp)
        neg = sb("neg", [3, H, P], where=tmp)
        gbr = sb("gbr", [1, H, P], where=tmp)
        xs = sb("xs", [P, D], where=tmp)
        xt = sb("xt", [D + 1, P], where=tmp)
        qt = sb("qt", [HD, H, P], where=tmp)
        kt = sb("kt", [HD, H, NB, KV], where=tmp)
        ks = sb("ks", [HD, H, NB], where=tmp)
        vs = sb("vs", [P, D], where=tmp)
        sc = sb("sc", [P, H, KV], where=tmp)
        ex = sb("ex", [P, H, KV], where=tmp)
        mk = sb("mk", [P, BS], where=tmp)
        mv = sb("mv", [P, BS], where=tmp)
        gg = sb("gg", [P, H, BS], where=tmp)
        gv = sb("gv", [P, H, BS], where=tmp)
        cb = sb("cb", [P, H, BS], where=tmp)
        cg = sb("cg", [P, H], where=tmp)
        ct = sb("ct", [P, H, BS], where=tmp)
        mx = sb("mx", [P, 4, H], where=tmp)
        xo = sb("xo", [P, D], where=tmp)
        xm = sb("xm", [P, D], where=tmp)
        ot = sb("ot", [D + 1, P], where=tmp)
        g_rec = sb("g_rec", [P, NT, 4], where=tmp)
        s_ghr = sem("s_ghr")
        s_aw, s_aw2, s_ac, s_gh, s_lr = sem("s_aw"), sem("s_aw2"), sem("s_ac"), sem("s_gh"), sem("s_lr")
        s_ape, s_aact, s_adve = sem("s_ape"), sem("s_aact"), sem("s_adve")
        NPE, NACT, NDVE = 6, 4, 7
        with nc.Block() as block:
            @block.sync
            def _(sp):
                sp.wait_ge(s_ac, 1)
                for n, w in enumerate((wq, wkk)):
                    sp.dma_start(w[0:D, :], qkv_wt[:, n * D:(n + 1) * D]).then_inc(s_aw, 16)
                    sp.dma_start(w[D:D + 1, :], qkv_b[:, n * D:(n + 1) * D]).then_inc(s_aw, 16)
                sp.dma_start(wv[0:D, :], qkv_wt[:, 2 * D:3 * D]).then_inc(s_aw, 16)
                sp.dma_start(wv[D:D + 1, :], qkv_b[:, 2 * D:3 * D]).then_inc(s_aw, 16)
                sp.dma_start(wo[0:D, :], proj_wt[:, :]).then_inc(s_aw, 16)
                sp.dma_start(wo[D:D + 1, :], proj_b[:, :]).then_inc(s_aw, 16)
                sp.dma_start(gw16[:, :], gate_w[0:1, :].broadcast_to([P, H * 4])).then_inc(s_aw, 16)
                sp.dma_start(gateb[:, :], gate_b[0:1, :].broadcast_to([P, H])).then_inc(s_aw, 16)
                sp.dma_start(gwt[:, :], gate_wt[:, :]).then_inc(s_aw, 16)
                sp.wait_ge(s_ac, 2)
                sp.dma_start(gr[4:7], neg[:, :, :]).then_inc(s_aw2, 16)
                sp.dma_start(gr[3:4], gbr[:, :, :]).then_inc(s_aw2, 16)
                sp.dma_start(gl[3:4], ones[0:1, :].unsqueeze(1).broadcast_to([1, H, P])).then_inc(s_aw2, 16)
                with sp.Fori(0, STEPS // 2) as i:
                    g_rank.sp_step(sp, i, 0)
                    g_rank.sp_step(sp, i, 1)
                    sp.wait_ge(s_ape, i * NPE + 3)
                    p3 = pos_d[0:3, bass.ds(i * P, P)].unsqueeze(1).broadcast_to([3, H, P])
                    sp.dma_start(gl[4:7], p3).then_inc(s_lr, 16)
                    sp.dma_start(gr[0:3], p3).then_inc(s_lr, 16)

            @block.tensor
            def _(pe):
                g_rank.pe_start(pe)
                pe.sem_inc(s_ape, 3)
                pe.wait_ge(s_aw, 16 * 11)
                pe.wait_ge(s_aw2, 48)
                with pe.Fori(0, STEPS // 2) as i:
                    def stage(slot):
                        dv, ac = (lambda n: pe.wait_ge(s_adve, i * NDVE + n)), (lambda n: pe.wait_ge(s_aact, i * NACT + n))
                        if slot == 1:
                            dv(1)
                            pe.sem_inc(s_tick, 1)
                            pe.transpose(wk[0][0:D, 0:P], xs[:, :], ident[:, :]).then_inc(s_ape, 1)
                        if slot == 3:
                            ac(1)
                            for h in range(H):
                                hd = slice(h * HD, (h + 1) * HD)
                                pe.matmul(wk[1][0:HD, bass.ts(h, P)], wq[:, hd], xt[:, :], start=True, stop=True)
                                pe.matmul(wk[2][0:HD, bass.ts(h, P)], wkk[:, hd], xt[:, :], start=True, stop=True)
                            pe.matmul(wk[0][:, P:P + D], xt[:, :], wv[:, :], start=True, stop=True).then_inc(s_ape, 1)
                        if slot == 6:
                            ac(2)
                            dv(2)
                            pe.wait_ge(s_lr, i * 32 + 32)
                            pe.sem_inc(s_tick, 1)
                            for b in range(NB):
                                q = slice(BS * b, BS * b + BS)
                                for h in range(H):
                                    pe.matmul(wk[2][q, h * KV:(h + 1) * KV], qt[:, h, q], kt[:, h, b, :], start=True, stop=True,
                                              tile_position=(0, BS * b))
                                    pe.matmul(wk[3][q, h * BS:(h + 1) * BS], gl[:, h, q], gr[:, h, q], start=True, stop=True,
                                              tile_position=(0, BS * b))
                            pe.matmul(wk[3][:, P:P + D], bavg[:, :], vs[:, :], start=True, stop=True).then_inc(s_ape, 1)
                        if slot == 10:
                            dv(4)
                            pe.sem_inc(s_tick, 1)
                            for b in range(NB):
                                q = slice(BS * b, BS * b + BS)
                                for h in range(H):
                                    x = pe.matmul(wk[0][q, P + h * HD:P + (h + 1) * HD], ct[q, h, :], vs[q, h * HD:(h + 1) * HD],
                                                  start=True, stop=True, tile_position=(BS * b, BS * b))
                            x.then_inc(s_ape, 1)
                        if slot == 12:
                            dv(5)
                            pe.sem_inc(s_tick, 1)
                            pe.transpose(wk[0][0:D, 2 * P:3 * P], xo[:, :], ident[:, :]).then_inc(s_ape, 1)
                        if slot == 14:
                            ac(4)
                            pe.matmul(wk[1][:, 2 * P:2 * P + D], ot[:, :], wo[:, :], start=True, stop=True).then_inc(s_ape, 1)
                    g_rank.pe_step(pe, i, 0, stage)
                    g_rank.pe_step(pe, i, 1, stage)

            @block.scalar
            def _(act):
                g_rank.act_start(act)
                with act.Fori(0, STEPS // 2) as i:
                    def stage(slot):
                        pe_ = lambda n: act.wait_ge(s_ape, i * NPE + 3 + n)
                        if slot == 2:
                            pe_(1)
                            act.activation(xt[0:D, :], wk[0][0:D, 0:P], ACT.Copy).then_inc(s_aact, 1)
                        if slot == 4:
                            pe_(2)
                            act.activation(qt[:, :, :].rearrange("p h q -> p (h q)"), wk[1][0:HD, :], ACT.Copy, scale=float(HD) ** -0.5)
                            act.activation(vs[:, :], wk[0][:, P:P + D], ACT.Copy).then_inc(s_aact, 1)
                        if slot == 8:
                            act.wait_ge(s_adve, i * NDVE + 3)
                            act.activation(ex[:, :, :], sc[:, :, :], ACT.Exp).then_inc(s_aact, 1)
                        if slot == 13:
                            pe_(5)
                            act.activation(ot[0:D, :], wk[0][0:D, 2 * P:3 * P], ACT.Copy).then_inc(s_aact, 1)
                    g_rank.act_step(act, i, 0, stage)
                    g_rank.act_step(act, i, 1, stage)

            @block.vector
            def _(dve):
                ch = Chain(dve, s_dve)
                ch.base = dve_n[0]
                dve.memset(bavg[:, :], 0.0)
                ch.link(dve.memset(xt[D:D + 1, :], 1.0))
                ch.link(dve.memset(ot[D:D + 1, :], 1.0))
                for b in range(NB):
                    ch.link(dve.memset(bavg[BS * b:BS * b + BS, BS * b:BS * b + BS], 1.0 / BS))
                dve.sem_inc(s_ac, 1)
                dve.wait_ge(s_const, 4)
                ch.link(dve.memset(g_rec[:, :, :], 0.0))
                gi = g_rec[:, :, :].bitcast(I32)
                ch.link(dve.tensor_copy(gi[:, :, 0], node_i[:, :]))
                ch.link(dve.tensor_copy(gi[:, :, 1], node_i[:, :]))
                dve.sem_inc(s_ghr, 1)
                dve.wait_ge(s_aw, 16 * 11)
                ch.link(dve.tensor_copy(gate4[:, :], gw16[:, :].rearrange("p (h k) -> p h k", k=4)[:, :, 3]))
                w3 = gwt[0:3, :].unsqueeze(2).broadcast_to([3, H, P])
                ch.link(dve.tensor_copy(gl[0:3], w3))
                ch.link(dve.tensor_scalar(neg[:, :, :], w3, -1.0, None, ALU.mult))
                ch.link(dve.tensor_copy(gbr[:, :, :], gateb[0:1, :].unsqueeze(2).broadcast_to([1, H, P])))
                dve.sem_inc(s_ac, 1)
                g_rank.dve_start(dve, ch)
                start = ch.base + ch.k
                with dve.Fori(0, STEPS // 2) as i:
                    ch.enter(i, 16, start)
                    tile = bass.ds(i, 1)
                    flat = lambda x: x.rearrange("p a d -> p (a d)")
                    row = lambda x: x.unsqueeze(1).broadcast_to([P, H, BS])
                    def stage(slot):
                        pe_ = lambda n: dve.wait_ge(s_ape, i * NPE + 3 + n)
                        if slot == 0:
                            ch.link(dve.tensor_tensor(xs[:, :], flat(h_all[:, tile, :]), mean[:, tile].broadcast_to([P, D]), ALU.subtract))
                            dve.tensor_tensor(xs[:, :], xs[:, :], rstd[:, tile].broadcast_to([P, D]), ALU.mult).then_inc(s_adve, 1)
                        if slot == 4:
                            pe_(2)
                            k4 = wk[2][0:HD, :].rearrange("p (h b c) -> p h b c", b=NB, c=BS)
                            dve.tensor_copy(kt[:, :, :, 0:BS], k4)
                            ch.link(dve.tensor_reduce(ks[:, :, :], k4, AX.X, ALU.add))
                            dve.tensor_scalar(kt[:, :, :, BS], ks[:, :, :], 1.0 / BS, None, ALU.mult).then_inc(s_adve, 1)
                        if slot == 7:
                            pe_(3)
                            dve.tensor_tensor(sc[:, :, 0:BS], wk[2][:, 0:H * KV].rearrange("p (h c) -> p h c", c=KV)[:, :, 0:BS],
                                              row(flat(a_vals[:, tile, :])), ALU.add)
                            ch.link(dve.tensor_scalar(sc[:, :, BS], wk[2][:, 0:H * KV].rearrange("p (h c) -> p h c", c=KV)[:, :, BS],
                                                      1.0, None, ALU.add))
                            ch.link(dve.tensor_reduce(mx[:, 0, :], sc[:, :, :], AX.X, ALU.max))
                            dve.tensor_tensor(sc[:, :, :], sc[:, :, :], mx[:, 0, :].unsqueeze(2).broadcast_to([P, H, KV]),
                                              ALU.subtract).then_inc(s_adve, 1)
                        if slot == 8:
                            ch.link(dve.tensor_scalar(mk[:, :], flat(a_vals[:, tile, :]), ABSENT / 2, None, ALU.is_gt))
                            ch.link(dve.tensor_tensor(mv[:, :], mk[:, :], flat(a_vals[:, tile, :]), ALU.mult))
                            ch.link(dve.tensor_tensor(gv[:, :, :], row(mv[:, :]), gate4[:, :].unsqueeze(2).broadcast_to([P, H, BS]), ALU.mult))
                            ch.link(dve.tensor_tensor(gg[:, :, :], wk[3][:, 0:P].rearrange("p (h c) -> p h c", c=BS), row(mk[:, :]), ALU.mult))
                            ch.link(dve.tensor_tensor(gg[:, :, :], gg[:, :, :], gv[:, :, :], ALU.add))
                        if slot == 9:
                            dve.wait_ge(s_aact, i * NACT + 3)
                            ch.link(dve.tensor_reduce(mx[:, 1, :], ex[:, :, :], AX.X, ALU.add))
                            ch.link(dve.reciprocal(mx[:, 2, :], mx[:, 1, :]))
                            ch.link(dve.tensor_tensor(sc[:, :, :], ex[:, :, :], mx[:, 2, :].unsqueeze(2).broadcast_to([P, H, KV]), ALU.mult))
                            ch.link(dve.tensor_tensor(cb[:, :, :], sc[:, :, 0:BS], gg[:, :, :], ALU.add))
                            dve.transpose(ct[:, :, :].rearrange("p h c -> p (h c)"), cb[:, :, :].rearrange("p h c -> p (h c)")).then_inc(s_adve, 1)
                            ch.link(dve.tensor_tensor(cg[:, :], sc[:, :, BS], gate4[:, :], ALU.add))
                            ch.link(dve.tensor_tensor(cg[:, :], cg[:, :], gateb[:, :], ALU.add))
                        if slot == 11:
                            pe_(4)
                            ch.link(dve.tensor_tensor(xm[:, :].rearrange("p (h d) -> p h d", d=HD),
                                                      wk[3][:, P:P + D].rearrange("p (h d) -> p h d", d=HD),
                                                      cg[:, :].unsqueeze(2).broadcast_to([P, H, HD]), ALU.mult))
                            dve.tensor_tensor(xo[:, :], wk[0][:, P:P + D], xm[:, :], ALU.add).then_inc(s_adve, 1)
                        if slot == 15:
                            pe_(6)
                            r = flat(h_all[:, tile, :])
                            dve.tensor_tensor(r, r, wk[1][:, 2 * P:2 * P + D], ALU.add).then_inc(s_adve, 2)
                    g_rank.dve_step(dve, i, 0, stage)
                    g_rank.dve_step(dve, i, 1, stage)
                ch.leave(STEPS // 2)
                dve_n[0] = ch.base

            @block.gpsimd
            def _(pool):
                pool.iota(node_i[:, :], [[P, P]], base=0, channel_multiplier=1).then_inc(s_const, 1)
                g_rank.pool_start(pool)
                pool.wait_ge(s_ghr, 1)
                for t in range(NT):
                    pool.indirect_dma_start(out=gsort_d[:, :], out_offset=bass.IndirectOffsetOnAxis(ap=g_head[:, t:t + 1], axis=0),
                                            in_=g_rec[:, t], in_offset=None, bounds_check=PLACES - 1,
                                            oob_is_err=False).then_inc(s_gh, 16)
                with pool.Fori(0, STEPS // 2) as i:
                    g_rank.pool_step(pool, i, 0)
                    g_rank.pool_step(pool, i, 1)
                g_rank.pool_end(pool)
                pool.wait_ge(s_gh, 16 * NT)
        tmp.close()
        both.close()

        G4 = 4 * P
        GN = N // G4
        x2t = sb("x2t", [P, N // 2])
        w1s = sb("w1s", [P, 2, NX, FF])
        w2s = sb("w2s", [FF, NX, D])
        b1s = sb("b1s", [FF, NX])
        b2s = sb("b2s", [P, NX * D])
        tmp = ExitStack()
        cen = sb("cen2", [P, NT, D], where=tmp)
        w24 = sb("w24", [P, 2, GW], where=tmp)
        att = sb("att", [P, 2, H * NX], where=tmp)
        attw = sb("attw", [P, 2, H * NX], where=tmp)
        x4 = sb("x4", [P, 2, 4, D], where=tmp)
        x4t = sb("x4t", [P, 2, 2 * P], where=tmp)
        nodes = sb("nodes", [P, NT, GW], where=tmp)
        zero4 = sb("zero4", [P, 4, GW], where=tmp)
        s_fw, s_w24, s_x4, s_tr, s_xc, s_nt, s_nc, s_var2, s_std2, s_nd = (sem(n) for n in (
            "s_fw", "s_w24", "s_x4", "s_tr", "s_xc", "s_nt", "s_nc", "s_var2", "s_std2", "s_nd"))
        with nc.Block() as block:
            @block.sync
            def _(sp):
                sp.wait_ge(s_w24, 1)
                for b in range(2):
                    sp.dma_start(w24[b * D:(b + 1) * D, b, 0:H * NX], w_gat[:, :]).then_inc(s_fw, 16)
                    sp.dma_start(w1s[b * D:(b + 1) * D, b], w1.rearrange("x d f -> d x f")).then_inc(s_fw, 16)
                sp.dma_start(att[:, 0], att_src[0:1, :].broadcast_to([P, H * NX])).then_inc(s_fw, 16)
                sp.dma_start(att[:, 1], att_dst[0:1, :].broadcast_to([P, H * NX])).then_inc(s_fw, 16)
                sp.dma_start(w2s[:, :, :], w2.rearrange("x f d -> f x d")).then_inc(s_fw, 16)
                sp.dma_start(b1s[:, :], b1t[:, :]).then_inc(s_fw, 16)
                sp.dma_start(b2s[:, :], b2[0:1, :].broadcast_to([P, NX * D])).then_inc(s_fw, 16)
                sp.wait_ge(s_nc, 2 + GN)
                sp.dma_start(node_d.rearrange("(t p) f -> p t f", p=P), nodes[:, :, :]).then_inc(s_nd, 16)
                sp.wait_ge(s_nd, 16)

            @block.vector
            def _(dve):
                ch = Chain(dve, s_dve)
                ch.base = dve_n[0]
                ch.link(dve.memset(w24[:, :, :], 0.0))
                ch.link(dve.memset(w1s[:, :, :, :], 0.0))
                dve.sem_inc(s_w24, 1)
                dve.wait_ge(s_fw, 16 * 9)
                for b in range(2):
                    w = w24[:, b:b + 1, 0:H * NX].broadcast_to([P, 2, H * NX])
                    ch.link(dve.tensor_tensor(attw[:, :, :], att[:, :, :], w, ALU.mult))
                    ch.link(dve.tensor_reduce(w24[:, b, H * NX:GW], attw[:, :, :].rearrange("d k (h x) -> d (k h) x", x=NX), AX.X, ALU.add))
                dve.sem_inc(s_w24, 1)
                ch.link(dve.memset(zero4[:, :, :], 0.0))
                stats(dve, ch, h_all, cen, s_var2, s_std2)
                start = ch.base + ch.k
                with dve.Fori(0, GN // 2) as i:
                    ch.enter(i, 2, start)
                    for par in range(2):
                        four = bass.ds(i * 8 + par * 4, 4)
                        wide = lambda x: x[:, four].unsqueeze(2).broadcast_to([P, 4, D])
                        dve.wait_ge(s_tr, i * 2 + (par + 1))
                        ch.link(dve.tensor_tensor(x4[:, par], h_all[:, four, :], wide(mean), ALU.subtract))
                        dve.tensor_tensor(x4[:, par], x4[:, par], wide(rstd), ALU.mult).then_inc(s_x4, 1)
                        dve.wait_ge(s_nt, i * 2 + (par + 1))
                        dve.tensor_tensor(nodes[:, four, :], wk[2 + par][:, 0:4 * GW].rearrange("p (t f) -> p t f", f=GW),
                                          zero4[:, :, :], ALU.add).then_inc(s_nc, 1)
                ch.leave(GN // 2)
                dve_n[0] = ch.base

            @block.tensor
            def _(pe):
                pe.sem_inc(s_tr, 2)
                pe.wait_ge(s_w24, 2)
                with pe.Fori(0, GN // 2) as i:
                    for par in range(2):
                        pe.wait_ge(s_x4, i * 2 + (par + 1))
                        pe.wait_ge(s_xc, i * 2 + (par + 1))
                        pe.sem_inc(s_tick, 1)
                        for t in range(2):
                            x = pe.transpose(wk[par][:, bass.ts(t, P)], x4[:, par, 2 * t:2 * t + 2].rearrange("p b d -> p (b d)"),
                                             ident[:, :])
                        x.then_inc(s_tr, 1)
                        pe.wait_ge(s_xc, i * 2 + (par + 3))
                        pe.wait_ge(s_nc, i * 2 + (par + 1))
                        pe.sem_inc(s_tick, 1)
                        for t in range(2):
                            x = pe.matmul(wk[2 + par][:, t * 2 * GW:(t + 1) * 2 * GW], x4t[:, par, bass.ts(t, P)],
                                          w24[:, :, :].rearrange("d b f -> d (b f)"), start=True, stop=True)
                        x.then_inc(s_nt, 1)

            @block.scalar
            def _(act):
                act.wait_ge(s_var2, 1)
                act.activation(rstd[:, :], rstd[:, :], ACT.Sqrt).then_inc(s_std2, 1)
                act.sem_inc(s_xc, 2)
                act.sem_inc(s_nc, 2)
                with act.Fori(0, GN // 2) as i:
                    for par in range(2):
                        act.wait_ge(s_tr, i * 2 + (par + 3))
                        act.activation(x2t[:, bass.ds(i * G4 + par * 2 * P, 2 * P)], wk[par][:, 0:2 * P], ACT.Copy)
                        act.wait_ge(s_nc, i * 2 + (par + 1))
                        act.activation(x4t[:, par], wk[par][:, 0:2 * P], ACT.Copy).then_inc(s_xc, 1)
        tmp.close()

        final = ExitStack()
        gsum = sb("gsum", [P, NT, GW])
        tmp = ExitStack()
        hid = scratch[:, 0:2 * G4].rearrange("p (b n) -> p b n", b=2)
        yb = scratch[:, 2 * G4:6 * G4].rearrange("p (b t x d) -> p b t x d", b=2, t=4, x=NX)
        gs = sb("gs", [P, RUN + 2 * GC, 4], where=tmp)
        rows = sb("rows", [P, 2, GC, GW], where=tmp)
        srci = sb("srci", [P, 2, GC], I32, tmp)
        keep = sb("keep", [P, 2, GC], where=tmp)
        head = sb("head", [P, 2, GC], where=tmp)
        drop = sb("drop", [P, 2, GC], where=tmp)
        adin = sb("adin", [P, GC, H], where=tmp)
        adst = sb("adst", [P, 2, GC, H], where=tmp)
        escore = sb("escore", [P, GC, H], where=tmp)
        mrun = sb("mrun", [P, 2, GC + 1, H], where=tmp)
        expin = sb("expin", [P, 2, 2, GC, H], where=tmp)
        expout = sb("expout", [P, 2, 2, GC, H], where=tmp)
        decay = sb("decay", [P, GC, H], where=tmp)
        msg = sb("msg", [P, GC, H * NX], where=tmp)
        scan = sb("scan", [P, 2, GC, GW], where=tmp)
        leadg = scratch[:, 6 * G4:6 * G4 + RUN]
        gfix = sb("gfix", [P, 6], where=tmp)
        gfixi = sb("gfixi", [P, 3], I32, tmp)
        first = sb("first", [P, GW], where=tmp)
        C = H + H * NX
        tm = sb("tm", [P, C], where=tmp)
        tv = sb("tv", [P, C], where=tmp)
        fb = sb("fb", [P, C], where=tmp)
        cx = rows[0:C, :, :, :].rearrange("p b t f -> p (b t f)")[:, 0:8 * P].rearrange("p (k n) -> p k n", k=8)
        fxr = sb("fxr", [P, GW], where=tmp)
        fx = sb("fx", [P, 7, C], where=tmp)
        s_gl, s_si, s_first, s_gfx, s_gpe, s_gfg, s_gfs, s_gsum = (sem(n) for n in (
            "s_gl", "s_si", "s_first", "s_gfx", "s_gpe", "s_gfg", "s_gfs", "s_gsum"))
        s_rows = [sem(f"s_rows{x}") for x in range(2)]
        s_ys = [sem(f"s_ys{x}") for x in range(2)]
        s_gst = [sem(f"s_gst{x}") for x in range(2)]
        s_m1, s_gel, s_m2, s_y, s_exi, s_exo, s_scan = (sem(n) for n in ("s_m1", "s_gel", "s_m2", "s_y", "s_exi", "s_exo", "s_scan"))
        s_seed, s_gsp = sem("s_seed"), sem("s_gsp")
        scan_g = gscan_d.rearrange("(p t) f -> p t f", p=P)
        experts_v = expert_d.rearrange("p (t b) x d -> p b t x d", b=2)
        with nc.Block() as block:
            @block.sync
            def _(sp):
                sp.dma_start(gs[:, 0:RUN, :], gsort_d.rearrange("(p t) f -> p t f", p=P)).then_inc(s_gl, 16)
                for par in range(2):
                    sp.dma_start(credit_d[par:par + 1, :], ones[0:1, :]).then_inc(s_gst[par], 16)
                    sp.dma_start(credit_d[par + 2:par + 3, :], ones[0:1, :]).then_inc(s_ys[par], 16)
                with sp.Fori(0, GN // 2) as i:
                    for par in range(2):
                        sp.wait_ge(s_y, i * (2 * NX) + (par * NX + NX + 2))
                        sp.dma_start(experts_v[:, par, bass.ds(i * 4, 4)], yb[:, par]).then_inc(s_ys[par], 16)
                with sp.Fori(0, GCN // 2) as i:
                    for par in range(2):
                        sp.wait_ge(s_scan, i * 2 + (par + 1))
                        sp.dma_start(scan_g[:, bass.ds(i * (2 * GC) + par * GC, GC), :], scan[:, par]).then_inc(s_gst[par], 16)
                for par in range(2):
                    sp.wait_ge(s_gst[par], 16 + 16 * (GCN // 2))
                    sp.wait_ge(s_ys[par], 16 + 16 * (GN // 2))
                sp.sem_inc(s_gsp, 1)

            @block.gpsimd
            def _(pool):
                def gather(dst, src, idx, signal):
                    pool.indirect_dma_start(out=dst, out_offset=None, in_=src,
                                            in_offset=bass.IndirectOffsetOnAxis(ap=idx, axis=0)).then_inc(signal, 16)
                pool.wait_ge(s_seed, 1)
                gather(first[:, :], node_d[:, :], gfixi[:, 2:3], s_first)
                with pool.Fori(0, GCN // 2) as i:
                    for par in range(2):
                        pool.wait_ge(s_si, i * 2 + (par + 1))
                        pool.sem_inc(s_tick, 1)
                        for t in range(GC):
                            gather(rows[:, par, t], node_d[:, :], srci[:, par, t:t + 1], s_rows[par])
                pool.wait_ge(s_gfx, 1)
                pool.wait_ge(s_gsp, 1)
                gather(fxr[:, :], gscan_d[:, :], gfixi[:, 0:1], s_gfg)
                pool.wait_ge(s_gfx, 3)
                pool.indirect_dma_start(out=gscan_d[:, :], out_offset=bass.IndirectOffsetOnAxis(ap=gfixi[:, 1:2], axis=0),
                                        in_=fxr[:, :], in_offset=None, bounds_check=PLACES - 1,
                                        oob_is_err=False).then_inc(s_gfs, 16)
                pool.wait_ge(s_gfs, 16)
                for t in range(NT):
                    gather(gsum[:, t], gscan_d[:, :], g_end[:, t:t + 1], s_gsum)
                pool.wait_ge(s_gsum, 16 * NT)

            @block.tensor
            def _(pe):
                with pe.Fori(0, GN // 2) as i:
                    for par in range(2):
                        for x in range(NX):
                            k = par * NX + x
                            pe.wait_ge(s_gel, i * (2 * NX) + (k + 1))
                            pe.matmul(wk[x % 2][:, :], w1s[:, par, x, :], x2t[:, bass.ds(i * G4, G4)],
                                      start=True, stop=True).then_inc(s_m1, 1)
                            pe.wait_ge(s_gel, i * (2 * NX) + (k + 3))
                            pe.wait_ge(s_y, i * (2 * NX) + (k + 1))
                            for t in range(4):
                                m = pe.matmul(wk[2 + x % 2][:, t * D:(t + 1) * D], hid[:, x % 2, bass.ts(t, P)], w2s[:, x, :],
                                              start=True, stop=True)
                            m.then_inc(s_m2, 1)
                pe.wait_ge(s_gfx, 1)
                pe.transpose(wk[0][0:C, 0:P], tm[:, :], ident[:, :])
                pe.transpose(wk[0][0:C, P:2 * P], tv[:, :], ident[:, :])
                pe.matmul(wk[0][0:C, 2 * P:3 * P], fb[:, :], ident[:, :], start=True, stop=True).then_inc(s_gpe, 1)
                pe.wait_ge(s_gfx, 2)
                pe.transpose(wk[0][:, 0:C], cx[:, 6], ident[0:C, 0:C])
                pe.transpose(wk[0][:, C:2 * C], cx[:, 7], ident[0:C, 0:C]).then_inc(s_gpe, 1)

            @block.scalar
            def _(act):
                act.sem_inc(s_gel, 2)
                with act.Fori(0, GN // 2) as i:
                    for par in range(2):
                        for x in range(NX):
                            k = par * NX + x
                            act.wait_ge(s_m1, i * (2 * NX) + (k + 1))
                            act.wait_ge(s_m2, i * (2 * NX) + (k + 1))
                            act.activation(hid[:, x % 2], wk[x % 2][:, :], ACT.Gelu, bias=b1s[:, x:x + 1]).then_inc(s_gel, 1)
                with act.Fori(0, GCN // 2) as i:
                    for par in range(2):
                        act.wait_ge(s_exi, i * 2 + (par + 1))
                        act.activation(expout[:, par], expin[:, par], ACT.Exp).then_inc(s_exo, 1)
                for n, (o, x) in enumerate(((cx[:, 5], cx[:, 4]), (fx[:, 5], fx[:, 4]))):
                    act.wait_ge(s_exi, GCN + 2 * n + 1)
                    act.activation(o, x, ACT.Exp).then_inc(s_exo, 1)
                    act.wait_ge(s_exi, GCN + 2 * n + 2)
                    act.activation(o, x, ACT.Exp).then_inc(s_exo, 1)

            @block.vector
            def _(dve):
                ch = Chain(dve, s_dve)
                ch.base = dve_n[0]
                dve.wait_ge(s_gl, 16)
                gsi = gs[:, :, :].bitcast(I32)
                kp = gs[:, 0:RUN, 2]
                ch.link(dve.tensor_copy(gfixi[:, 2:3], gsi[:, 0, 1:2]))
                dve.sem_inc(s_seed, 1)
                for par in range(2):
                    ch.link(dve.tensor_copy(srci[:, par], gsi[:, par * GC:(par + 1) * GC, 0]))
                    dve.sem_inc(s_si, 1)
                ch.link(dve.memset(gs[:, RUN:RUN + 2 * GC, :], 0.0))
                ch.link(dve.tensor_tensor_scan(leadg[:, :], kp, kp, 1.0, ALU.mult, ALU.mult))
                ch.link(dve.tensor_reduce(gfix[:, 0:1], leadg[:, :], AX.X, ALU.add))
                ch.link(dve.tensor_scalar(gfix[:, 1:2], gfix[:, 0:1], float(RUN), None, ALU.is_equal))
                ch.link(dve.tensor_copy(fb[:, :], gfix[:, 1:2].broadcast_to([P, C])))
                ch.link(dve.tensor_tensor(gfix[:, 2:3], gfix[:, 0:1], part_f[:, :], ALU.add))
                ch.link(dve.tensor_scalar(gfix[:, 3:4], gfix[:, 2:3], -1.0, 0.0, ALU.add, ALU.max))
                ch.link(dve.tensor_copy(gfixi[:, 0:1], gfix[:, 3:4]))
                ch.link(dve.tensor_scalar(gfix[:, 4:5], gfix[:, 0:1], 0.0, SKIP, ALU.is_equal, ALU.mult))
                ch.link(dve.tensor_tensor(gfix[:, 5:6], gfix[:, 3:4], gfix[:, 4:5], ALU.add))
                ch.link(dve.tensor_copy(gfixi[:, 1:2], gfix[:, 5:6]))
                dve.sem_inc(s_m2, 2)
                dve.sem_inc(s_y, 2)
                start = ch.base + ch.k
                with dve.Fori(0, GN // 2) as i:
                    for par in range(2):
                        dve.wait_ge(s_ys[par], i * 16 + 16)
                        for x in range(NX):
                            k = par * NX + x
                            dve.wait_ge(s_m2, i * (2 * NX) + (k + 3))
                            dve.tensor_tensor(yb[:, par, :, x, :], wk[2 + x % 2][:, 0:4 * D].rearrange("p (t d) -> p t d", d=D),
                                              b2s[:, x * D:(x + 1) * D].unsqueeze(1).broadcast_to([P, 4, D]), ALU.add).then_inc(s_y, 1)
                ch.link(dve.memset(scan[:, 1, GC - 1, :], 0.0))
                ch.link(dve.memset(mrun[:, 1, GC, :], ABSENT))
                dve.wait_ge(s_first, 16)
                ch.link(dve.tensor_copy(adst[:, 1, GC - 1, :], first[:, GW - H:GW]))
                start = ch.base + ch.k
                with dve.Fori(0, GCN // 2) as i:
                    ch.enter(i, 34, start)
                    for par in range(2):
                        wide = lambda x: x.unsqueeze(2).broadcast_to([P, GC, H])
                        dve.wait_ge(s_rows[par], i * (16 * GC) + 16 * GC)
                        r = rows[:, par]
                        here = bass.ds(i * (2 * GC) + par * GC, GC)
                        ch.link(dve.tensor_scalar(keep[:, par], gs[:, here, 2], 0.0, None, ALU.add))
                        ch.link(dve.tensor_scalar(head[:, par], keep[:, par], -1.0, 1.0, ALU.mult, ALU.add))
                        ch.link(dve.tensor_scalar(drop[:, par], head[:, par], ABSENT, None, ALU.mult))
                        ch.link(dve.tensor_tensor(adin[:, :, :], r[:, :, GW - H:GW], wide(head[:, par]), ALU.mult))
                        for h in range(H):
                            x = dve.tensor_tensor_scan(adst[:, par, :, h], keep[:, par], adin[:, :, h],
                                                       adst[:, 1 - par, GC - 1, h:h + 1], ALU.mult, ALU.add)
                        ch.link(x)
                        ch.link(dve.tensor_tensor(escore[:, :, :], r[:, :, H * NX:H * NX + H], adst[:, par], ALU.add))
                        ch.link(dve.scalar_tensor_tensor(out=escore[:, :, :], in0=escore[:, :, :], scalar=0.2,
                                                         in1=escore[:, :, :], op0=ALU.mult, op1=ALU.max))
                        ch.link(dve.tensor_copy(mrun[:, par, 0, :], mrun[:, 1 - par, GC, :]))
                        for h in range(H):
                            x = dve.tensor_tensor_scan(mrun[:, par, 1:GC + 1, h], drop[:, par], escore[:, :, h],
                                                       mrun[:, par, 0, h:h + 1], ALU.add, ALU.max)
                        ch.link(x)
                        ch.link(dve.tensor_tensor(expin[:, par, 0], mrun[:, par, 0:GC, :], mrun[:, par, 1:GC + 1, :], ALU.subtract))
                        ch.link(dve.tensor_scalar(expin[:, par, 0], expin[:, par, 0], 0.0, None, ALU.min))
                        ch.link(dve.tensor_tensor(expin[:, par, 1], escore[:, :, :], mrun[:, par, 1:GC + 1, :], ALU.subtract))
                        dve.sem_inc(s_exi, 1)
                        dve.wait_ge(s_exo, i * 2 + (par + 1))
                        ch.link(dve.tensor_tensor(decay[:, :, :], expout[:, par, 0], wide(keep[:, par]), ALU.mult))
                        ch.link(dve.tensor_tensor(msg[:, :, :].rearrange("p t (h x) -> p t h x", x=NX),
                                                  r[:, :, 0:H * NX].rearrange("p t (h x) -> p t h x", x=NX),
                                                  expout[:, par, 1].unsqueeze(3).broadcast_to([P, GC, H, NX]), ALU.mult))
                        dve.wait_ge(s_gst[par], i * 16 + 16)
                        ch.link(dve.tensor_copy(scan[:, par, :, H:2 * H], mrun[:, par, 1:GC + 1, :]))
                        for h in range(H):
                            dve.tensor_tensor_scan(scan[:, par, :, h], decay[:, :, h], expout[:, par, 1, :, h],
                                                   scan[:, 1 - par, GC - 1, h:h + 1], ALU.mult, ALU.add)
                            for x in range(NX):
                                c = h * NX + x
                                y = dve.tensor_tensor_scan(scan[:, par, :, 2 * H + c], decay[:, :, h], msg[:, :, c],
                                                           scan[:, 1 - par, GC - 1, 2 * H + c:2 * H + c + 1], ALU.mult, ALU.add)
                        ch.link(y)
                        dve.sem_inc(s_scan, 1)
                        ahead = bass.ds(i * (2 * GC) + (par + 2) * GC, GC)
                        ch.link(dve.tensor_copy(srci[:, par], gsi[:, ahead, 0]))
                        dve.sem_inc(s_si, 1)
                ch.leave(GCN // 2)
                t = scan[:, 1, GC - 1, :]
                m20 = lambda o, m: (dve.tensor_copy(o[:, 0:H], m),
                                    dve.tensor_copy(o[:, H:C].rearrange("p (h x) -> p h x", x=NX),
                                                    m.unsqueeze(2).broadcast_to([P, H, NX])))[1]
                v20 = lambda o, r: (dve.tensor_copy(o[:, 0:H], r[:, 0:H]), dve.tensor_copy(o[:, H:C], r[:, 2 * H:GW]))[1]
                ch.link(m20(tm, t[:, H:2 * H]))
                ch.link(v20(tv, t))
                dve.sem_inc(s_gfx, 1)
                dve.wait_ge(s_gpe, 1)
                TM, TV, F, CM, EX, EO, MP, CV = (cx[:, n] for n in range(8))
                ch.link(dve.tensor_copy(TM, wk[0][0:C, 0:P]))
                ch.link(dve.tensor_copy(TV, wk[0][0:C, P:2 * P]))
                ch.link(dve.tensor_scalar(F, wk[0][0:C, 2 * P:3 * P], -1.0, -ABSENT, ALU.add, ALU.mult))
                ch.link(dve.tensor_tensor_scan(CM, F, TM, ABSENT, ALU.add, ALU.max))
                ch.link(dve.tensor_copy(F, wk[0][0:C, 2 * P:3 * P]))
                ch.link(dve.memset(MP[:, 0:1], ABSENT))
                ch.link(dve.tensor_copy(MP[:, 1:P], CM[:, 0:P - 1]))
                ch.link(dve.tensor_tensor(EX, MP, CM, ALU.subtract))
                ch.link(dve.tensor_scalar(EX, EX, 0.0, None, ALU.min))
                dve.sem_inc(s_exi, 1)
                dve.wait_ge(s_exo, GCN + 1)
                ch.link(dve.tensor_tensor(F, F, EO, ALU.mult))
                ch.link(dve.tensor_tensor(EX, TM, CM, ALU.subtract))
                dve.sem_inc(s_exi, 1)
                dve.wait_ge(s_exo, GCN + 2)
                ch.link(dve.tensor_tensor(TV, TV, EO, ALU.mult))
                ch.link(dve.tensor_tensor_scan(CM, F, TV, 0.0, ALU.mult, ALU.add))
                ch.link(dve.memset(CV[:, 0:1], 0.0))
                ch.link(dve.tensor_copy(CV[:, 1:P], CM[:, 0:P - 1]))
                dve.sem_inc(s_gfx, 1)
                dve.wait_ge(s_gpe, 2)
                dve.wait_ge(s_gfg, 16)
                FM, FV, CMP, CVP, X, O, M = (fx[:, n] for n in range(7))
                ch.link(m20(FM, fxr[:, H:2 * H]))
                ch.link(v20(FV, fxr))
                ch.link(dve.tensor_copy(CMP, wk[0][:, 0:C]))
                ch.link(dve.tensor_copy(CVP, wk[0][:, C:2 * C]))
                ch.link(dve.tensor_tensor(M, FM, CMP, ALU.max))
                ch.link(dve.tensor_tensor(X, FM, M, ALU.subtract))
                dve.sem_inc(s_exi, 1)
                dve.wait_ge(s_exo, GCN + 3)
                ch.link(dve.tensor_tensor(FV, FV, O, ALU.mult))
                ch.link(dve.tensor_tensor(X, CMP, M, ALU.subtract))
                dve.sem_inc(s_exi, 1)
                dve.wait_ge(s_exo, GCN + 4)
                ch.link(dve.tensor_tensor(CVP, CVP, O, ALU.mult))
                ch.link(dve.tensor_tensor(FV, FV, CVP, ALU.add))
                dve.tensor_copy(fxr[:, 0:H], FV[:, 0:H])
                dve.tensor_copy(fxr[:, H:2 * H], M[:, 0:H])
                ch.link(dve.tensor_copy(fxr[:, 2 * H:GW], FV[:, H:C]))
                dve.sem_inc(s_gfx, 1)
                dve_n[0] = ch.base + ch.k
        tmp.close()

        agg = sb("agg", [P, NT, H * NX])
        sqr = sb("sqr", [P, NT, H * NX])
        consts = sb("consts", [P, 3, H * NX])
        st = sb("st", [P, 4, NT])
        score = sb("score", [P, NT, NX])
        rank = sb("rank", [P, NT, NX])
        cmp_ = sb("cmp", [P, NT])
        gate = sb("gate", [P, NT, NX])
        ye = sb("ye", [P, 2, 4, NX, D])
        yp = sb("yp", [P, 2, 4, NX, D])
        yo = sb("yo", [P, 2, 4, D])
        s_k, s_v3, s_s3, s_e3, s_x3, s_yf, s_of = (sem(n) for n in ("s_k", "s_v3", "s_s3", "s_e3", "s_x3", "s_yf", "s_of"))
        s_yl = [sem(f"s_yl{x}") for x in range(2)]
        s_o = [sem(f"s_o{x}") for x in range(2)]
        with nc.Block() as block:
            @block.sync
            def _(sp):
                for n, c in enumerate((b_gat, ln_g, ln_b)):
                    sp.dma_start(consts[:, n], c[0:1, :].broadcast_to([P, H * NX])).then_inc(s_k, 16)
                for par in range(2):
                    sp.dma_start(credit_d[par:par + 1, :], ones[0:1, :]).then_inc(s_o[par], 16)
                with sp.Fori(0, GN // 2) as i:
                    for par in range(2):
                        sp.wait_ge(s_yf, i * 2 + (par + 1))
                        sp.dma_start(ye[:, par], expert_d[:, bass.ds(i * 8 + par * 4, 4)]).then_inc(s_yl[par], 16)
                    for par in range(2):
                        sp.wait_ge(s_of, i * 2 + (par + 1))
                        sp.dma_start(out[:, bass.ds(i * 8 + par * 4, 4), :], yo[:, par]).then_inc(s_o[par], 16)
                for par in range(2):
                    sp.wait_ge(s_o[par], 16 + 16 * (GN // 2))

            @block.scalar
            def _(act):
                act.wait_ge(s_v3, 1)
                act.activation(st[:, 1], st[:, 1], ACT.Sqrt).then_inc(s_s3, 1)
                act.wait_ge(s_e3, 1)
                act.activation(gate[:, :, :], gate[:, :, :], ACT.Exp).then_inc(s_x3, 1)

            @block.vector
            def _(dve):
                ch = Chain(dve, s_dve)
                ch.base = dve_n[0]
                HX = H * NX
                per = lambda x: x.unsqueeze(2).broadcast_to([P, NT, HX])
                con = lambda n: consts[:, n].unsqueeze(1).broadcast_to([P, NT, HX])
                dve.wait_ge(s_k, 48)
                ch.link(dve.tensor_scalar(gsum[:, :, 0:H], gsum[:, :, 0:H], 1e-16, None, ALU.add))
                ch.link(dve.reciprocal(gsum[:, :, H:2 * H], gsum[:, :, 0:H]))
                ch.link(dve.tensor_tensor(agg[:, :, :].rearrange("p t (h x) -> p t h x", x=NX),
                                          gsum[:, :, 2 * H:GW].rearrange("p t (h x) -> p t h x", x=NX),
                                          gsum[:, :, H:2 * H].unsqueeze(3).broadcast_to([P, NT, H, NX]), ALU.mult))
                ch.link(dve.tensor_tensor(agg[:, :, :], agg[:, :, :], con(0), ALU.add))
                ch.link(dve.tensor_reduce(st[:, 0], agg[:, :, :], AX.X, ALU.add))
                ch.link(dve.tensor_scalar(st[:, 0], st[:, 0], 1.0 / HX, None, ALU.mult))
                ch.link(dve.tensor_tensor(agg[:, :, :], agg[:, :, :], per(st[:, 0]), ALU.subtract))
                ch.link(dve.tensor_tensor(sqr[:, :, :], agg[:, :, :], agg[:, :, :], ALU.mult))
                ch.link(dve.tensor_reduce(st[:, 1], sqr[:, :, :], AX.X, ALU.add))
                ch.link(dve.tensor_scalar(st[:, 1], st[:, 1], 1.0 / HX, EPS, ALU.mult, ALU.add))
                dve.sem_inc(s_v3, 1)
                dve.wait_ge(s_s3, 1)
                ch.link(dve.reciprocal(st[:, 2], st[:, 1]))
                ch.link(dve.tensor_tensor(agg[:, :, :], agg[:, :, :], per(st[:, 2]), ALU.mult))
                ch.link(dve.tensor_tensor(agg[:, :, :], agg[:, :, :], con(1), ALU.mult))
                ch.link(dve.tensor_tensor(agg[:, :, :], agg[:, :, :], con(2), ALU.add))
                ch.link(dve.tensor_reduce(score[:, :, :], agg[:, :, :].rearrange("p t (h x) -> p t x h", x=NX), AX.X, ALU.add))
                ch.link(dve.tensor_scalar(score[:, :, :], score[:, :, :], 1.0 / H, None, ALU.mult))
                ch.link(dve.memset(rank[:, :, :], 0.0))
                for a in range(NX):
                    for b in range(NX):
                        if a != b:
                            ch.link(dve.tensor_tensor(cmp_[:, :], score[:, :, b], score[:, :, a], ALU.is_ge if b < a else ALU.is_gt))
                            ch.link(dve.tensor_tensor(rank[:, :, a], rank[:, :, a], cmp_[:, :], ALU.add))
                ch.link(dve.tensor_reduce(st[:, 3], score[:, :, :], AX.X, ALU.max))
                ch.link(dve.tensor_tensor(gate[:, :, :], score[:, :, :], st[:, 3].unsqueeze(2).broadcast_to([P, NT, NX]), ALU.subtract))
                dve.sem_inc(s_e3, 1)
                dve.wait_ge(s_x3, 1)
                ch.link(dve.scalar_tensor_tensor(out=gate[:, :, :], in0=rank[:, :, :], scalar=1.5, in1=gate[:, :, :],
                                                 op0=ALU.is_lt, op1=ALU.mult))
                ch.link(dve.tensor_reduce(st[:, 0], gate[:, :, :], AX.X, ALU.add))
                ch.link(dve.reciprocal(st[:, 1], st[:, 0]))
                ch.link(dve.tensor_tensor(gate[:, :, :], gate[:, :, :], st[:, 1].unsqueeze(2).broadcast_to([P, NT, NX]), ALU.mult))
                dve.sem_inc(s_yf, 2)
                start = ch.base + ch.k
                with dve.Fori(0, GN // 2) as i:
                    ch.enter(i, 4, start)
                    for par in range(2):
                        four = bass.ds(i * 8 + par * 4, 4)
                        dve.wait_ge(s_yl[par], i * 16 + 16)
                        ch.link(dve.tensor_tensor(yp[:, par], ye[:, par], gate[:, four, :].unsqueeze(3).broadcast_to([P, 4, NX, D]), ALU.mult))
                        dve.sem_inc(s_yf, 1)
                        dve.wait_ge(s_o[par], i * 16 + 16)
                        ch.link(dve.tensor_reduce(yo[:, par], yp[:, par].rearrange("p t x d -> p t d x"), AX.X, ALU.add))
                        dve.tensor_tensor(yo[:, par], yo[:, par], h_all[:, four, :], ALU.add).then_inc(s_of, 1)
                ch.leave(GN // 2)


_OUTS = [((16, 1024, 64), "float32")]


def kernel(**inputs):
    import numpy as np
    import concourse.bacc as bacc
    from concourse.bass_utils import run_bass_kernel_spmd

    a = {k: np.asarray(v) for k, v in inputs.items()}
    tiles = lambda x: x.reshape(2, ET, P)
    arrays = {
        "ids": a["x"].reshape(NT, P).T,
        "emb": a["L0_tok_base_embeddings"],
        "rule_mats": a["L0_tok_rule_transform"].reshape(RULES, D * D),
        "rules": a["L0_tok_token_rules"],
        "a_edge_t": tiles(a["L0_attn_edge_index"]).transpose(0, 2, 1),
        "a_edge_n": tiles(a["L0_attn_edge_index"]),
        "a_val_t": a["L0_attn_edge_values"].reshape(ET, P).T,
        "pos_t": a["L0_attn_positions"].T,
        "qkv_wt": a["L0_attn_qkv_w"].T,
        "qkv_b": a["L0_attn_qkv_b"].reshape(1, 3 * D),
        "proj_wt": a["L0_attn_proj_w"].T,
        "proj_b": a["L0_attn_proj_b"].reshape(1, D),
        "gate_w": a["L0_attn_gate_w"].reshape(1, H * 4),
        "gate_wt": a["L0_attn_gate_w"].T,
        "gate_b": a["L0_attn_gate_b"].reshape(1, H),
        "w_gat": a["L0_ffn_W_gat"],
        "att_src": a["L0_ffn_att_src"].reshape(1, H * NX),
        "att_dst": a["L0_ffn_att_dst"].reshape(1, H * NX),
        "b_gat": a["L0_ffn_b_gat"].reshape(1, H * NX),
        "ln_g": a["L0_ffn_ln_gamma"].reshape(1, H * NX),
        "ln_b": a["L0_ffn_ln_beta"].reshape(1, H * NX),
        "w1": a["L0_ffn_W1"],
        "b1t": a["L0_ffn_b1"].T,
        "w2": a["L0_ffn_W2"],
        "b2": a["L0_ffn_b2"].reshape(1, NX * D),
        "g_edge_t": tiles(a["L0_ffn_edge_index"]).transpose(0, 2, 1),
        "g_edge_n": tiles(a["L0_ffn_edge_index"]),
    }
    nc = bacc.Bacc("TRN2", target_bir_lowering=False, num_devices=1)
    given, args = {}, []
    for name, x in arrays.items():
        given[f"in_{name}"] = np.ascontiguousarray(x)
        args.append(nc.dram_tensor(f"in_{name}", x.shape, mybir.dt.from_np(x.dtype), kind="ExternalInput").ap())
    shape, dtype = _OUTS[0]
    args.append(nc.dram_tensor("out_0", (P, NT, D), mybir.dt.from_np(np.dtype(dtype)), kind="ExternalOutput").ap())
    tower(nc, *args)
    r = run_bass_kernel_spmd(nc, [given], core_ids=[0])
    return r.results[0]["out_0"].transpose(1, 0, 2).reshape(shape)
```

```python
from contextlib import ExitStack

import concourse.bass as bass
from concourse import mybir

FP32 = mybir.dt.float32
BF16 = mybir.dt.bfloat16
I32 = mybir.dt.int32
ALU = mybir.AluOpType
ACT = mybir.ActivationFunctionType
AX = mybir.AxisListType

P = 128
N = 16384
AN = 1024
AT = AN // P
AL = AN // P
NT = N // P
E = 262144
ET = E // P
J = 8
STEPS = ET // J
PLACES = E + N
RUN = PLACES // P
D = 64
H = 4
HD = 16
BS = 32
NB = P // BS
KV = BS + 1
VOCAB = 8000
VP = 125
VT = VOCAB // VP
RULES = 100
NX = 4
FF = 128
GW = 24
EPS = 1e-5
ABSENT = -1e30
SKIP = float(1 << 20)
MAGIC = 8388608.0
LC = 136
LCN = RUN // LC
GC = 68
GCN = RUN // GC


class Chain:

    def __init__(self, eng, sem):
        self.eng, self.sem, self.base, self.k = eng, sem, 0, 0

    def link(self, ins):
        ins.then_inc(self.sem, 1)
        self.k += 1
        self.eng.wait_ge(self.sem, self.base + self.k)

    def put(self, ins):
        ins.then_inc(self.sem, 1)
        self.k += 1

    def settle(self):
        self.eng.wait_ge(self.sem, self.base + self.k)

    def enter(self, i, per, start):
        self.base, self.k, self.per, self.start = i * per + start, 0, per, start

    def leave(self, times):
        assert self.k == self.per, (self.k, self.per)
        self.base, self.k = self.start + self.per * times, 0


def tower(nc, ids, emb, rule_mats, rules, a_edge_t, a_edge_n, a_val_t, pos_t, qkv_wt, qkv_b, proj_wt,
          proj_b, gate_w, gate_wt, gate_b, w_gat, att_src, att_dst, b_gat, ln_g, ln_b, w1, b1t, w2, b2,
          g_edge_t, g_edge_n, out):
    ctx = ExitStack()
    with ctx:
        def sem(name):
            return ctx.enter_context(nc.semaphore(name))

        def sb(name, shape, dt=FP32, where=None):
            return (where or ctx).enter_context(nc.sbuf_tensor(name, shape, dt))

        def dram(name, shape, dt=FP32):
            return nc.dram_tensor(name, shape, dt, kind="Internal").ap()

        words_d = dram("words_d", [VOCAB, D])
        akey_d = dram("akey_d", [ET, 2, P], BF16)
        gkey_d = dram("gkey_d", [ET, 2, P], BF16)
        aend_d = dram("aend_d", [AN], I32)
        asort_d = dram("asort_d", [PLACES, 4])
        gsort_d = dram("gsort_d", [PLACES, 4])
        ascan_d = dram("ascan_d", [PLACES, BS])
        gscan_d = dram("gscan_d", [PLACES, GW])
        node_d = dram("node_d", [N, GW])
        expert_d = dram("expert_d", [P, NT, NX, D])
        credit_d = dram("credit_d", [4, P])

        bank = [ctx.enter_context(nc.psum_tensor(f"bank{n}", [P, 512], FP32)) for n in range(7)]
        cnt_ps = bank[2]
        wk = bank[3:7]
        oht_ps = ctx.enter_context(nc.psum_tensor("oht_ps", [P, 1024], BF16))

        ident = sb("ident", [P, P])
        identb = sb("identb", [P, P], BF16)
        earlier = sb("earlier", [P, P])
        prefix = sb("prefix", [P, P])
        zerob = sb("zerob", [P, P], BF16)
        iota = sb("iota", [P, P])
        iotai = sb("iotai", [P, P], I32)
        node_i = sb("node_i", [P, P], I32)
        node_f = sb("node_f", [P, P])
        sel = sb("sel", [2 * J, J, P], BF16)
        part_f = sb("part_f", [P, 1])
        part_i = sb("part_i", [P, 1], I32)
        ones = sb("ones", [P, P])
        g_head, g_end = (sb(n, [P, NT], I32) for n in ("g_head", "g_end"))
        a_head, a_ends = (sb(n, [P, AL], I32) for n in ("a_head", "a_ends"))
        a_end = sb("a_end", [P, AT], I32)
        a_first, g_first = sb("a_first", [P, AL]), sb("g_first", [P, P])
        node_a = sb("node_a", [P, AL])
        scratch = sb("scratch", [P, 6 * J * P])
        oh_hi = scratch[:, 0:J * P].bitcast(BF16).rearrange("p (b e j) -> p b e j", b=2, j=J)
        oh_lo = scratch[:, J * P:2 * J * P].bitcast(BF16).rearrange("p (b e j) -> p b e j", b=2, j=J)
        oht = scratch[:, 2 * J * P:4 * J * P].rearrange("p (b j e) -> p b j e", b=2, j=J)
        junk = scratch[:, 4 * J * P:6 * J * P].bitcast(BF16).rearrange("p (b k j e) -> p b k j e", b=2, k=2, j=J)
        table = sb("table", [P, 2, P])
        krow = sb("krow", [2 * J, 2, P], BF16)
        keys = sb("keys", [P, 2, 3 * J])
        before = sb("before", [P, 2, 3, J])
        place = sb("place", [P, 2, J], I32)
        record = sb("record", [P, 2, J, 4])

        s_const, s_load, s_dve, s_act, s_pool = (sem(n) for n in ("s_const", "s_load", "s_dve", "s_act", "s_pool"))
        s_tick = sem("s_tick")
        dve_n = [0]

        both = ctx.enter_context(ExitStack())
        a_val = sb("a_val", [P, AT, BS])
        h_slots = sb("h_slots", [P, NT + 1, D])
        h_all = h_slots[:, 1:NT + 1, :]
        mean = sb("mean", [P, NT])
        rstd = sb("rstd", [P, NT])
        g_keys = sb("g_keys", [P, (STEPS + 1) * 3 * J], where=both)
        g_parts = sb("g_parts", [P, (STEPS + 1) * 2 * J], BF16, both)
        iotab = sb("iotab", [P, P, J], BF16, both)
        g_pay = sb("g_pay", [P, ET * 2], I32, both)

        early = ExitStack()
        a_keys = sb("a_keys", [P, (STEPS + 1) * 3 * J], where=early)
        a_parts = sb("a_parts", [P, (STEPS + 1) * 2 * J], BF16, early)
        a_pay = sb("a_pay", [P, ET * 2], where=early)
        prep = ExitStack()
        er = sb("er", [P, ET], I32, prep)
        ec = sb("ec", [P, ET], I32, prep)
        spare = h_all[:, :, :].rearrange("p t d -> p (t d)")
        t0, t1 = (spare[:, x * ET:(x + 1) * ET].bitcast(I32) for x in range(2))
        f0, f1 = (spare[:, x * ET:(x + 1) * ET] for x in range(2, 4))
        parts = [scratch[:, x * ET:(x + 1) * ET].bitcast(BF16).rearrange("p (k e) -> p k e", k=2) for x in range(2)]
        sel_f = scratch[0:2 * J, 2 * ET:2 * ET + J * P].rearrange("p (j e) -> p j e", j=J)
        s_er, s_free, s_keys, s_kd = sem("s_er"), sem("s_free"), sem("s_keys"), sem("s_kd")
        s_ms = sem("s_ms")
        with nc.Block() as block:
            @block.sync
            def _(sp):
                natural = lambda a: a.rearrange("(b q) p -> q b p", q=P)
                blocks = lambda a: a[:, :].rearrange("q (b p) -> q b p", p=P)
                sp.dma_start(er[:, :], a_edge_t[0]).then_inc(s_er, 16)
                sp.dma_start(ec[:, :], a_edge_t[1]).then_inc(s_er, 16)
                sp.dma_start(f0[:, :], a_val_t[:, :]).then_inc(s_er, 16)
                sp.wait_ge(s_free, 1)
                sp.dma_start(blocks(er), natural(a_edge_n[0])).then_inc(s_er, 16)
                sp.dma_start(blocks(ec), natural(a_edge_n[1])).then_inc(s_er, 16)
                sp.wait_ge(s_keys, 1)
                for k in range(2):
                    sp.dma_start(natural(akey_d[:, k]), blocks(parts[0][:, k])).then_inc(s_kd, 16)
                sp.dma_start(er[:, :], g_edge_t[1]).then_inc(s_er, 16)
                sp.dma_start(ec[:, :], g_edge_t[0]).then_inc(s_er, 16)
                sp.wait_ge(s_free, 2)
                sp.dma_start(blocks(er), natural(g_edge_n[1])).then_inc(s_er, 16)
                sp.wait_ge(s_keys, 2)
                for k in range(2):
                    sp.dma_start(natural(gkey_d[:, k]), blocks(parts[1][:, k])).then_inc(s_kd, 16)
                sp.wait_ge(s_kd, 64)

            @block.vector
            def _(dve):
                ch = Chain(dve, s_dve)

                def attention_keys(key, valid):
                    ch.link(dve.tensor_scalar(t0[:, :], er[:, :], 5, None, ALU.logical_shift_right))
                    ch.link(dve.tensor_scalar(t1[:, :], ec[:, :], 5, None, ALU.logical_shift_right))
                    ch.link(dve.tensor_tensor(valid[:, :], t0[:, :], t1[:, :], ALU.is_equal))
                    ch.link(dve.tensor_scalar(t1[:, :], er[:, :], float(AN), None, ALU.is_lt))
                    ch.link(dve.tensor_tensor(valid[:, :], valid[:, :], t1[:, :], ALU.mult))
                    ch.link(dve.scalar_tensor_tensor(out=key, in0=er[:, :], scalar=-float(N), in1=valid[:, :],
                                                     op0=ALU.add, op1=ALU.mult))
                    ch.link(dve.tensor_scalar(key, key, float(N), None, ALU.add))

                def two_parts(key, part):
                    ch.link(dve.tensor_copy(t0[:, :], key[:, :]))
                    ch.link(dve.tensor_scalar(t1[:, :], t0[:, :], P - 1, None, ALU.bitwise_and))
                    ch.link(dve.tensor_copy(part[:, 1], t1[:, :]))
                    ch.link(dve.tensor_tensor(part[:, 0], key[:, :], t1[:, :], ALU.subtract))

                def split(keys_, parts_, key, lower):
                    f = keys_[:, :].rearrange("p (s f j) -> p f s j", f=3, j=J)
                    g = parts_[:, :].rearrange("p (s f j) -> p f s j", f=2, j=J)
                    tiles = lambda x: x[:, :].rearrange("p (s j) -> p s j", j=J)
                    ch.link(dve.tensor_copy(f[:, 0, 0:STEPS], tiles(key)))
                    ch.link(dve.tensor_copy(t0[:, :], key[:, :]))
                    ch.link(dve.tensor_scalar(t1[:, :], t0[:, :], lower - 1, None, ALU.bitwise_and))
                    ch.link(dve.tensor_copy(f[:, 1, 0:STEPS], tiles(t1)))
                    ch.link(dve.tensor_copy(g[:, 1, 0:STEPS], f[:, 1, 0:STEPS]))
                    ch.link(dve.tensor_scalar(t1[:, :], t0[:, :], lower.bit_length() - 1, None, ALU.logical_shift_right))
                    ch.link(dve.tensor_copy(g[:, 0, 0:STEPS], tiles(t1)))
                    ch.link(dve.memset(f[:, :, STEPS, :], 0.0))
                    ch.link(dve.memset(g[:, :, STEPS, :], 0.0))
                    return f[:, 2, 0:STEPS], tiles

                dve.wait_ge(s_er, 48)
                ch.link(dve.tensor_copy(a_pay[:, :].rearrange("p (t f) -> p t f", f=2)[:, :, 1], f0[:, :]))
                attention_keys(f0[:, :], f1)
                inv, tiles = split(a_keys, a_parts, f0, AL)
                ch.link(dve.tensor_scalar(inv, tiles(f1), -SKIP, SKIP, ALU.mult, ALU.add))
                ch.link(dve.tensor_scalar(t0[:, :], ec[:, :], BS - 1, None, ALU.bitwise_and))
                ins = dve.tensor_copy(a_pay[:, :].rearrange("p (t f) -> p t f", f=2)[:, :, 0], t0[:, :])
                ch.link(ins)
                dve.sem_inc(s_free, 1)
                dve.wait_ge(s_er, 80)
                attention_keys(f0[:, :], f1)
                two_parts(f0, parts[0])
                dve.sem_inc(s_keys, 1)
                dve.wait_ge(s_er, 112)
                ch.link(dve.tensor_copy(f1[:, :], er[:, :]))
                inv, _ = split(g_keys, g_parts, f1, P)
                ch.link(dve.memset(inv, 0.0))
                pay = g_pay[:, :].rearrange("p (t f) -> p t f", f=2)
                ch.link(dve.tensor_copy(pay[:, :, 0], ec[:, :]))
                ch.link(dve.tensor_copy(pay[:, :, 1], er[:, :]))
                dve.sem_inc(s_free, 1)
                dve.wait_ge(s_er, 128)
                ch.link(dve.tensor_copy(f1[:, :], er[:, :]))
                two_parts(f1, parts[1])
                dve.sem_inc(s_keys, 1)
                dve.wait_ge(s_const, 3)
                ch.link(dve.tensor_copy(iota[:, :], iotai[:, :]))
                ch.link(dve.tensor_copy(iotab[:, :, :], iota[:, :].unsqueeze(2).broadcast_to([P, P, J])))
                ch.link(dve.tensor_copy(node_f[:, :], node_i[:, :]))
                ch.link(dve.tensor_scalar(node_a[:, :], node_f[:, 0:1].broadcast_to([P, AL]), AL / P, None, ALU.mult))
                ch.link(dve.tensor_tensor(node_a[:, :], node_a[:, :], iota[:, 0:AL], ALU.add))
                ch.link(dve.tensor_copy(part_f[:, :], part_i[:, :]))
                dve.wait_ge(s_ms, 11)
                ch.link(dve.tensor_copy(identb[:, :], ident[:, :]))
                ch.link(dve.tensor_copy(sel[:, :, :], sel_f[:, :, :]))
                dve_n[0] = ch.k

            @block.gpsimd
            def _(pool):
                pool.iota(iotai[:, :], [[1, P]], base=0, channel_multiplier=0).then_inc(s_const, 1)
                pool.iota(node_i[:, :], [[1, P]], base=0, channel_multiplier=P).then_inc(s_const, 1)
                pool.iota(part_i[:, :], [[0, 1]], base=0, channel_multiplier=RUN).then_inc(s_const, 1)
                pool.memset(zerob[:, :], 0.0).then_inc(s_ms, 1)
                pool.memset(ident[:, :], 0.0).then_inc(s_ms, 1)
                pool.memset(ones[:, :], 1.0).then_inc(s_ms, 1)
                pool.memset(earlier[:, :], 1.0).then_inc(s_ms, 1)
                pool.memset(prefix[:, :], 1.0).then_inc(s_ms, 1)
                pool.memset(sel_f[:, :, :], 0.0).then_inc(s_ms, 1)
                pool.wait_ge(s_ms, 6)
                pool.affine_select(out=ident[:, :], in_=ident[:, :], compare_op=ALU.not_equal, fill=1.0, base=0,
                                   pattern=[[-1, P]], channel_multiplier=1).then_inc(s_ms, 1)
                pool.affine_select(out=earlier[:, :], in_=earlier[:, :], compare_op=ALU.is_gt, fill=0.0, base=0,
                                   pattern=[[-1, P]], channel_multiplier=1).then_inc(s_ms, 1)
                pool.affine_select(out=prefix[:, :], in_=prefix[:, :], compare_op=ALU.is_gt, fill=0.0, base=0,
                                   pattern=[[1, P]], channel_multiplier=-1).then_inc(s_ms, 1)
                pool.affine_select(out=sel_f[:, :, :], in_=sel_f[:, :, :], compare_op=ALU.not_equal, fill=1.0, base=0,
                                   pattern=[[-2, J], [0, P]], channel_multiplier=1).then_inc(s_ms, 1)
                pool.wait_ge(s_ms, 10)
                pool.affine_select(out=sel_f[:, :, :], in_=sel_f[:, :, :], compare_op=ALU.not_equal, fill=1.0, base=-1,
                                   pattern=[[-2, J], [0, P]], channel_multiplier=1).then_inc(s_ms, 1)
        prep.close()

        def one_hot(dve, buf, parts_, step, field, tiles, width):
            f = parts_[:, :].rearrange("p (s f) -> p s f", f=2 * J)
            n = tiles.stop - tiles.start
            k = f[:, bass.ds(step, 1), field * J + tiles.start:field * J + tiles.stop]
            return dve.tensor_tensor(buf[:, 0:width, tiles], k.broadcast_to([P, width, n]), iotab[:, 0:width, tiles], ALU.is_equal)

        class Count:

            def __init__(self, tag, parts_, lower, ps, hi, lo):
                self.parts, self.lower, self.ps, self.hi, self.lo, self.tag = parts_, lower, ps, hi, lo, tag
                self.oh, self.used, self.sum, self.st = (sem(f"{tag}_{n}") for n in ("oh", "used", "sum", "st"))

            def dve_part(self, dve, step, par, n):
                if n == 0:
                    dve.wait_ge(self.used, step + 1)
                tiles = slice(n % 2 * J // 2, (n % 2 + 1) * J // 2)
                buf, field, width = ((self.hi, 0, P), (self.lo, 1, self.lower))[n // 2]
                one_hot(dve, buf[:, par], self.parts, step, field, tiles, width).then_inc(self.oh, 1)

            def pe_start(self, pe, free):
                pe.sem_inc(self.used, free)
                pe.matmul(self.ps[:, 0:self.lower], zerob[:, :], zerob[:, 0:self.lower], start=True, stop=False, skip_group_check=True)

            def pe_step(self, pe, step, par):
                pe.wait_ge(self.oh, step * 4 + 4)
                for j in range(J):
                    m = pe.matmul(self.ps[:, 0:self.lower], self.hi[:, par, :, j], self.lo[:, par, 0:self.lower, j],
                                  start=False, stop=False, skip_group_check=True)
                m.then_inc(self.used, 1)

            def pe_end(self, pe):
                pe.matmul(self.ps[:, 0:self.lower], zerob[:, :], zerob[:, 0:self.lower], start=False, stop=True,
                          skip_group_check=True).then_inc(self.sum, 1)

            def starts(self, first, node, head, end, counted=None):
                tmp = ExitStack()
                n = self.lower
                cnt, inc, hp, ep = (sb(f"{self.tag}_{x}", [P, n], where=tmp) for x in ("c", "i", "h", "e"))
                with nc.Block() as block:
                    @block.vector
                    def _(dve):
                        ch = Chain(dve, s_dve)
                        ch.base = dve_n[0]
                        if counted:
                            counted.dve(dve)
                        dve.wait_ge(self.sum, 1)
                        ch.link(dve.tensor_copy(cnt[:, :], self.ps[:, 0:n]))
                        ch.link(dve.tensor_tensor_scan(inc[:, :], ones[:, 0:n], cnt[:, :], 0.0, ALU.mult, ALU.add))
                        dve.sem_inc(self.st, 1)
                        dve.wait_ge(self.sum, 2)
                        ch.link(dve.tensor_tensor(hp[:, :], inc[:, :], cnt[:, :], ALU.subtract))
                        ch.link(dve.tensor_scalar(hp[:, :], hp[:, :], self.ps[:, P:P + 1], None, ALU.add))
                        ch.link(dve.tensor_tensor(hp[:, :], hp[:, :], node[:, :], ALU.add))
                        ch.link(dve.tensor_tensor(ep[:, :], hp[:, :], cnt[:, :], ALU.add))
                        ch.link(dve.tensor_scalar(first[:, :], hp[:, :], 1.0, None, ALU.add))
                        if n == P:
                            dve.sem_inc(self.st, 1)
                            dve.wait_ge(self.sum, 3)
                            ch.link(dve.tensor_copy(head[:, :], wk[0][:, 0:P]))
                            ch.link(dve.tensor_copy(end[:, :], wk[0][:, P:2 * P]))
                        else:
                            ch.link(dve.tensor_copy(head[:, :], hp[:, :]))
                            ch.link(dve.tensor_copy(end[:, :], ep[:, :]))
                        dve_n[0] += ch.k

                    @block.tensor
                    def _(pe):
                        if counted:
                            counted.pe(pe)
                        self.pe_end(pe)
                        pe.wait_ge(self.st, 1)
                        pe.matmul(self.ps[:, P:P + 1], prefix[:, :], inc[:, n - 1:n], start=True, stop=True).then_inc(self.sum, 1)
                        if n == P:
                            pe.wait_ge(self.st, 2)
                            pe.transpose(wk[0][:, 0:P], hp[:, :], ident[:, :])
                            pe.transpose(wk[0][:, P:2 * P], ep[:, :], ident[:, :]).then_inc(self.sum, 1)
                tmp.close()

        a_count = Count("ac", a_parts, AL, cnt_ps, oh_hi, oh_lo)

        class CountAlone:

            @staticmethod
            def dve(dve):
                with dve.Fori(0, STEPS // 2) as i:
                    for par in range(2):
                        for n in range(4):
                            a_count.dve_part(dve, i * 2 + par, par, n)

            @staticmethod
            def pe(pe):
                a_count.pe_start(pe, 2)
                with pe.Fori(0, STEPS // 2) as i:
                    for par in range(2):
                        a_count.pe_step(pe, i * 2 + par, par)

        a_count.starts(a_first, node_a, a_head, a_ends, CountAlone)

        class Rank:

            def __init__(self, tag, keys_, parts_, pay, first, key_d, sort_d, rec_f, lower, banks):
                self.banks = banks
                self.parts, self.lower, self.oh_hi, self.oh_lo = parts_, lower, sem(tag + "_ohh"), sem(tag + "_ohl")
                self.keys, self.pay, self.first, self.key_d, self.sort_d, self.rec_f = keys_, pay, first, key_d, sort_d, rec_f
                self.ready, self.used = sem(tag + "_ready"), sem(tag + "_used2")
                self.oht_ps, self.oht_sb, self.upd = sem(tag + "_oht_ps"), sem(tag + "_oht_sb"), sem(tag + "_upd")
                self.tab, self.place, self.sum = sem(tag + "_tab"), sem(tag + "_place"), sem(tag + "_sum")
                self.done = [sem(f"{tag}_done{x}") for x in range(2)]
                self.kr = [sem(f"{tag}_kr{x}") for x in range(2)]

            def sp_step(self, sp, i, par, last=False):
                sp.wait_ge(self.upd, i * (2 * J) + (par * J + J + 1))
                rows = self.key_d.rearrange("t k p -> (t k) p")
                sp.dma_start(krow[:, par], rows[bass.ds(i * (4 * J) + par * 2 * J, 2 * J), :]).then_inc(self.kr[par], 16)

            def pe_start(self, pe):
                pe.matmul(cnt_ps[:, 0:self.lower], ident[:, :], self.first[:, :], start=True, stop=False,
                          skip_group_check=True).then_inc(self.upd, 2 * J + 1)
                self.pe_transposes(pe, 0, 0)

            def pe_transposes(self, pe, par, step):
                pe.wait_ge(self.oh_hi, step * 2 + 2)
                pe.wait_ge(self.oht_sb, step * 2 + 2)
                for j in range(J):
                    m = pe.transpose(oht_ps[:, j * P:(j + 1) * P], oh_hi[:, par, :, j], identb[:, :])
                m.then_inc(self.oht_ps, 1)

            def pe_step(self, pe, i, par, between=None):
                pe.wait_ge(self.kr[par], i * 16 + 16)
                for j in range(J):
                    if j == 0:
                        pe.wait_ge(self.oh_lo, i * 4 + (par * 2 + 2))
                    self.pe_tile(pe, i, par, j)
                    if j == J // 2 + 1:
                        self.pe_transposes(pe, 1 - par, i * 2 + (par + 1))
                    if between:
                        between(par * J + j)

            def act_step(self, act, i, par, between=None):
                for j in range(J):
                    self.act_tile(act, i, par, j)
                    if j >= J - 2:
                        self.act_ahead(act, i, par, j - (J - 2))
                    if between:
                        between(par * J + j)

            def dve_step(self, dve, i, par, between=None):
                self.dve_ahead(dve, i, par)
                for j in range(J):
                    self.dve_tile(dve, i, par, j)
                    if j in (0, 3, 6):
                        self.dve_part(dve, i * 2 + (par + 1), 1 - par, 1 + j // 3)
                    if between:
                        between(par * J + j)
                self.dve_places(dve, i, par)

            def pe_tile(self, pe, i, par, j):
                ps = self.banks[j // 2 % len(self.banks)]
                if j % 2 == 0:
                    pe.wait_ge(self.used, i * J + (par * J // 2 + j // 2 + 1))
                pe.matmul(ps[:, bass.ts(j % 2, P)], sel[:, j], krow[:, par], start=True, stop=True)
                pe.wait_ge(self.tab, i * (2 * J) + (par * J + j + 1))
                pe.matmul(cnt_ps[:, 0:self.lower], oh_hi[:, par, :, j], oh_lo[:, par, 0:self.lower, j], start=False, stop=False,
                          skip_group_check=True).then_inc(self.upd, 1)
                x = pe.matmul(ps[:, (2 + j % 2) * P:(2 + j % 2) * P + self.lower], oht[:, par, j], table[:, j % 2, 0:self.lower],
                              start=True, stop=True)
                if j % 2:
                    x.then_inc(self.ready, 1)

            def act_start(self, act):
                act.sem_inc(self.oht_sb, 2)
                act.wait_ge(self.oht_ps, 1)
                for half in range(2):
                    self.oht_copy(act, 0, half)

            def oht_copy(self, act, par, half):
                tiles = slice(half * J // 2, (half + 1) * J // 2)
                act.activation(oht[:, par, tiles].rearrange("p j e -> p (j e)"), oht_ps[:, tiles.start * P:tiles.stop * P],
                               ACT.Copy).then_inc(self.oht_sb, 1)

            def act_ahead(self, act, i, par, half):
                act.wait_ge(self.oht_ps, i * 2 + (par + 2))
                self.oht_copy(act, 1 - par, half)

            def act_tile(self, act, i, par, j):
                act.wait_ge(self.upd, i * (2 * J) + (par * J + j + 2 * J + 1))
                if j % J == 0:
                    act.wait_ge(self.oht_sb, i * 4 + (par * 2 + 4))
                act.activation(table[:, j % 2, 0:self.lower], cnt_ps[:, 0:self.lower], ACT.Copy).then_inc(self.tab, 1)

            def row(self, par, j):
                if self.lower == P:
                    return junk[:, par, 1, j]
                return oh_lo[:, par, self.lower * (j + 1):self.lower * (j + 2), 0]

            def dve_start(self, dve, ch):
                ch.link(dve.memset(record[:, :, :, :], 1.0))
                dve.sem_inc(self.used, len(self.banks))
                dve.wait_ge(self.upd, 1)
                for n in range(4):
                    self.dve_part(dve, 0, 0, n)

            def dve_part(self, dve, step, par, n):
                tiles = slice(n % 2 * J // 2, (n % 2 + 1) * J // 2)
                buf, field, width, signal = ((oh_hi, 0, P, self.oh_hi), (oh_lo, 1, self.lower, self.oh_lo))[n // 2]
                one_hot(dve, buf[:, par], self.parts, step, field, tiles, width).then_inc(signal, 1)

            def dve_ahead(self, dve, i, par):
                dve.wait_ge(self.upd, i * (2 * J) + (par * J + 2 * J + 1))
                self.dve_part(dve, i * 2 + (par + 1), 1 - par, 0)
                f = self.keys[:, :].rearrange("p (s f) -> p s f", f=3 * J)
                dve.tensor_scalar(keys[:, par], f[:, bass.ds(i * 2 + par, 1), :].rearrange("p a f -> p (a f)"), 0.0, None,
                                  ALU.add).then_inc(self.sum, 1)
                dve.wait_ge(self.sum, i * 6 + (par * 3 + 1))

            def dve_tile(self, dve, i, par, j):
                ps = self.banks[j // 2 % len(self.banks)]
                if j % 2 == 0:
                    dve.wait_ge(self.ready, i * J + (par * J // 2 + j // 2 + 1))
                dve.scalar_tensor_tensor(out=junk[:, par, 0, j], in0=ps[:, bass.ts(j % 2, P)], scalar=keys[:, par, j:j + 1],
                                         in1=earlier[:, :], op0=ALU.is_equal, op1=ALU.mult,
                                         accum_out=before[:, par, 0, j:j + 1])
                x = dve.scalar_tensor_tensor(out=self.row(par, j), in0=iota[:, 0:self.lower],
                                             scalar=keys[:, par, J + j:J + j + 1],
                                             in1=ps[:, (2 + j % 2) * P:(2 + j % 2) * P + self.lower], op0=ALU.is_equal, op1=ALU.mult,
                                             accum_out=before[:, par, 1, j:j + 1])
                if j % 2:
                    x.then_inc(self.used, 1)

            def dve_places(self, dve, i, par):
                dve.wait_ge(self.used, i * J + ((par + 1) * J // 2 + len(self.banks)))
                dve.wait_ge(self.done[par], i * (16 * J) + 16)
                dve.tensor_tensor(before[:, par, 2], before[:, par, 0], before[:, par, 1], ALU.add).then_inc(self.sum, 1)
                pv = self.pay[:, :].rearrange("p (s j f) -> p s (j f)", j=J, f=2)
                src = pv[:, bass.ds(i * 2 + par, 1), :].rearrange("p a (j f) -> p (a j) f", f=2)
                rec = record[:, par] if self.rec_f == FP32 else record[:, par].bitcast(I32)
                off = 1 if self.rec_f == FP32 else 0
                dve.tensor_copy(rec[:, :, off:off + 2], src).then_inc(self.sum, 1)
                dve.wait_ge(self.sum, i * 6 + (par * 3 + 3))
                dve.tensor_tensor(place[:, par], before[:, par, 2], keys[:, par, 2 * J:3 * J], ALU.add).then_inc(self.place, 1)

            def pool_start(self, pool):
                for par in range(2):
                    pool.dma_start(credit_d[par:par + 1, :], ones[0:1, :]).then_inc(self.done[par], 16)

            def pool_step(self, pool, i, par):
                pool.wait_ge(self.place, i * 2 + (par + 1))
                pool.sem_inc(s_tick, 1)
                for j in range(J):
                    pool.indirect_dma_start(
                        out=self.sort_d[:, :], out_offset=bass.IndirectOffsetOnAxis(ap=place[:, par, j:j + 1], axis=0),
                        in_=record[:, par, j], in_offset=None, bounds_check=PLACES - 1,
                        oob_is_err=False).then_inc(self.done[par], 16)

            def pool_end(self, pool):
                for par in range(2):
                    pool.wait_ge(self.done[par], 16 + 16 * J * (STEPS // 2))

        a_rank = Rank("ar", a_keys, a_parts, a_pay, a_first, akey_d, asort_d, FP32, AL,
                      [bank[0], bank[1], wk[2], wk[3]])
        g_rank = Rank("gr", g_keys, g_parts, g_pay, g_first, gkey_d, gsort_d, I32, P, bank[0:2])

        tmp = ExitStack()
        mats = sb("mats", [VP, D * D], where=tmp)
        prod = sb("prod", [VP, D * D], where=tmp)
        wsum = sb("wsum", [VP, D], where=tmp)
        words = h_all[0:VP, 0:VT, :]
        rule_i = sb("rule_i", [VP, VT], I32, tmp)
        rule_c = sb("rule_c", [VP, VT], I32, tmp)
        ridx = sb("ridx", [VP, 2], I32, tmp)
        FILL = RUN // 34
        a_rec = sb("a_rec", [P, FILL, 4], where=tmp)
        g_hi = sb("g_hi", [P, 2, P, J], BF16, tmp)
        g_lo = scratch[:, 4 * J * P:6 * J * P].bitcast(BF16).rearrange("p (b k e j) -> p b k e j", b=2, k=2, j=J)[:, :, 1]
        g_count = Count("gc", g_parts, P, wk[1], g_hi, g_lo)
        s_w, s_ridx, s_mat, s_wd, s_hd, s_arec, s_wst, s_fill = (sem(n) for n in ("s_w", "s_ridx", "s_mat", "s_wd", "s_hd", "s_arec", "s_wst", "s_fill"))
        s_ends = sem("s_ends")
        with nc.Block() as block:
            @block.sync
            def _(sp):
                sp.dma_start(words[:, :, :], emb.rearrange("(p t) d -> p t d", t=VT)).then_inc(s_w, 16)
                sp.dma_start(rule_i[:, :], rules.rearrange("(p t) -> p t", t=VT)).then_inc(s_w, 16)
                sp.wait_ge(s_arec, 1)
                sp.dma_start(asort_d.rearrange("(p r t) f -> p r (t f)", p=P, t=FILL),
                             a_rec[:, :, :].rearrange("p t f -> p (t f)").unsqueeze(1).broadcast_to([P, RUN // FILL, FILL * 4])
                             ).then_inc(s_fill, 16)
                sp.dma_start(aend_d.rearrange("(p c) -> p c", c=AL), a_ends[:, :]).then_inc(s_ends, 16)
                sp.wait_ge(s_ends, 16)
                for t in range(AT):
                    sp.dma_start(a_end[:, t:t + 1], aend_d[t * P:(t + 1) * P].unsqueeze(1)).then_inc(s_ends, 16)
                with sp.Fori(0, STEPS // 2) as i:
                    for par in range(2):
                        a_rank.sp_step(sp, i, par)
                sp.wait_ge(s_wd, VT)
                sp.dma_start(words_d.rearrange("(p t) d -> p t d", t=VT), words[:, :, :]).then_inc(s_wst, 16)
                sp.wait_ge(s_wst, 16)
                sp.wait_ge(s_ends, 16 + 16 * AT)

            @block.tensor
            def _(pe):
                a_rank.pe_start(pe)
                g_count.pe_start(pe, 1)
                with pe.Fori(0, STEPS // 2) as i:
                    for par in range(2):
                        def between(slot):
                            if slot % J == 3:
                                g_count.pe_step(pe, i * 2 + par, 1 - par)
                        a_rank.pe_step(pe, i, par, between)
                g_count.pe_step(pe, STEPS, (STEPS - 1) % 2)

            @block.scalar
            def _(act):
                a_rank.act_start(act)
                with act.Fori(0, STEPS // 2) as i:
                    for par in range(2):
                        a_rank.act_step(act, i, par)

            @block.vector
            def _(dve):
                ch = Chain(dve, s_dve)
                ch.base = dve_n[0]
                dve.memset(g_hi[:, 1], 0.0)
                ch.link(dve.memset(g_lo[:, 1], 0.0))
                dve.sem_inc(g_count.oh, 4)
                ch.link(dve.memset(a_rec[:, :, :], 0.0))
                ch.link(dve.memset(a_rec[:, :, 2], ABSENT))
                dve.sem_inc(s_arec, 1)
                dve.wait_ge(s_w, 32)
                ch.link(dve.tensor_scalar(rule_c[:, :], rule_i[:, :], 0.0, float(RULES - 1), ALU.max, ALU.min))
                a_rank.dve_start(dve, ch)
                start = ch.base + ch.k
                with dve.Fori(0, VT) as i:
                    ch.enter(i, 4, start)
                    ch.link(dve.tensor_copy(ridx[:, 0:1], rule_c[:, bass.ds(i, 1)]))
                    dve.sem_inc(s_ridx, 1)
                    w = words[:, bass.ds(i, 1), :].rearrange("p a d -> p (a d)")
                    grid = lambda x: x[:, :].rearrange("p (d e) -> p d e", e=D)
                    for step in range(4):
                        def between(slot):
                            slot %= J
                            if slot in (1, 2, 4, 5):
                                g_count.dve_part(dve, i * 4 + step, step % 2, {1: 0, 2: 1, 4: 2, 5: 3}[slot])
                            n = {(2, 0): 0, (2, 3): 1, (2, 6): 2, (2, 7): 3}.get((step, slot))
                            if n is not None:
                                if n == 0:
                                    dve.wait_ge(s_mat, i * 16 + 16)
                                q = slice(n * D // 4, (n + 1) * D // 4)
                                x = dve.tensor_tensor(grid(prod)[:, q], grid(mats)[:, q], w[:, q].unsqueeze(2).broadcast_to([VP, D // 4, D]),
                                                      ALU.mult)
                                if n == 3:
                                    ch.link(x)
                            n = {(3, 0): 0, (3, 3): 1, (3, 6): 2, (3, 7): 3}.get((step, slot))
                            if n is not None:
                                q = slice(n * D // 4, (n + 1) * D // 4)
                                x = dve.tensor_reduce(wsum[:, q], grid(prod)[:, :, q].rearrange("p d e -> p e d"), AX.X, ALU.add)
                                if n == 3:
                                    ch.link(x)
                        a_rank.dve_step(dve, i * 2 + step // 2, step % 2, between)
                    ch.link(dve.tensor_scalar(w, wsum[:, :], 0.0, None, ALU.add))
                    dve.sem_inc(s_wd, 1)
                ch.leave(VT)
                dve_n[0] = ch.base

            @block.gpsimd
            def _(pool):
                a_rank.pool_start(pool)
                pool.wait_ge(s_fill, 16)
                for t in range(AL):
                    pool.indirect_dma_start(out=asort_d[:, :], out_offset=bass.IndirectOffsetOnAxis(ap=a_head[:, t:t + 1], axis=0),
                                            in_=a_rec[:, 0], in_offset=None, bounds_check=PLACES - 1,
                                            oob_is_err=False).then_inc(s_hd, 16)
                with pool.Fori(0, VT) as i:
                    pool.wait_ge(s_ridx, i + 1)
                    pool.sem_inc(s_tick, 1)
                    pool.indirect_dma_start(out=mats[:, :], out_offset=None, in_=rule_mats[:, :],
                                            in_offset=bass.IndirectOffsetOnAxis(ap=ridx[:, 0:1], axis=0)).then_inc(s_mat, 16)
                    for step in range(4):
                        a_rank.pool_step(pool, i * 2 + step // 2, step % 2)
                a_rank.pool_end(pool)
                pool.wait_ge(s_hd, 16 * AL)
        tmp.close()
        g_count.starts(g_first, node_f, g_head, g_end)
        early.close()

        a_vals = sb("a_vals", [P, NT, BS], where=both)
        tmp = ExitStack()
        work = sb("work", [P, 2 * LC * BS], where=tmp)
        cen = work[:, 0:NT * D].rearrange("p (t d) -> p t d", d=D)
        rec = scratch[:, 0:8 * LC].rearrange("p (b t f) -> p b t f", b=2, f=4)
        lead = scratch[:, 8 * LC:10 * LC].rearrange("p (b t) -> p b t", b=2)
        keepm = work[:, 0:LC * BS].rearrange("p (t c) -> p t c", c=BS)
        evin = work[:, LC * BS:2 * LC * BS].rearrange("p (t c) -> p t c", c=BS)
        last = sb("last", [P, 2, LC, BS], where=tmp)
        nlead = sb("nlead", [P, 1], where=tmp)
        part = sb("part", [P, 1], where=tmp)
        thru = sb("thru", [P, 1], where=tmp)
        thrub = sb("thrub", [P, BS], where=tmp)
        tt = scratch[0:BS, 10 * LC + 0 * P:10 * LC + 1 * P]
        d0 = scratch[0:BS, 10 * LC + 1 * P:10 * LC + 2 * P]
        d1 = scratch[0:BS, 10 * LC + 2 * P:10 * LC + 3 * P]
        cout = scratch[0:BS, 10 * LC + 3 * P:10 * LC + 4 * P]
        cinn = scratch[0:BS, 10 * LC + 4 * P:10 * LC + 5 * P]
        fixf = sb("fixf", [P, 4], where=tmp)
        fixi = sb("fixi", [P, 2], I32, tmp)
        fixv = sb("fixv", [P, BS], where=tmp)
        fixw = sb("fixw", [P, BS], where=tmp)
        g_rec = sb("g_rec", [P, NT, 4], where=tmp)
        diag = sb("diag", [P, BS], where=tmp)
        ndiag = sb("ndiag", [P, BS], where=tmp)
        id_raw = scratch[:, 10 * LC + 5 * P:10 * LC + 6 * P].bitcast(I32)
        id_f = scratch[:, 10 * LC + 6 * P:10 * LC + 7 * P]
        id_n = scratch[:, 10 * LC + 7 * P:10 * LC + 8 * P]
        id_i = scratch[:, 10 * LC + 8 * P:10 * LC + 9 * P].bitcast(I32)

        def stats(dve, ch, x, cen, s_var, s_std):
            n = 1.0 / D
            ch.link(dve.tensor_reduce(mean[:, :], x[:, :, :], AX.X, ALU.add))
            ch.link(dve.tensor_scalar(mean[:, :], mean[:, :], n, None, ALU.mult))
            ch.link(dve.tensor_tensor(cen[:, :, :], x[:, :, :], mean[:, :].unsqueeze(2).broadcast_to([P, NT, D]), ALU.subtract))
            ch.link(dve.tensor_tensor(cen[:, :, :], cen[:, :, :], cen[:, :, :], ALU.mult))
            ch.link(dve.tensor_reduce(rstd[:, :], cen[:, :, :], AX.X, ALU.add))
            ch.link(dve.tensor_scalar(rstd[:, :], rstd[:, :], n, EPS, ALU.mult, ALU.add))
            dve.sem_inc(s_var, 1)
            dve.wait_ge(s_std, 1)
            ch.link(dve.reciprocal(rstd[:, :], rstd[:, :]))

        s_pos, s_ghr, s_gh = sem("s_pos"), sem("s_ghr"), sem("s_gh")
        pos_d = dram("pos_d", [3, N])
        s_id, s_idx, s_tok, s_var, s_std = sem("s_id"), sem("s_idx"), sem("s_tok"), sem("s_var"), sem("s_std")
        s_rec = [sem(f"s_rec{x}") for x in range(2)]
        s_st = [sem(f"s_st{x}") for x in range(2)]
        s_rfree, s_last = sem("s_rfree"), sem("s_last")
        s_fx, s_fpe, s_fg, s_fs, s_av = sem("s_fx"), sem("s_fpe"), sem("s_fg"), sem("s_fs"), sem("s_av")
        scan_v = ascan_d.rearrange("(p t) f -> p t f", p=P)
        with nc.Block() as block:
            @block.sync
            def _(sp):
                sp.dma_start(id_raw[:, :], ids[:, :]).then_inc(s_id, 16)
                sp.dma_start(pos_d.rearrange("k (s n) -> k s n", n=AN),
                             pos_t[:, 0:AN].unsqueeze(1).broadcast_to([3, NT // AT, AN])).then_inc(s_pos, 16)
                sp.wait_ge(s_pos, 16)
                for par in range(2):
                    sp.dma_start(credit_d[par:par + 1, :], ones[0:1, :]).then_inc(s_st[par], 16)
                v = asort_d.rearrange("(p t) f -> p t f", p=P)
                with sp.Fori(0, LCN // 2) as i:
                    for par in range(2):
                        sp.wait_ge(s_rfree, i * 2 + (par + 1))
                        sp.dma_start(rec[:, par], v[:, bass.ds(i * (2 * LC) + par * LC, LC), :]).then_inc(s_rec[par], 16)
                    for par in range(2):
                        sp.wait_ge(s_last, i * 2 + (par + 1))
                        sp.dma_start(scan_v[:, bass.ds(i * (2 * LC) + par * LC, LC), :], last[:, par]).then_inc(s_st[par], 16)
                for par in range(2):
                    sp.wait_ge(s_st[par], 16 + 16 * (LCN // 2))

            @block.vector
            def _(dve):
                ch = Chain(dve, s_dve)
                ch.base = dve_n[0]
                dve.wait_ge(s_id, 16)
                ch.link(dve.tensor_copy(id_f[:, :], id_raw[:, :]))
                ch.link(dve.tensor_scalar(id_n[:, :], id_f[:, :], 0.0, float(VOCAB), ALU.is_lt, ALU.mult))
                ch.link(dve.tensor_tensor(id_f[:, :], id_f[:, :], id_n[:, :], ALU.add))
                ch.link(dve.tensor_scalar(id_i[:, :], id_f[:, :], 0.0, float(VOCAB - 1), ALU.max, ALU.min))
                dve.sem_inc(s_idx, 1)
                dve.wait_ge(s_const, 4)
                ch.link(dve.memset(g_rec[:, :, :], 0.0))
                gi = g_rec[:, :, :].bitcast(I32)
                ch.link(dve.tensor_copy(gi[:, :, 0], node_i[:, :]))
                ch.link(dve.tensor_copy(gi[:, :, 1], node_i[:, :]))
                dve.sem_inc(s_ghr, 1)
                ch.link(dve.memset(last[:, 1, LC - 1, :], ABSENT))
                ch.link(dve.memset(lead[:, 1, LC - 1:LC], 1.0))
                ch.link(dve.memset(nlead[:, :], 0.0))
                ch.link(dve.tensor_reduce(diag[:, :], ident[:, :].rearrange("p (b c) -> p c b", c=BS), AX.X, ALU.add))
                ch.link(dve.tensor_scalar(ndiag[:, :], diag[:, :], -1.0, 1.0, ALU.mult, ALU.add))
                dve.sem_inc(s_rfree, 2)
                start = ch.base + ch.k
                with dve.Fori(0, LCN // 2) as i:
                    ch.enter(i, 12, start)
                    for par in range(2):
                        dve.wait_ge(s_rec[par], i * 16 + 16)
                        dve.wait_ge(s_st[par], i * 16 + 16)
                        keep, col, val = (rec[:, par, :, f] for f in range(3))
                        for c in range(BS):
                            x = dve.scalar_tensor_tensor(out=keepm[:, :, c], in0=keep, scalar=float(c), in1=col,
                                                         op0=ALU.mult, op1=ALU.not_equal)
                        ch.link(x)
                        ch.link(dve.scalar_tensor_tensor(out=evin[:, :, :], in0=keepm[:, :, :], scalar=0.5,
                                                         in1=val.unsqueeze(2).broadcast_to([P, LC, BS]),
                                                         op0=ALU.is_lt, op1=ALU.mult))
                        for c in range(BS):
                            x = dve.tensor_tensor_scan(last[:, par, :, c], keepm[:, :, c], evin[:, :, c],
                                                       last[:, 1 - par, LC - 1, c:c + 1], ALU.mult, ALU.add)
                        ch.link(x)
                        dve.sem_inc(s_last, 1)
                        ch.link(dve.tensor_tensor_scan(lead[:, par], keep, keep, lead[:, 1 - par, LC - 1:LC], ALU.mult, ALU.mult))
                        ch.link(dve.tensor_reduce(part[:, :], lead[:, par], AX.X, ALU.add))
                        dve.sem_inc(s_rfree, 1)
                        ch.link(dve.tensor_tensor(nlead[:, :], nlead[:, :], part[:, :], ALU.add))
                ch.leave(LCN // 2)
                ch.link(dve.tensor_scalar(thru[:, :], nlead[:, :], float(RUN), None, ALU.is_equal))
                ch.link(dve.tensor_copy(thrub[:, :], thru[:, :].broadcast_to([P, BS])))
                ch.link(dve.tensor_tensor(fixf[:, 0:1], nlead[:, :], part_f[:, :], ALU.add))
                ch.link(dve.tensor_scalar(fixf[:, 0:1], fixf[:, 0:1], -1.0, None, ALU.add))
                ch.link(dve.tensor_scalar(fixf[:, 1:2], fixf[:, 0:1], 0.0, None, ALU.max))
                ch.link(dve.tensor_copy(fixi[:, 0:1], fixf[:, 1:2]))
                ch.link(dve.tensor_scalar(fixf[:, 2:3], nlead[:, :], 0.0, SKIP, ALU.is_equal, ALU.mult))
                ch.link(dve.tensor_tensor(fixf[:, 3:4], fixf[:, 1:2], fixf[:, 2:3], ALU.add))
                ch.link(dve.tensor_copy(fixi[:, 1:2], fixf[:, 3:4]))
                dve.sem_inc(s_fx, 1)
                dve.wait_ge(s_fpe, 1)
                ch.link(dve.tensor_copy(tt[:, :], wk[0][0:BS, 0:P]))
                ch.link(dve.scalar_tensor_tensor(out=d0[:, :], in0=tt[:, :], scalar=ABSENT, in1=wk[0][0:BS, P:2 * P],
                                                 op0=ALU.is_equal, op1=ALU.mult))
                ch.link(dve.scalar_tensor_tensor(out=d1[:, :], in0=d0[:, :], scalar=0.5, in1=tt[:, :],
                                                 op0=ALU.is_lt, op1=ALU.mult))
                ch.link(dve.tensor_tensor_scan(cout[:, :], d0[:, :], d1[:, :], ABSENT, ALU.mult, ALU.add))
                ch.link(dve.memset(cinn[:, 0:1], ABSENT))
                ch.link(dve.tensor_copy(cinn[:, 1:P], cout[:, 0:P - 1]))
                dve.sem_inc(s_fx, 1)
                dve.wait_ge(s_fpe, 2)
                dve.wait_ge(s_fg, 16)
                ch.link(dve.scalar_tensor_tensor(out=fixw[:, :], in0=fixv[:, :], scalar=ABSENT, in1=wk[0][:, 0:BS],
                                                 op0=ALU.is_equal, op1=ALU.mult))
                ch.link(dve.scalar_tensor_tensor(out=fixv[:, :], in0=fixv[:, :], scalar=ABSENT, in1=fixv[:, :],
                                                 op0=ALU.not_equal, op1=ALU.mult))
                ch.link(dve.tensor_tensor(fixv[:, :], fixv[:, :], fixw[:, :], ALU.add))
                dve.sem_inc(s_fx, 1)
                dve.wait_ge(s_tok, 16 * NT)
                stats(dve, ch, h_all, cen, s_var, s_std)
                dve.wait_ge(s_av, 16 * AT)
                full = lambda x: x[:, :].unsqueeze(1).broadcast_to([P, AT, BS])
                own = a_val[:, :, :]
                ch.link(dve.tensor_tensor(own, own, full(ndiag), ALU.mult))
                ch.link(dve.tensor_tensor(own, own, full(diag), ALU.add))
                for seq in range(NT // AT):
                    x = dve.tensor_copy(a_vals[:, seq * AT:(seq + 1) * AT, :], own)
                ch.link(x)
                dve_n[0] = ch.base + ch.k

            @block.scalar
            def _(act):
                act.wait_ge(s_var, 1)
                act.activation(rstd[:, :], rstd[:, :], ACT.Sqrt).then_inc(s_std, 1)

            @block.tensor
            def _(pe):
                pe.wait_ge(s_fx, 1)
                pe.transpose(wk[0][0:BS, 0:P], last[:, 1, LC - 1, :], ident[:, :])
                pe.matmul(wk[0][0:BS, P:2 * P], thrub[:, :], ident[:, :], start=True, stop=True).then_inc(s_fpe, 1)
                pe.wait_ge(s_fx, 2)
                pe.transpose(wk[0][:, 0:BS], cinn[:, :], ident[0:BS, 0:BS]).then_inc(s_fpe, 1)

            @block.gpsimd
            def _(pool):
                def gather(dst, src, idx, signal):
                    pool.indirect_dma_start(out=dst, out_offset=None, in_=src,
                                            in_offset=bass.IndirectOffsetOnAxis(ap=idx, axis=0)).then_inc(signal, 16)
                pool.iota(node_i[:, :], [[P, P]], base=0, channel_multiplier=1).then_inc(s_const, 1)
                pool.wait_ge(s_idx, 1)
                for t in range(NT):
                    gather(h_all[:, t], words_d[:, :], id_i[:, t:t + 1], s_tok)
                pool.wait_ge(s_ghr, 1)
                for t in range(NT):
                    pool.indirect_dma_start(out=gsort_d[:, :], out_offset=bass.IndirectOffsetOnAxis(ap=g_head[:, t:t + 1], axis=0),
                                            in_=g_rec[:, t], in_offset=None, bounds_check=PLACES - 1,
                                            oob_is_err=False).then_inc(s_gh, 16)
                pool.wait_ge(s_fx, 1)
                for par in range(2):
                    pool.wait_ge(s_st[par], 16 + 16 * (LCN // 2))
                gather(fixv[:, :], ascan_d[:, :], fixi[:, 0:1], s_fg)
                pool.wait_ge(s_fx, 3)
                pool.indirect_dma_start(out=ascan_d[:, :], out_offset=bass.IndirectOffsetOnAxis(ap=fixi[:, 1:2], axis=0),
                                        in_=fixv[:, :], in_offset=None, bounds_check=PLACES - 1,
                                        oob_is_err=False).then_inc(s_fs, 16)
                pool.wait_ge(s_fs, 16)
                for t in range(AT):
                    gather(a_val[:, t], ascan_d[:, :], a_end[:, t:t + 1], s_av)
                pool.wait_ge(s_tok, 16 * NT)
                pool.wait_ge(s_gh, 16 * NT)
        tmp.close()

        tmp = ExitStack()
        wq = sb("wq", [D + 1, D], where=tmp)
        wkk = sb("wkk", [D + 1, D], where=tmp)
        wv = sb("wv", [D + 1, D], where=tmp)
        wo = sb("wo", [D + 1, D], where=tmp)
        bavg = sb("bavg", [P, P], where=tmp)
        gate4 = sb("gate4", [P, H], where=tmp)
        gateb = sb("gateb", [P, H], where=tmp)
        gw16 = sb("gw16", [P, H * 4], where=tmp)
        gwt = sb("gwt", [4, H], where=tmp)
        gl = sb("gl", [7, H, P], where=tmp)
        gr = sb("gr", [7, H, P], where=tmp)
        neg = sb("neg", [3, H, P], where=tmp)
        gbr = sb("gbr", [1, H, P], where=tmp)
        xs = sb("xs", [P, D], where=tmp)
        xt = sb("xt", [D + 1, P], where=tmp)
        qt = sb("qt", [D, P], where=tmp)
        kt = sb("kt", [D, NB, H, KV], where=tmp)
        ks = sb("ks", [D, NB], where=tmp)
        hm = sb("hm", [D, 2, H], where=tmp)
        vs = sb("vs", [P, D], where=tmp)
        sc = sb("sc", [P, H, KV], where=tmp)
        ex = sb("ex", [P, H, KV], where=tmp)
        mk = sb("mk", [P, BS], where=tmp)
        mv = sb("mv", [P, BS], where=tmp)
        gg = sb("gg", [P, H, BS], where=tmp)
        gv = sb("gv", [P, H, BS], where=tmp)
        cb = sb("cb", [P, H, BS], where=tmp)
        cg = sb("cg", [P, H], where=tmp)
        ct = sb("ct", [P, H, BS], where=tmp)
        mx = sb("mx", [P, 4, H], where=tmp)
        xo = sb("xo", [P, D], where=tmp)
        xm = sb("xm", [P, D], where=tmp)
        ot = sb("ot", [D + 1, P], where=tmp)
        s_aw, s_aw2, s_ac, s_lr = sem("s_aw"), sem("s_aw2"), sem("s_ac"), sem("s_lr")
        s_ape, s_aact, s_adve = sem("s_ape"), sem("s_aact"), sem("s_adve")
        NPE, NACT, NDVE = 6, 4, 6
        with nc.Block() as block:
            @block.sync
            def _(sp):
                sp.wait_ge(s_ac, 1)
                for n, w in enumerate((wq, wkk)):
                    sp.dma_start(w[0:D, :], qkv_wt[:, n * D:(n + 1) * D]).then_inc(s_aw, 16)
                    sp.dma_start(w[D:D + 1, :], qkv_b[:, n * D:(n + 1) * D]).then_inc(s_aw, 16)
                sp.dma_start(wv[0:D, :], qkv_wt[:, 2 * D:3 * D]).then_inc(s_aw, 16)
                sp.dma_start(wv[D:D + 1, :], qkv_b[:, 2 * D:3 * D]).then_inc(s_aw, 16)
                sp.dma_start(wo[0:D, :], proj_wt[:, :]).then_inc(s_aw, 16)
                sp.dma_start(wo[D:D + 1, :], proj_b[:, :]).then_inc(s_aw, 16)
                sp.dma_start(gw16[:, :], gate_w[0:1, :].broadcast_to([P, H * 4])).then_inc(s_aw, 16)
                sp.dma_start(gateb[:, :], gate_b[0:1, :].broadcast_to([P, H])).then_inc(s_aw, 16)
                sp.dma_start(gwt[:, :], gate_wt[:, :]).then_inc(s_aw, 16)
                sp.wait_ge(s_ac, 2)
                sp.dma_start(gr[4:7], neg[:, :, :]).then_inc(s_aw2, 16)
                sp.dma_start(gr[3:4], gbr[:, :, :]).then_inc(s_aw2, 16)
                sp.dma_start(gl[3:4], ones[0:1, :].unsqueeze(1).broadcast_to([1, H, P])).then_inc(s_aw2, 16)
                with sp.Fori(0, STEPS // 2) as i:
                    g_rank.sp_step(sp, i, 0)
                    g_rank.sp_step(sp, i, 1)
                    sp.wait_ge(s_ape, i * NPE + 1)
                    p3 = pos_d[0:3, bass.ds(i * P, P)].unsqueeze(1).broadcast_to([3, H, P])
                    sp.dma_start(gl[4:7], p3).then_inc(s_lr, 16)
                    sp.dma_start(gr[0:3], p3).then_inc(s_lr, 16)

            @block.tensor
            def _(pe):
                g_rank.pe_start(pe)
                pe.matmul(wk[3][:, P:P + D], zerob[:, :], zerob[:, 0:D], start=True, stop=True).then_inc(s_ape, 1)
                pe.wait_ge(s_aw, 16 * 11)
                pe.wait_ge(s_aw2, 48)

                def values(i):
                    pe.wait_ge(s_adve, i * NDVE + 1)
                    pe.sem_inc(s_tick, 1)
                    for b in range(NB):
                        q = slice(BS * b, BS * b + BS)
                        for h in range(H):
                            x = pe.matmul(wk[0][q, P + h * HD:P + (h + 1) * HD], ct[q, h, :], vs[q, h * HD:(h + 1) * HD],
                                          start=True, stop=True, tile_position=(BS * b, BS * b))
                    x.then_inc(s_ape, 1)

                def output_transposed(i, n):
                    pe.wait_ge(s_adve, i * NDVE + n)
                    pe.sem_inc(s_tick, 1)
                    pe.transpose(wk[0][0:D, 2 * P:3 * P], xo[:, :], ident[:, :]).then_inc(s_ape, 1)

                def projection(i, n):
                    pe.wait_ge(s_aact, i * NACT + n)
                    pe.matmul(wk[3][:, P + D:P + 2 * D], ot[:, :], wo[:, :], start=True, stop=True).then_inc(s_ape, 1)

                with pe.Fori(0, STEPS // 2) as i:
                    def stage(slot):
                        dv, ac = (lambda n: pe.wait_ge(s_adve, i * NDVE + (n + 1))), (lambda n: pe.wait_ge(s_aact, i * NACT + n))
                        if slot == 2:
                            values(i)
                        if slot == 3:
                            dv(1)
                            pe.sem_inc(s_tick, 1)
                            pe.transpose(wk[1][0:D, 0:P], xs[:, :], ident[:, :]).then_inc(s_ape, 1)
                        if slot == 5:
                            output_transposed(i, 3)
                            ac(1)
                            pe.matmul(wk[1][0:D, 0:P], wq[:, :], xt[:, :], start=True, stop=True)
                            pe.matmul(wk[2][0:D, 0:P], wkk[:, :], xt[:, :], start=True, stop=True)
                        if slot == 7:
                            projection(i, 2)
                            pe.matmul(wk[0][:, P:P + D], xt[:, :], wv[:, :], start=True, stop=True).then_inc(s_ape, 1)
                        if slot == 10:
                            ac(3)
                            dv(4)
                            pe.wait_ge(s_lr, i * 32 + 32)
                            pe.sem_inc(s_tick, 1)
                        if slot in (10, 11):
                            for b in range(slot * 2 - 20, slot * 2 - 18):
                                q = slice(BS * b, BS * b + BS)
                                pe.matmul(wk[2][q, 0:H * KV], qt[:, q], kt[:, b].rearrange("d h c -> d (h c)"), start=True, stop=True,
                                          tile_position=(0, BS * b))
                                for h in range(H):
                                    pe.matmul(wk[3][q, h * BS:(h + 1) * BS], gl[:, h, q], gr[:, h, q], start=True, stop=True,
                                              tile_position=(0, BS * b))
                        if slot == 11:
                            pe.matmul(wk[3][:, P:P + D], bavg[:, :], vs[:, :], start=True, stop=True).then_inc(s_ape, 1)
                    g_rank.pe_step(pe, i, 0, stage)
                    g_rank.pe_step(pe, i, 1, stage)
                values(NT)
                output_transposed(NT, 2)
                projection(NT, 1)

            @block.scalar
            def _(act):
                g_rank.act_start(act)

                def output_copied(i, n):
                    act.wait_ge(s_ape, i * NPE + n)
                    act.activation(ot[0:D, :], wk[0][0:D, 2 * P:3 * P], ACT.Copy).then_inc(s_aact, 1)

                with act.Fori(0, STEPS // 2) as i:
                    def stage(slot):
                        pe_ = lambda n: act.wait_ge(s_ape, i * NPE + 1 + n)
                        if slot == 4:
                            pe_(2)
                            act.activation(xt[0:D, :], wk[1][0:D, 0:P], ACT.Copy).then_inc(s_aact, 1)
                        if slot == 6:
                            output_copied(i, 4)
                        if slot == 8:
                            pe_(5)
                            act.activation(qt[:, :], wk[1][0:D, 0:P], ACT.Copy, scale=float(HD) ** -0.5)
                            act.activation(vs[:, :], wk[0][:, P:P + D], ACT.Copy).then_inc(s_aact, 1)
                        if slot == 14:
                            act.wait_ge(s_adve, i * NDVE + 6)
                            act.activation(ex[:, :, :], sc[:, :, :], ACT.Exp).then_inc(s_aact, 1)
                    g_rank.act_step(act, i, 0, stage)
                    g_rank.act_step(act, i, 1, stage)
                output_copied(NT, 3)

            @block.vector
            def _(dve):
                ch = Chain(dve, s_dve)
                ch.base = dve_n[0]
                dve.memset(bavg[:, :], 0.0)
                ch.link(dve.memset(xt[D:D + 1, :], 1.0))
                ch.link(dve.memset(ot[D:D + 1, :], 1.0))
                for b in range(NB):
                    ch.link(dve.memset(bavg[BS * b:BS * b + BS, BS * b:BS * b + BS], 1.0 / BS))
                dve.sem_inc(s_ac, 1)
                dve.wait_ge(s_aw, 16 * 11)
                ch.link(dve.tensor_copy(gate4[:, :], gw16[:, :].rearrange("p (h k) -> p h k", k=4)[:, :, 3]))
                w3 = gwt[0:3, :].unsqueeze(2).broadcast_to([3, H, P])
                ch.link(dve.tensor_copy(gl[0:3], w3))
                ch.link(dve.tensor_scalar(neg[:, :, :], w3, -1.0, None, ALU.mult))
                ch.link(dve.tensor_copy(gbr[:, :, :], gateb[0:1, :].unsqueeze(2).broadcast_to([1, H, P])))
                dve.sem_inc(s_ac, 1)
                ch.link(dve.tensor_reduce(hm[:, 0], ident[0:D, 0:D].rearrange("p (h c) -> p h c", c=HD), AX.X, ALU.add))
                ch.link(dve.tensor_scalar(hm[:, 1], hm[:, 0], 1.0 / BS, None, ALU.mult))
                for x in (ct[:, :, :], vs[:, :], cg[:, :]):
                    ch.link(dve.memset(x, 0.0))
                ch.link(dve.memset(h_slots[:, 0, :], 0.0))
                dve.sem_inc(s_adve, 1)
                g_rank.dve_start(dve, ch)
                start = ch.base + ch.k
                flat = lambda x: x.rearrange("p a d -> p (a d)")

                def add_mean(i):
                    dve.wait_ge(s_ape, i * NPE + 2)
                    ch.link(dve.tensor_tensor(xm[:, :].rearrange("p (h d) -> p h d", d=HD),
                                              wk[3][:, P:P + D].rearrange("p (h d) -> p h d", d=HD),
                                              cg[:, :].unsqueeze(2).broadcast_to([P, H, HD]), ALU.mult))
                    dve.tensor_tensor(xo[:, :], wk[0][:, P:P + D], xm[:, :], ALU.add).then_inc(s_adve, 1)

                def residual(i, n):
                    dve.wait_ge(s_ape, i * NPE + n)
                    r = flat(h_slots[:, bass.ds(i, 1), :])
                    dve.tensor_tensor(r, r, wk[3][:, P + D:P + 2 * D], ALU.add).then_inc(s_adve, 1)

                with dve.Fori(0, STEPS // 2) as i:
                    ch.enter(i, 16, start)
                    tile = bass.ds(i, 1)
                    row = lambda x: x.unsqueeze(1).broadcast_to([P, H, BS])
                    def stage(slot):
                        pe_ = lambda n: dve.wait_ge(s_ape, i * NPE + 1 + n)
                        if slot == 0:
                            ch.link(dve.tensor_tensor(xs[:, :], flat(h_all[:, tile, :]), mean[:, tile].broadcast_to([P, D]), ALU.subtract))
                            dve.tensor_tensor(xs[:, :], xs[:, :], rstd[:, tile].broadcast_to([P, D]), ALU.mult).then_inc(s_adve, 1)
                        if slot == 2:
                            add_mean(i)
                        if slot == 1:
                            ch.put(dve.tensor_scalar(mk[:, :], flat(a_vals[:, tile, :]), ABSENT / 2, None, ALU.is_gt))
                        if slot == 3:
                            ch.settle()
                            ch.put(dve.tensor_tensor(mv[:, :], flat(a_vals[:, tile, :]), mk[:, :], ALU.mult))
                        if slot == 4:
                            ch.settle()
                            ch.put(dve.tensor_tensor(gv[:, :, :], row(mv[:, :]), gate4[:, :].unsqueeze(2).broadcast_to([P, H, BS]), ALU.mult))
                        if slot == 6:
                            ch.settle()
                            residual(i, 5)
                            pe_(5)
                            k4 = wk[2][0:D, 0:P].rearrange("p (b c) -> p b c", c=BS)
                            dve.tensor_tensor(kt[:, :, :, 0:BS], k4.unsqueeze(2).broadcast_to([D, NB, H, BS]),
                                              hm[:, 0].unsqueeze(1).unsqueeze(3).broadcast_to([D, NB, H, BS]), ALU.mult)
                            ch.link(dve.tensor_reduce(ks[:, :], k4, AX.X, ALU.add))
                            dve.tensor_tensor(kt[:, :, :, BS], ks[:, :].unsqueeze(2).broadcast_to([D, NB, H]),
                                              hm[:, 1].unsqueeze(1).broadcast_to([D, NB, H]), ALU.mult).then_inc(s_adve, 1)
                        if slot == 11:
                            pe_(6)
                            dve.tensor_tensor(sc[:, :, 0:BS], wk[2][:, 0:H * KV].rearrange("p (h c) -> p h c", c=KV)[:, :, 0:BS],
                                              row(flat(a_vals[:, tile, :])), ALU.add)
                            ch.link(dve.tensor_scalar(sc[:, :, BS], wk[2][:, 0:H * KV].rearrange("p (h c) -> p h c", c=KV)[:, :, BS],
                                                      1.0, None, ALU.add))
                            ch.link(dve.tensor_reduce(mx[:, 0, :], sc[:, :, :], AX.X, ALU.max))
                            dve.tensor_tensor(sc[:, :, :], sc[:, :, :], mx[:, 0, :].unsqueeze(2).broadcast_to([P, H, KV]),
                                              ALU.subtract).then_inc(s_adve, 1)
                        if slot == 12:
                            ch.link(dve.tensor_tensor(gg[:, :, :], wk[3][:, 0:P].rearrange("p (h c) -> p h c", c=BS), row(mk[:, :]), ALU.mult))
                            ch.put(dve.tensor_tensor(gg[:, :, :], gg[:, :, :], gv[:, :, :], ALU.add))
                        if slot == 13:
                            dve.wait_ge(s_aact, i * NACT + 4)
                            ch.link(dve.tensor_reduce(mx[:, 1, :], ex[:, :, :], AX.X, ALU.add))
                            ch.link(dve.reciprocal(mx[:, 2, :], mx[:, 1, :]))
                            ch.link(dve.tensor_tensor(sc[:, :, :], ex[:, :, :], mx[:, 2, :].unsqueeze(2).broadcast_to([P, H, KV]), ALU.mult))
                            ch.link(dve.tensor_tensor(cb[:, :, :], sc[:, :, 0:BS], gg[:, :, :], ALU.add))
                            dve.transpose(ct[:, :, :].rearrange("p h c -> p (h c)"), cb[:, :, :].rearrange("p h c -> p (h c)")).then_inc(s_adve, 1)
                            ch.put(dve.tensor_tensor(cg[:, :], sc[:, :, BS], gate4[:, :], ALU.add))
                        if slot == 14:
                            ch.settle()
                            ch.put(dve.tensor_tensor(cg[:, :], cg[:, :], gateb[:, :], ALU.add))
                        if slot == 15:
                            ch.settle()
                    g_rank.dve_step(dve, i, 0, stage)
                    g_rank.dve_step(dve, i, 1, stage)
                ch.leave(STEPS // 2)
                ch.base, ch.k = ch.base + ch.k, 0
                add_mean(NT)
                residual(NT, 4)
                dve_n[0] = ch.base + ch.k

            @block.gpsimd
            def _(pool):
                g_rank.pool_start(pool)
                with pool.Fori(0, STEPS // 2) as i:
                    g_rank.pool_step(pool, i, 0)
                    g_rank.pool_step(pool, i, 1)
                g_rank.pool_end(pool)
        tmp.close()
        both.close()

        G4 = 4 * P
        GN = N // G4
        x2t = sb("x2t", [P, N // 2])
        w1s = sb("w1s", [P, 2, NX, FF])
        w2s = sb("w2s", [FF, NX, D])
        b1s = sb("b1s", [FF, NX])
        b2s = sb("b2s", [P, NX * D])
        tmp = ExitStack()
        cen = sb("cen2", [P, NT, D], where=tmp)
        w24 = sb("w24", [P, 2, GW], where=tmp)
        att = sb("att", [P, 2, H * NX], where=tmp)
        attw = sb("attw", [P, 2, H * NX], where=tmp)
        x4 = sb("x4", [P, 2, 4, D], where=tmp)
        x4t = sb("x4t", [P, 2, 2 * P], where=tmp)
        nodes = sb("nodes", [P, NT, GW], where=tmp)
        zero4 = sb("zero4", [P, 4, GW], where=tmp)
        s_fw, s_w24, s_x4, s_tr, s_xc, s_nt, s_nc, s_var2, s_std2, s_nd = (sem(n) for n in (
            "s_fw", "s_w24", "s_x4", "s_tr", "s_xc", "s_nt", "s_nc", "s_var2", "s_std2", "s_nd"))
        with nc.Block() as block:
            @block.sync
            def _(sp):
                sp.wait_ge(s_w24, 1)
                for b in range(2):
                    sp.dma_start(w24[b * D:(b + 1) * D, b, 0:H * NX], w_gat[:, :]).then_inc(s_fw, 16)
                    sp.dma_start(w1s[b * D:(b + 1) * D, b], w1.rearrange("x d f -> d x f")).then_inc(s_fw, 16)
                sp.dma_start(att[:, 0], att_src[0:1, :].broadcast_to([P, H * NX])).then_inc(s_fw, 16)
                sp.dma_start(att[:, 1], att_dst[0:1, :].broadcast_to([P, H * NX])).then_inc(s_fw, 16)
                sp.dma_start(w2s[:, :, :], w2.rearrange("x f d -> f x d")).then_inc(s_fw, 16)
                sp.dma_start(b1s[:, :], b1t[:, :]).then_inc(s_fw, 16)
                sp.dma_start(b2s[:, :], b2[0:1, :].broadcast_to([P, NX * D])).then_inc(s_fw, 16)
                sp.wait_ge(s_nc, 2 + GN)
                sp.dma_start(node_d.rearrange("(t p) f -> p t f", p=P), nodes[:, :, :]).then_inc(s_nd, 16)
                sp.wait_ge(s_nd, 16)

            @block.vector
            def _(dve):
                ch = Chain(dve, s_dve)
                ch.base = dve_n[0]
                ch.link(dve.memset(w24[:, :, :], 0.0))
                ch.link(dve.memset(w1s[:, :, :, :], 0.0))
                dve.sem_inc(s_w24, 1)
                dve.wait_ge(s_fw, 16 * 9)
                for b in range(2):
                    w = w24[:, b:b + 1, 0:H * NX].broadcast_to([P, 2, H * NX])
                    ch.link(dve.tensor_tensor(attw[:, :, :], att[:, :, :], w, ALU.mult))
                    ch.link(dve.tensor_reduce(w24[:, b, H * NX:GW], attw[:, :, :].rearrange("d k (h x) -> d (k h) x", x=NX), AX.X, ALU.add))
                dve.sem_inc(s_w24, 1)
                ch.link(dve.memset(zero4[:, :, :], 0.0))
                stats(dve, ch, h_all, cen, s_var2, s_std2)
                start = ch.base + ch.k
                with dve.Fori(0, GN // 2) as i:
                    ch.enter(i, 2, start)
                    for par in range(2):
                        four = bass.ds(i * 8 + par * 4, 4)
                        wide = lambda x: x[:, four].unsqueeze(2).broadcast_to([P, 4, D])
                        dve.wait_ge(s_tr, i * 2 + (par + 1))
                        ch.link(dve.tensor_tensor(x4[:, par], h_all[:, four, :], wide(mean), ALU.subtract))
                        dve.tensor_tensor(x4[:, par], x4[:, par], wide(rstd), ALU.mult).then_inc(s_x4, 1)
                    for par in range(2):
                        four = bass.ds(i * 8 + par * 4, 4)
                        dve.wait_ge(s_nt, i * 2 + (par + 1))
                        dve.tensor_tensor(nodes[:, four, :], wk[2 + par][:, 0:4 * GW].rearrange("p (t f) -> p t f", f=GW),
                                          zero4[:, :, :], ALU.add).then_inc(s_nc, 1)
                ch.leave(GN // 2)
                dve_n[0] = ch.base

            @block.tensor
            def _(pe):
                pe.sem_inc(s_tr, 2)
                pe.wait_ge(s_w24, 2)
                with pe.Fori(0, GN // 2) as i:
                    for par in range(2):
                        pe.wait_ge(s_x4, i * 2 + (par + 1))
                        pe.wait_ge(s_xc, i * 2 + (par + 1))
                        pe.sem_inc(s_tick, 1)
                        for t in range(2):
                            x = pe.transpose(wk[par][:, bass.ts(t, P)], x4[:, par, 2 * t:2 * t + 2].rearrange("p b d -> p (b d)"),
                                             ident[:, :])
                        x.then_inc(s_tr, 1)
                        pe.wait_ge(s_xc, i * 2 + (par + 3))
                        pe.wait_ge(s_nc, i * 2 + (par + 1))
                        pe.sem_inc(s_tick, 1)
                        for t in range(2):
                            x = pe.matmul(wk[2 + par][:, t * 2 * GW:(t + 1) * 2 * GW], x4t[:, par, bass.ts(t, P)],
                                          w24[:, :, :].rearrange("d b f -> d (b f)"), start=True, stop=True)
                        x.then_inc(s_nt, 1)

            @block.scalar
            def _(act):
                act.wait_ge(s_var2, 1)
                act.activation(rstd[:, :], rstd[:, :], ACT.Sqrt).then_inc(s_std2, 1)
                act.sem_inc(s_xc, 2)
                act.sem_inc(s_nc, 2)
                with act.Fori(0, GN // 2) as i:
                    for par in range(2):
                        act.wait_ge(s_tr, i * 2 + (par + 3))
                        act.activation(x2t[:, bass.ds(i * G4 + par * 2 * P, 2 * P)], wk[par][:, 0:2 * P], ACT.Copy)
                        act.wait_ge(s_nc, i * 2 + (par + 1))
                        act.activation(x4t[:, par], wk[par][:, 0:2 * P], ACT.Copy).then_inc(s_xc, 1)
        tmp.close()

        final = ExitStack()
        gsum = sb("gsum", [P, NT, GW])
        tmp = ExitStack()
        hid = scratch[:, 0:2 * G4].rearrange("p (b n) -> p b n", b=2)
        yb = scratch[:, 2 * G4:6 * G4].rearrange("p (b t x d) -> p b t x d", b=2, t=4, x=NX)
        gs = sb("gs", [P, RUN + 2 * GC, 4], where=tmp)
        rows = sb("rows", [P, 2, GC, GW], where=tmp)
        srci = sb("srci", [P, 2, GC], I32, tmp)
        keep = sb("keep", [P, 2, GC], where=tmp)
        head = sb("head", [P, 2, GC], where=tmp)
        drop = sb("drop", [P, 2, GC], where=tmp)
        adin = sb("adin", [P, GC, H], where=tmp)
        adst = sb("adst", [P, 2, GC, H], where=tmp)
        escore = sb("escore", [P, GC, H], where=tmp)
        mrun = sb("mrun", [P, 2, GC + 1, H], where=tmp)
        expin = sb("expin", [P, 2, 2, GC, H], where=tmp)
        expout = sb("expout", [P, 2, 2, GC, H], where=tmp)
        decay = sb("decay", [P, GC, H], where=tmp)
        msg = sb("msg", [P, GC, H * NX], where=tmp)
        scan = sb("scan", [P, 2, GC, GW], where=tmp)
        leadg = scratch[:, 6 * G4:6 * G4 + RUN]
        gfix = sb("gfix", [P, 6], where=tmp)
        gfixi = sb("gfixi", [P, 3], I32, tmp)
        first = sb("first", [P, GW], where=tmp)
        C = H + H * NX
        tm = sb("tm", [P, C], where=tmp)
        tv = sb("tv", [P, C], where=tmp)
        fb = sb("fb", [P, C], where=tmp)
        cx = rows[0:C, :, :, :].rearrange("p b t f -> p (b t f)")[:, 0:8 * P].rearrange("p (k n) -> p k n", k=8)
        fxr = sb("fxr", [P, GW], where=tmp)
        fx = sb("fx", [P, 7, C], where=tmp)
        s_gl, s_si, s_first, s_gfx, s_gpe, s_gfg, s_gfs, s_gsum = (sem(n) for n in (
            "s_gl", "s_si", "s_first", "s_gfx", "s_gpe", "s_gfg", "s_gfs", "s_gsum"))
        s_rows = [sem(f"s_rows{x}") for x in range(2)]
        s_ys = [sem(f"s_ys{x}") for x in range(2)]
        s_gst = [sem(f"s_gst{x}") for x in range(2)]
        s_m1, s_gel, s_m2, s_y, s_exi, s_exo, s_scan = (sem(n) for n in ("s_m1", "s_gel", "s_m2", "s_y", "s_exi", "s_exo", "s_scan"))
        s_seed, s_gsp = sem("s_seed"), sem("s_gsp")
        assert GCN == GN
        scan_g = gscan_d.rearrange("(p t) f -> p t f", p=P)
        experts_v = expert_d.rearrange("p (t b) x d -> p b t x d", b=2)
        with nc.Block() as block:
            @block.sync
            def _(sp):
                sp.dma_start(gs[:, 0:RUN, :], gsort_d.rearrange("(p t) f -> p t f", p=P)).then_inc(s_gl, 16)
                for par in range(2):
                    sp.dma_start(credit_d[par:par + 1, :], ones[0:1, :]).then_inc(s_gst[par], 16)
                    sp.dma_start(credit_d[par + 2:par + 3, :], ones[0:1, :]).then_inc(s_ys[par], 16)
                with sp.Fori(0, GCN // 2) as i:
                    for par in range(2):
                        sp.wait_ge(s_y, i * (2 * NX) + (par * NX + NX + 2))
                        sp.dma_start(experts_v[:, par, bass.ds(i * 4, 4)], yb[:, par]).then_inc(s_ys[par], 16)
                        sp.wait_ge(s_scan, i * 2 + (par + 1))
                        sp.dma_start(scan_g[:, bass.ds(i * (2 * GC) + par * GC, GC), :], scan[:, par]).then_inc(s_gst[par], 16)
                for par in range(2):
                    sp.wait_ge(s_gst[par], 16 + 16 * (GCN // 2))
                    sp.wait_ge(s_ys[par], 16 + 16 * (GN // 2))
                sp.sem_inc(s_gsp, 1)

            @block.gpsimd
            def _(pool):
                def gather(dst, src, idx, signal):
                    pool.indirect_dma_start(out=dst, out_offset=None, in_=src,
                                            in_offset=bass.IndirectOffsetOnAxis(ap=idx, axis=0)).then_inc(signal, 16)
                pool.wait_ge(s_seed, 1)
                gather(first[:, :], node_d[:, :], gfixi[:, 2:3], s_first)
                with pool.Fori(0, GCN // 2) as i:
                    for par in range(2):
                        pool.wait_ge(s_si, i * 2 + (par + 1))
                        pool.sem_inc(s_tick, 1)
                        for t in range(GC):
                            gather(rows[:, par, t], node_d[:, :], srci[:, par, t:t + 1], s_rows[par])
                pool.wait_ge(s_gfx, 1)
                pool.wait_ge(s_gsp, 1)
                gather(fxr[:, :], gscan_d[:, :], gfixi[:, 0:1], s_gfg)
                pool.wait_ge(s_gfx, 3)
                pool.indirect_dma_start(out=gscan_d[:, :], out_offset=bass.IndirectOffsetOnAxis(ap=gfixi[:, 1:2], axis=0),
                                        in_=fxr[:, :], in_offset=None, bounds_check=PLACES - 1,
                                        oob_is_err=False).then_inc(s_gfs, 16)
                pool.wait_ge(s_gfs, 16)
                for t in range(NT):
                    gather(gsum[:, t], gscan_d[:, :], g_end[:, t:t + 1], s_gsum)
                pool.wait_ge(s_gsum, 16 * NT)

            @block.tensor
            def _(pe):
                with pe.Fori(0, GN // 2) as i:
                    for par in range(2):
                        for x in range(NX):
                            k = par * NX + x
                            pe.wait_ge(s_gel, i * (2 * NX) + (k + 1))
                            pe.matmul(wk[x % 2][:, :], w1s[:, par, x, :], x2t[:, bass.ds(i * G4, G4)],
                                      start=True, stop=True).then_inc(s_m1, 1)
                            pe.wait_ge(s_gel, i * (2 * NX) + (k + 3))
                            pe.wait_ge(s_y, i * (2 * NX) + (k + 1))
                            for t in range(4):
                                m = pe.matmul(wk[2 + x % 2][:, t * D:(t + 1) * D], hid[:, x % 2, bass.ts(t, P)], w2s[:, x, :],
                                              start=True, stop=True)
                            m.then_inc(s_m2, 1)
                pe.wait_ge(s_gfx, 1)
                pe.transpose(wk[0][0:C, 0:P], tm[:, :], ident[:, :])
                pe.transpose(wk[0][0:C, P:2 * P], tv[:, :], ident[:, :])
                pe.matmul(wk[0][0:C, 2 * P:3 * P], fb[:, :], ident[:, :], start=True, stop=True).then_inc(s_gpe, 1)
                pe.wait_ge(s_gfx, 2)
                pe.transpose(wk[0][:, 0:C], cx[:, 6], ident[0:C, 0:C])
                pe.transpose(wk[0][:, C:2 * C], cx[:, 7], ident[0:C, 0:C]).then_inc(s_gpe, 1)

            @block.scalar
            def _(act):
                act.sem_inc(s_gel, 2)
                with act.Fori(0, GN // 2) as i:
                    for par in range(2):
                        for x in range(NX):
                            k = par * NX + x
                            act.wait_ge(s_m1, i * (2 * NX) + (k + 1))
                            act.wait_ge(s_m2, i * (2 * NX) + (k + 1))
                            act.activation(hid[:, x % 2], wk[x % 2][:, :], ACT.Gelu, bias=b1s[:, x:x + 1]).then_inc(s_gel, 1)
                        act.wait_ge(s_exi, i * 2 + (par + 1))
                        act.activation(expout[:, par], expin[:, par], ACT.Exp).then_inc(s_exo, 1)
                for n, (o, x) in enumerate(((cx[:, 5], cx[:, 4]), (fx[:, 5], fx[:, 4]))):
                    act.wait_ge(s_exi, GCN + 2 * n + 1)
                    act.activation(o, x, ACT.Exp).then_inc(s_exo, 1)
                    act.wait_ge(s_exi, GCN + 2 * n + 2)
                    act.activation(o, x, ACT.Exp).then_inc(s_exo, 1)

            @block.vector
            def _(dve):
                ch = Chain(dve, s_dve)
                ch.base = dve_n[0]
                dve.wait_ge(s_gl, 16)
                gsi = gs[:, :, :].bitcast(I32)
                kp = gs[:, 0:RUN, 2]
                ch.link(dve.tensor_copy(gfixi[:, 2:3], gsi[:, 0, 1:2]))
                dve.sem_inc(s_seed, 1)
                for par in range(2):
                    ch.link(dve.tensor_copy(srci[:, par], gsi[:, par * GC:(par + 1) * GC, 0]))
                    dve.sem_inc(s_si, 1)
                ch.link(dve.memset(gs[:, RUN:RUN + 2 * GC, :], 0.0))
                ch.link(dve.tensor_tensor_scan(leadg[:, :], kp, kp, 1.0, ALU.mult, ALU.mult))
                ch.link(dve.tensor_reduce(gfix[:, 0:1], leadg[:, :], AX.X, ALU.add))
                ch.link(dve.tensor_scalar(gfix[:, 1:2], gfix[:, 0:1], float(RUN), None, ALU.is_equal))
                ch.link(dve.tensor_copy(fb[:, :], gfix[:, 1:2].broadcast_to([P, C])))
                ch.link(dve.tensor_tensor(gfix[:, 2:3], gfix[:, 0:1], part_f[:, :], ALU.add))
                ch.link(dve.tensor_scalar(gfix[:, 3:4], gfix[:, 2:3], -1.0, 0.0, ALU.add, ALU.max))
                ch.link(dve.tensor_copy(gfixi[:, 0:1], gfix[:, 3:4]))
                ch.link(dve.tensor_scalar(gfix[:, 4:5], gfix[:, 0:1], 0.0, SKIP, ALU.is_equal, ALU.mult))
                ch.link(dve.tensor_tensor(gfix[:, 5:6], gfix[:, 3:4], gfix[:, 4:5], ALU.add))
                ch.link(dve.tensor_copy(gfixi[:, 1:2], gfix[:, 5:6]))
                dve.sem_inc(s_m2, 2)
                dve.sem_inc(s_y, 2)
                start = ch.base + ch.k
                ch.link(dve.memset(scan[:, 1, GC - 1, :], 0.0))
                ch.link(dve.memset(mrun[:, 1, GC, :], ABSENT))
                dve.wait_ge(s_first, 16)
                ch.link(dve.tensor_copy(adst[:, 1, GC - 1, :], first[:, GW - H:GW]))
                start = ch.base + ch.k
                with dve.Fori(0, GCN // 2) as i:
                    ch.enter(i, 34, start)
                    for par in range(2):
                        dve.wait_ge(s_ys[par], i * 16 + 16)
                        for x in range(NX):
                            dve.wait_ge(s_m2, i * (2 * NX) + (par * NX + x + 3))
                            dve.tensor_tensor(yb[:, par, :, x, :], wk[2 + x % 2][:, 0:4 * D].rearrange("p (t d) -> p t d", d=D),
                                              b2s[:, x * D:(x + 1) * D].unsqueeze(1).broadcast_to([P, 4, D]), ALU.add).then_inc(s_y, 1)
                        wide = lambda x: x.unsqueeze(2).broadcast_to([P, GC, H])
                        dve.wait_ge(s_rows[par], i * (16 * GC) + 16 * GC)
                        r = rows[:, par]
                        here = bass.ds(i * (2 * GC) + par * GC, GC)
                        ch.link(dve.tensor_scalar(keep[:, par], gs[:, here, 2], 0.0, None, ALU.add))
                        ch.link(dve.tensor_scalar(head[:, par], keep[:, par], -1.0, 1.0, ALU.mult, ALU.add))
                        ch.link(dve.tensor_scalar(drop[:, par], head[:, par], ABSENT, None, ALU.mult))
                        ch.link(dve.tensor_tensor(adin[:, :, :], r[:, :, GW - H:GW], wide(head[:, par]), ALU.mult))
                        for h in range(H):
                            x = dve.tensor_tensor_scan(adst[:, par, :, h], keep[:, par], adin[:, :, h],
                                                       adst[:, 1 - par, GC - 1, h:h + 1], ALU.mult, ALU.add)
                        ch.link(x)
                        ch.link(dve.tensor_tensor(escore[:, :, :], r[:, :, H * NX:H * NX + H], adst[:, par], ALU.add))
                        ch.link(dve.scalar_tensor_tensor(out=escore[:, :, :], in0=escore[:, :, :], scalar=0.2,
                                                         in1=escore[:, :, :], op0=ALU.mult, op1=ALU.max))
                        ch.link(dve.tensor_copy(mrun[:, par, 0, :], mrun[:, 1 - par, GC, :]))
                        for h in range(H):
                            x = dve.tensor_tensor_scan(mrun[:, par, 1:GC + 1, h], drop[:, par], escore[:, :, h],
                                                       mrun[:, par, 0, h:h + 1], ALU.add, ALU.max)
                        ch.link(x)
                        ch.link(dve.tensor_tensor(expin[:, par, 0], mrun[:, par, 0:GC, :], mrun[:, par, 1:GC + 1, :], ALU.subtract))
                        ch.link(dve.tensor_scalar(expin[:, par, 0], expin[:, par, 0], 0.0, None, ALU.min))
                        ch.link(dve.tensor_tensor(expin[:, par, 1], escore[:, :, :], mrun[:, par, 1:GC + 1, :], ALU.subtract))
                        dve.sem_inc(s_exi, 1)
                        dve.wait_ge(s_exo, i * 2 + (par + 1))
                        ch.link(dve.tensor_tensor(decay[:, :, :], expout[:, par, 0], wide(keep[:, par]), ALU.mult))
                        ch.link(dve.tensor_tensor(msg[:, :, :].rearrange("p t (h x) -> p t h x", x=NX),
                                                  r[:, :, 0:H * NX].rearrange("p t (h x) -> p t h x", x=NX),
                                                  expout[:, par, 1].unsqueeze(3).broadcast_to([P, GC, H, NX]), ALU.mult))
                        dve.wait_ge(s_gst[par], i * 16 + 16)
                        ch.link(dve.tensor_copy(scan[:, par, :, H:2 * H], mrun[:, par, 1:GC + 1, :]))
                        for h in range(H):
                            dve.tensor_tensor_scan(scan[:, par, :, h], decay[:, :, h], expout[:, par, 1, :, h],
                                                   scan[:, 1 - par, GC - 1, h:h + 1], ALU.mult, ALU.add)
                            for x in range(NX):
                                c = h * NX + x
                                y = dve.tensor_tensor_scan(scan[:, par, :, 2 * H + c], decay[:, :, h], msg[:, :, c],
                                                           scan[:, 1 - par, GC - 1, 2 * H + c:2 * H + c + 1], ALU.mult, ALU.add)
                        ch.link(y)
                        dve.sem_inc(s_scan, 1)
                        ahead = bass.ds(i * (2 * GC) + (par + 2) * GC, GC)
                        ch.link(dve.tensor_copy(srci[:, par], gsi[:, ahead, 0]))
                        dve.sem_inc(s_si, 1)
                ch.leave(GCN // 2)
                t = scan[:, 1, GC - 1, :]
                m20 = lambda o, m: (dve.tensor_copy(o[:, 0:H], m),
                                    dve.tensor_copy(o[:, H:C].rearrange("p (h x) -> p h x", x=NX),
                                                    m.unsqueeze(2).broadcast_to([P, H, NX])))[1]
                v20 = lambda o, r: (dve.tensor_copy(o[:, 0:H], r[:, 0:H]), dve.tensor_copy(o[:, H:C], r[:, 2 * H:GW]))[1]
                ch.link(m20(tm, t[:, H:2 * H]))
                ch.link(v20(tv, t))
                dve.sem_inc(s_gfx, 1)
                dve.wait_ge(s_gpe, 1)
                TM, TV, F, CM, EX, EO, MP, CV = (cx[:, n] for n in range(8))
                ch.link(dve.tensor_copy(TM, wk[0][0:C, 0:P]))
                ch.link(dve.tensor_copy(TV, wk[0][0:C, P:2 * P]))
                ch.link(dve.tensor_scalar(F, wk[0][0:C, 2 * P:3 * P], -1.0, -ABSENT, ALU.add, ALU.mult))
                ch.link(dve.tensor_tensor_scan(CM, F, TM, ABSENT, ALU.add, ALU.max))
                ch.link(dve.tensor_copy(F, wk[0][0:C, 2 * P:3 * P]))
                ch.link(dve.memset(MP[:, 0:1], ABSENT))
                ch.link(dve.tensor_copy(MP[:, 1:P], CM[:, 0:P - 1]))
                ch.link(dve.tensor_tensor(EX, MP, CM, ALU.subtract))
                ch.link(dve.tensor_scalar(EX, EX, 0.0, None, ALU.min))
                dve.sem_inc(s_exi, 1)
                dve.wait_ge(s_exo, GCN + 1)
                ch.link(dve.tensor_tensor(F, F, EO, ALU.mult))
                ch.link(dve.tensor_tensor(EX, TM, CM, ALU.subtract))
                dve.sem_inc(s_exi, 1)
                dve.wait_ge(s_exo, GCN + 2)
                ch.link(dve.tensor_tensor(TV, TV, EO, ALU.mult))
                ch.link(dve.tensor_tensor_scan(CM, F, TV, 0.0, ALU.mult, ALU.add))
                ch.link(dve.memset(CV[:, 0:1], 0.0))
                ch.link(dve.tensor_copy(CV[:, 1:P], CM[:, 0:P - 1]))
                dve.sem_inc(s_gfx, 1)
                dve.wait_ge(s_gpe, 2)
                dve.wait_ge(s_gfg, 16)
                FM, FV, CMP, CVP, X, O, M = (fx[:, n] for n in range(7))
                ch.link(m20(FM, fxr[:, H:2 * H]))
                ch.link(v20(FV, fxr))
                ch.link(dve.tensor_copy(CMP, wk[0][:, 0:C]))
                ch.link(dve.tensor_copy(CVP, wk[0][:, C:2 * C]))
                ch.link(dve.tensor_tensor(M, FM, CMP, ALU.max))
                ch.link(dve.tensor_tensor(X, FM, M, ALU.subtract))
                dve.sem_inc(s_exi, 1)
                dve.wait_ge(s_exo, GCN + 3)
                ch.link(dve.tensor_tensor(FV, FV, O, ALU.mult))
                ch.link(dve.tensor_tensor(X, CMP, M, ALU.subtract))
                dve.sem_inc(s_exi, 1)
                dve.wait_ge(s_exo, GCN + 4)
                ch.link(dve.tensor_tensor(CVP, CVP, O, ALU.mult))
                ch.link(dve.tensor_tensor(FV, FV, CVP, ALU.add))
                dve.tensor_copy(fxr[:, 0:H], FV[:, 0:H])
                dve.tensor_copy(fxr[:, H:2 * H], M[:, 0:H])
                ch.link(dve.tensor_copy(fxr[:, 2 * H:GW], FV[:, H:C]))
                dve.sem_inc(s_gfx, 1)
                dve_n[0] = ch.base + ch.k
        tmp.close()

        agg = sb("agg", [P, NT, H * NX])
        sqr = sb("sqr", [P, NT, H * NX])
        consts = sb("consts", [P, 3, H * NX])
        st = sb("st", [P, 4, NT])
        score = sb("score", [P, NT, NX])
        rank = sb("rank", [P, NT, NX])
        cmp_ = sb("cmp", [P, NT])
        gate = sb("gate", [P, NT, NX])
        ye = sb("ye", [P, 2, 4, NX, D])
        yp = sb("yp", [P, 2, 4, NX, D])
        yo = sb("yo", [P, 2, 4, D])
        s_k, s_v3, s_s3, s_e3, s_x3, s_yf, s_of = (sem(n) for n in ("s_k", "s_v3", "s_s3", "s_e3", "s_x3", "s_yf", "s_of"))
        s_yl = [sem(f"s_yl{x}") for x in range(2)]
        s_o = [sem(f"s_o{x}") for x in range(2)]
        with nc.Block() as block:
            @block.sync
            def _(sp):
                for n, c in enumerate((b_gat, ln_g, ln_b)):
                    sp.dma_start(consts[:, n], c[0:1, :].broadcast_to([P, H * NX])).then_inc(s_k, 16)
                for par in range(2):
                    sp.dma_start(credit_d[par:par + 1, :], ones[0:1, :]).then_inc(s_o[par], 16)
                with sp.Fori(0, GN // 2) as i:
                    for par in range(2):
                        sp.wait_ge(s_yf, i * 2 + (par + 1))
                        sp.dma_start(ye[:, par], expert_d[:, bass.ds(i * 8 + par * 4, 4)]).then_inc(s_yl[par], 16)
                    for par in range(2):
                        sp.wait_ge(s_of, i * 2 + (par + 1))
                        sp.dma_start(out[:, bass.ds(i * 8 + par * 4, 4), :], yo[:, par]).then_inc(s_o[par], 16)
                for par in range(2):
                    sp.wait_ge(s_o[par], 16 + 16 * (GN // 2))

            @block.scalar
            def _(act):
                act.wait_ge(s_v3, 1)
                act.activation(st[:, 1], st[:, 1], ACT.Sqrt).then_inc(s_s3, 1)
                act.wait_ge(s_e3, 1)
                act.activation(gate[:, :, :], gate[:, :, :], ACT.Exp).then_inc(s_x3, 1)

            @block.vector
            def _(dve):
                ch = Chain(dve, s_dve)
                ch.base = dve_n[0]
                HX = H * NX
                per = lambda x: x.unsqueeze(2).broadcast_to([P, NT, HX])
                con = lambda n: consts[:, n].unsqueeze(1).broadcast_to([P, NT, HX])
                dve.wait_ge(s_k, 48)
                ch.link(dve.tensor_scalar(gsum[:, :, 0:H], gsum[:, :, 0:H], 1e-16, None, ALU.add))
                ch.link(dve.reciprocal(gsum[:, :, H:2 * H], gsum[:, :, 0:H]))
                ch.link(dve.tensor_tensor(agg[:, :, :].rearrange("p t (h x) -> p t h x", x=NX),
                                          gsum[:, :, 2 * H:GW].rearrange("p t (h x) -> p t h x", x=NX),
                                          gsum[:, :, H:2 * H].unsqueeze(3).broadcast_to([P, NT, H, NX]), ALU.mult))
                ch.link(dve.tensor_tensor(agg[:, :, :], agg[:, :, :], con(0), ALU.add))
                ch.link(dve.tensor_reduce(st[:, 0], agg[:, :, :], AX.X, ALU.add))
                ch.link(dve.tensor_scalar(st[:, 0], st[:, 0], 1.0 / HX, None, ALU.mult))
                ch.link(dve.tensor_tensor(agg[:, :, :], agg[:, :, :], per(st[:, 0]), ALU.subtract))
                ch.link(dve.tensor_tensor(sqr[:, :, :], agg[:, :, :], agg[:, :, :], ALU.mult))
                ch.link(dve.tensor_reduce(st[:, 1], sqr[:, :, :], AX.X, ALU.add))
                ch.link(dve.tensor_scalar(st[:, 1], st[:, 1], 1.0 / HX, EPS, ALU.mult, ALU.add))
                dve.sem_inc(s_v3, 1)
                dve.wait_ge(s_s3, 1)
                ch.link(dve.reciprocal(st[:, 2], st[:, 1]))
                ch.link(dve.tensor_tensor(agg[:, :, :], agg[:, :, :], per(st[:, 2]), ALU.mult))
                ch.link(dve.tensor_tensor(agg[:, :, :], agg[:, :, :], con(1), ALU.mult))
                ch.link(dve.tensor_tensor(agg[:, :, :], agg[:, :, :], con(2), ALU.add))
                ch.link(dve.tensor_reduce(score[:, :, :], agg[:, :, :].rearrange("p t (h x) -> p t x h", x=NX), AX.X, ALU.add))
                ch.link(dve.tensor_scalar(score[:, :, :], score[:, :, :], 1.0 / H, None, ALU.mult))
                ch.link(dve.memset(rank[:, :, :], 0.0))
                for a in range(NX):
                    for b in range(NX):
                        if a != b:
                            ch.link(dve.tensor_tensor(cmp_[:, :], score[:, :, b], score[:, :, a], ALU.is_ge if b < a else ALU.is_gt))
                            ch.link(dve.tensor_tensor(rank[:, :, a], rank[:, :, a], cmp_[:, :], ALU.add))
                ch.link(dve.tensor_reduce(st[:, 3], score[:, :, :], AX.X, ALU.max))
                ch.link(dve.tensor_tensor(gate[:, :, :], score[:, :, :], st[:, 3].unsqueeze(2).broadcast_to([P, NT, NX]), ALU.subtract))
                dve.sem_inc(s_e3, 1)
                dve.wait_ge(s_x3, 1)
                ch.link(dve.scalar_tensor_tensor(out=gate[:, :, :], in0=rank[:, :, :], scalar=1.5, in1=gate[:, :, :],
                                                 op0=ALU.is_lt, op1=ALU.mult))
                ch.link(dve.tensor_reduce(st[:, 0], gate[:, :, :], AX.X, ALU.add))
                ch.link(dve.reciprocal(st[:, 1], st[:, 0]))
                ch.link(dve.tensor_tensor(gate[:, :, :], gate[:, :, :], st[:, 1].unsqueeze(2).broadcast_to([P, NT, NX]), ALU.mult))
                dve.sem_inc(s_yf, 2)
                start = ch.base + ch.k
                with dve.Fori(0, GN // 2) as i:
                    ch.enter(i, 4, start)
                    for par in range(2):
                        four = bass.ds(i * 8 + par * 4, 4)
                        dve.wait_ge(s_yl[par], i * 16 + 16)
                        ch.link(dve.tensor_tensor(yp[:, par], ye[:, par], gate[:, four, :].unsqueeze(3).broadcast_to([P, 4, NX, D]), ALU.mult))
                        dve.sem_inc(s_yf, 1)
                        dve.wait_ge(s_o[par], i * 16 + 16)
                        ch.link(dve.tensor_reduce(yo[:, par], yp[:, par].rearrange("p t x d -> p t d x"), AX.X, ALU.add))
                        dve.tensor_tensor(yo[:, par], yo[:, par], h_all[:, four, :], ALU.add).then_inc(s_of, 1)
                ch.leave(GN // 2)


_OUTS = [((16, 1024, 64), "float32")]


def kernel(**inputs):
    import numpy as np
    import concourse.bacc as bacc
    from concourse.bass_utils import run_bass_kernel_spmd

    a = {k: np.asarray(v) for k, v in inputs.items()}
    tiles = lambda x: x.reshape(2, ET, P)
    arrays = {
        "ids": a["x"].reshape(NT, P).T,
        "emb": a["L0_tok_base_embeddings"],
        "rule_mats": a["L0_tok_rule_transform"].reshape(RULES, D * D),
        "rules": a["L0_tok_token_rules"],
        "a_edge_t": tiles(a["L0_attn_edge_index"]).transpose(0, 2, 1),
        "a_edge_n": tiles(a["L0_attn_edge_index"]),
        "a_val_t": a["L0_attn_edge_values"].reshape(ET, P).T,
        "pos_t": a["L0_attn_positions"].T,
        "qkv_wt": a["L0_attn_qkv_w"].T,
        "qkv_b": a["L0_attn_qkv_b"].reshape(1, 3 * D),
        "proj_wt": a["L0_attn_proj_w"].T,
        "proj_b": a["L0_attn_proj_b"].reshape(1, D),
        "gate_w": a["L0_attn_gate_w"].reshape(1, H * 4),
        "gate_wt": a["L0_attn_gate_w"].T,
        "gate_b": a["L0_attn_gate_b"].reshape(1, H),
        "w_gat": a["L0_ffn_W_gat"],
        "att_src": a["L0_ffn_att_src"].reshape(1, H * NX),
        "att_dst": a["L0_ffn_att_dst"].reshape(1, H * NX),
        "b_gat": a["L0_ffn_b_gat"].reshape(1, H * NX),
        "ln_g": a["L0_ffn_ln_gamma"].reshape(1, H * NX),
        "ln_b": a["L0_ffn_ln_beta"].reshape(1, H * NX),
        "w1": a["L0_ffn_W1"],
        "b1t": a["L0_ffn_b1"].T,
        "w2": a["L0_ffn_W2"],
        "b2": a["L0_ffn_b2"].reshape(1, NX * D),
        "g_edge_t": tiles(a["L0_ffn_edge_index"]).transpose(0, 2, 1),
        "g_edge_n": tiles(a["L0_ffn_edge_index"]),
    }
    nc = bacc.Bacc("TRN2", target_bir_lowering=False, num_devices=1)
    given, args = {}, []
    for name, x in arrays.items():
        given[f"in_{name}"] = np.ascontiguousarray(x)
        args.append(nc.dram_tensor(f"in_{name}", x.shape, mybir.dt.from_np(x.dtype), kind="ExternalInput").ap())
    shape, dtype = _OUTS[0]
    args.append(nc.dram_tensor("out_0", (P, NT, D), mybir.dt.from_np(np.dtype(dtype)), kind="ExternalOutput").ap())
    tower(nc, *args)
    r = run_bass_kernel_spmd(nc, [given], core_ids=[0])
    return r.results[0]["out_0"].transpose(1, 0, 2).reshape(shape)
```
